# Optimizing a Trainium2 kernel written in Bass

```python
import numpy as np
import jax
import jax.numpy as jnp

def _softmax(x, axis=-1):
    return jax.nn.softmax(x, axis=axis)
def _gelu(x):
    return jax.nn.gelu(x, approximate=True)
def _silu(x):
    return jax.nn.silu(x)
def _sigmoid(x):
    return jax.nn.sigmoid(x)
def _layernorm(x, axis=-1, eps=1e-5):
    m = jnp.mean(x, axis=axis, keepdims=True)
    v = jnp.var(x, axis=axis, keepdims=True)
    return (x - m) / jnp.sqrt(v + eps)
def _scatter_add(tgt, idx, src, axis=0):
    return tgt.at[idx].add(src)
def _segment_sum(src, seg, n):
    return jax.ops.segment_sum(src, seg, n)

kernel_name = 'mk_adj_preln_d4_adj_512_a4b08d'

def setup_inputs(seed: int = 0):
    np.random.seed(seed)
    _w = jnp.asarray
    def _rec_inputs():
        import jax
        import jax.numpy as jnp
        _gk = jax.random.key(seed)
        x = -0.0005207 + 1.001 * jax.random.normal(jax.random.fold_in(_gk, 1), (2708, 512), jnp.float32)
        _w = (1.0 + jnp.arange(2708, dtype=jnp.float32)) ** -0.5
        _w = _w / _w.mean()
        _pij = jnp.clip(0.0014771 * _w[:, None] * _w[None, :], 0.0, 1.0)
        _a = jax.random.uniform(jax.random.fold_in(_gk, 2), (2708, 2708)) < _pij
        _af = _a.astype(jnp.float32)
        adj = _af
        return x, adj
    x, adj = _rec_inputs()
    def _L0_gnn_setup():
        import jax, jax.numpy as jnp
        import numpy as np
        ALPHA = 0.2
        NEG_INF = -1000000000000.0
        key = jax.random.key(seed)
        k1, k2, k3, k4, k5 = jax.random.split(key, 5)
        N, F = (4096, 512)
        inp = jax.random.normal(k1, (N, F), dtype=jnp.float32)
        adj = jax.random.randint(k2, (N, N), 0, 2).astype(jnp.float32)
        W = jax.random.normal(k3, (F, F), dtype=jnp.float32) * (1.414 / np.sqrt(F))
        a = jax.random.normal(k4, (2 * F, 1), dtype=jnp.float32) * 0.05
        wtrans = jax.random.normal(k5, (2 * F, F), dtype=jnp.float32) * (1.414 / np.sqrt(1.5 * F))
        return {'inp': inp, 'adj': adj, 'W': W, 'a': a, 'wtrans': wtrans}
    _L0_gnn_all = _L0_gnn_setup()
    _L0_gnn_in = {k: v for k, v in _L0_gnn_all.items() if k in ('W', 'a', 'wtrans', )}
    del _L0_gnn_all

    def _L1_gnn_setup():
        import jax, jax.numpy as jnp
        import numpy as np
        N, IN_DIM, OUT_DIM, NHEAD = (4096, 512, 64, 8)
        LK_ALPHA = 0.2
        EPS = 1e-06
        NEG_FILL = -32768.0
        key = jax.random.key(seed)
        kx, kw, ka1, ka2, kg = jax.random.split(key, 5)
        x = jax.random.normal(kx, (N, IN_DIM), dtype=jnp.float32)
        lim_w = 1.414 * np.sqrt(6.0 / (IN_DIM + OUT_DIM * NHEAD))
        W = jax.random.uniform(kw, (IN_DIM, OUT_DIM * NHEAD), minval=-lim_w, maxval=lim_w, dtype=jnp.float32)
        lim_a = 1.414 * np.sqrt(6.0 / (OUT_DIM + NHEAD))
        a1 = jax.random.uniform(ka1, (OUT_DIM, NHEAD), minval=-lim_a, maxval=lim_a, dtype=jnp.float32)
        a2 = jax.random.uniform(ka2, (OUT_DIM, NHEAD), minval=-lim_a, maxval=lim_a, dtype=jnp.float32)
        adj = (jax.random.uniform(kg, (N, N)) < 0.05).astype(jnp.float32)
        adj = jnp.maximum(adj, jnp.eye(N, dtype=jnp.float32))
        graph = adj
        mask = adj.astype(bool)
        a_ln = jnp.ones((OUT_DIM,), dtype=jnp.float32)
        b_ln = jnp.zeros((OUT_DIM,), dtype=jnp.float32)
        return {'x': x, 'graph': graph, 'mask': mask, 'W': W, 'a1': a1, 'a2': a2, 'a_ln': a_ln, 'b_ln': b_ln}
    _L1_gnn_all = _L1_gnn_setup()
    _L1_gnn_in = {k: v for k, v in _L1_gnn_all.items() if k in ('W', 'a1', 'a2', 'a_ln', 'b_ln', )}
    del _L1_gnn_all

    def _L2_gnn_setup():
        import jax, jax.numpy as jnp
        import numpy as np
        KAPPA = -1.0
        EPS = 1e-10
        N, D_IN, D_OUT = (8192, 512, 512)

        def _artan_k(x):
            sc = np.sqrt(-KAPPA)
            return jnp.arctanh(jnp.clip(sc * x, -1.0 + 1e-07, 1.0 - 1e-07)) / sc

        def _tan_k(x):
            sc = np.sqrt(-KAPPA)
            return jnp.tanh(sc * x) / sc

        def _clamp_abs(x, eps=EPS):
            return jnp.where(x >= 0, 1.0, -1.0) * jnp.maximum(jnp.abs(x), eps)

        def _norm(x):
            return jnp.sqrt(jnp.maximum(jnp.sum(x * x, axis=-1, keepdims=True), EPS * EPS))

        def mobius_matvec(W, x):
            x_norm = _norm(x)
            mx = x @ W
            mx_norm = _norm(mx)
            res = _tan_k(mx_norm / x_norm * _artan_k(x_norm)) * (mx / mx_norm)
            return jnp.where(mx_norm <= EPS, 0.0, res)

        def mobius_scalar_mul(r, x):
            x_norm = _norm(x)
            return _tan_k(r * _artan_k(x_norm)) * (x / x_norm)

        def weighted_midpoint_lincomb(A, X):
            gamma = jnp.maximum(2.0 / (1.0 + KAPPA * jnp.sum(X * X, axis=-1, keepdims=True)), 1e-15)
            denom = _clamp_abs(A @ (gamma - 1.0))
            nom = A @ (gamma * X)
            two_mean = nom / denom
            sq = jnp.sum(two_mean * two_mean, axis=-1, keepdims=True)
            a_mean = two_mean / (1.0 + jnp.sqrt(jnp.maximum(1.0 + KAPPA * sq, EPS)))
            alpha = jnp.sum(A, axis=-1, keepdims=True)
            return mobius_scalar_mul(alpha, a_mean)

        def logmap0(x):
            xn = _norm(x)
            return _artan_k(xn) * x / xn

        def expmap0(u):
            un = _norm(u)
            return _tan_k(un) * u / un
        key = jax.random.key(seed)
        k1, k2, k3 = jax.random.split(key, 3)
        X = jax.random.normal(k1, (N, D_IN), dtype=jnp.float32) * 0.001
        A_hat = jax.random.uniform(k2, (N, N), dtype=jnp.float32) / N
        W = jax.random.normal(k3, (D_IN, D_OUT), dtype=jnp.float32) * 0.01
        return {'X': X, 'A_hat': A_hat, 'W': W}
    _L2_gnn_all = _L2_gnn_setup()
    _L2_gnn_in = {k: v for k, v in _L2_gnn_all.items() if k in ('W', )}
    del _L2_gnn_all

    def _L3_gnn_setup():
        import jax, jax.numpy as jnp
        import numpy as np
        N = 8192
        D_IN = 512
        D_OUT = 512
        NEG_BIG = -9000000000000000.0
        key = jax.random.key(seed)
        kx, ka, kw, kb, kn, ke = jax.random.split(key, 6)
        x = jax.random.normal(kx, (N, D_IN), dtype=jnp.float32)
        adj = (jax.random.uniform(ka, (N, N)) > 0.9).astype(jnp.float32)
        stdv = 1.0 / np.sqrt(D_OUT)
        weight = jax.random.uniform(kw, (D_IN, D_OUT), minval=-stdv, maxval=stdv, dtype=jnp.float32)
        bias = jax.random.uniform(kb, (D_OUT,), minval=-stdv, maxval=stdv, dtype=jnp.float32)
        node_w = jax.random.uniform(kn, (D_IN, 1), minval=-1.0, maxval=1.0, dtype=jnp.float32)
        stdv_e = 1.0 / np.sqrt(D_IN)
        edge_w = jax.random.uniform(ke, (D_IN, D_IN), minval=-stdv_e, maxval=stdv_e, dtype=jnp.float32)
        return {'x': x, 'adj': adj, 'weight': weight, 'bias': bias, 'node_w': node_w, 'edge_w': edge_w}
    _L3_gnn_all = _L3_gnn_setup()
    _L3_gnn_in = {k: v for k, v in _L3_gnn_all.items() if k in ('weight', 'bias', 'node_w', 'edge_w', )}
    del _L3_gnn_all

    return {
        "x": x,
        "adj": adj,
        "L0_gnn_W": _L0_gnn_in["W"],
        "L0_gnn_a": _L0_gnn_in["a"],
        "L0_gnn_wtrans": _L0_gnn_in["wtrans"],
        "L1_gnn_W": _L1_gnn_in["W"],
        "L1_gnn_a1": _L1_gnn_in["a1"],
        "L1_gnn_a2": _L1_gnn_in["a2"],
        "L1_gnn_a_ln": _L1_gnn_in["a_ln"],
        "L1_gnn_b_ln": _L1_gnn_in["b_ln"],
        "L2_gnn_W": _L2_gnn_in["W"],
        "L3_gnn_weight": _L3_gnn_in["weight"],
        "L3_gnn_bias": _L3_gnn_in["bias"],
        "L3_gnn_node_w": _L3_gnn_in["node_w"],
        "L3_gnn_edge_w": _L3_gnn_in["edge_w"],
    }

def reference(x, adj, L0_gnn_W, L0_gnn_a, L0_gnn_wtrans, L1_gnn_W, L1_gnn_a1, L1_gnn_a2, L1_gnn_a_ln, L1_gnn_b_ln, L2_gnn_W, L3_gnn_weight, L3_gnn_bias, L3_gnn_node_w, L3_gnn_edge_w):
    import jax
    import jax.numpy as jnp
    def _L0_gnn_ref(inp, adj, W, a, wtrans):
        import jax, jax.numpy as jnp
        import numpy as np
        ALPHA = 0.2
        NEG_INF = -1000000000000.0
        F_out = W.shape[1]
        h = inp @ W
        Wh1 = h @ a[:F_out, :]
        Wh2 = h @ a[F_out:, :]
        e = jax.nn.leaky_relu(Wh1 + Wh2.T, ALPHA)
        mask = adj > 0
        attention = jax.nn.softmax(jnp.where(mask, e, NEG_INF), axis=1)
        negative_attention = -jax.nn.softmax(jnp.where(mask, -e, NEG_INF), axis=1)
        h_prime = attention @ inp
        h_prime_negative = negative_attention @ inp
        h_prime_double = jnp.concatenate([h_prime, h_prime_negative], axis=1)
        new_h_prime = h_prime_double @ wtrans
        return jax.nn.elu(new_h_prime)

    def _L1_gnn_ref(x, graph, mask, W, a1, a2, a_ln, b_ln):
        import jax, jax.numpy as jnp
        import numpy as np
        N, IN_DIM, OUT_DIM, NHEAD = (4096, 512, 64, 8)
        LK_ALPHA = 0.2
        EPS = 1e-06
        NEG_FILL = -32768.0
        n = x.shape[0]
        nX = (x @ W).reshape(n, NHEAD, OUT_DIM).transpose(1, 0, 2)
        mean = nX.mean(-1, keepdims=True)
        std = jnp.std(nX, axis=-1, ddof=1, keepdims=True)
        nX = a_ln * (nX - mean) / (std + EPS) + b_ln
        at1 = jnp.einsum('kno,ok->kn', nX, a1)[:, :, None]
        at2 = jnp.einsum('kno,ok->kn', nX, a2)[:, :, None]
        kg = at1 + at2.transpose(0, 2, 1)
        kg = jax.nn.leaky_relu(kg, negative_slope=LK_ALPHA)
        kg = kg * graph[None, :, :]
        mg = jnp.where(mask[None, :, :], kg, NEG_FILL)
        attention = jax.nn.softmax(mg, axis=-1)
        y = attention @ nX + nX
        y = y.transpose(1, 0, 2).reshape(n, NHEAD * OUT_DIM)
        return jax.nn.elu(y)

    def _L2_gnn_ref(X, A_hat, W):
        import jax, jax.numpy as jnp
        import numpy as np
        KAPPA = -1.0
        EPS = 1e-10
        N, D_IN, D_OUT = (8192, 512, 512)

        def _artan_k(x):
            sc = np.sqrt(-KAPPA)
            return jnp.arctanh(jnp.clip(sc * x, -1.0 + 1e-07, 1.0 - 1e-07)) / sc

        def _tan_k(x):
            sc = np.sqrt(-KAPPA)
            return jnp.tanh(sc * x) / sc

        def _clamp_abs(x, eps=EPS):
            return jnp.where(x >= 0, 1.0, -1.0) * jnp.maximum(jnp.abs(x), eps)

        def _norm(x):
            return jnp.sqrt(jnp.maximum(jnp.sum(x * x, axis=-1, keepdims=True), EPS * EPS))

        def mobius_matvec(W, x):
            x_norm = _norm(x)
            mx = x @ W
            mx_norm = _norm(mx)
            res = _tan_k(mx_norm / x_norm * _artan_k(x_norm)) * (mx / mx_norm)
            return jnp.where(mx_norm <= EPS, 0.0, res)

        def mobius_scalar_mul(r, x):
            x_norm = _norm(x)
            return _tan_k(r * _artan_k(x_norm)) * (x / x_norm)

        def weighted_midpoint_lincomb(A, X):
            gamma = jnp.maximum(2.0 / (1.0 + KAPPA * jnp.sum(X * X, axis=-1, keepdims=True)), 1e-15)
            denom = _clamp_abs(A @ (gamma - 1.0))
            nom = A @ (gamma * X)
            two_mean = nom / denom
            sq = jnp.sum(two_mean * two_mean, axis=-1, keepdims=True)
            a_mean = two_mean / (1.0 + jnp.sqrt(jnp.maximum(1.0 + KAPPA * sq, EPS)))
            alpha = jnp.sum(A, axis=-1, keepdims=True)
            return mobius_scalar_mul(alpha, a_mean)

        def logmap0(x):
            xn = _norm(x)
            return _artan_k(xn) * x / xn

        def expmap0(u):
            un = _norm(u)
            return _tan_k(un) * u / un
        XW = mobius_matvec(W, X)
        AXW = weighted_midpoint_lincomb(A_hat, XW)
        return expmap0(jax.nn.relu(logmap0(AXW)))

    def _L3_gnn_ref(x, adj, weight, bias, node_w, edge_w):
        import jax, jax.numpy as jnp
        import numpy as np
        N = 8192
        D_IN = 512
        D_OUT = 512
        NEG_BIG = -9000000000000000.0
        node_att = jax.nn.softmax(x @ node_w, axis=0)
        h = x @ edge_w
        e = h @ h.T
        e = jnp.where(adj > 0, e, NEG_BIG)
        edge_att = jax.nn.softmax(e, axis=1)
        combined_att = node_att * edge_att
        support = x @ weight
        output = adj * combined_att @ support
        return output + bias

    h = jnp.maximum(_layernorm(x, axis=-1), 0.0)
    x = x + _L0_gnn_ref(h, adj, L0_gnn_W, L0_gnn_a, L0_gnn_wtrans)
    h = jnp.maximum(_layernorm(x, axis=-1), 0.0)
    x = x + _L1_gnn_ref(h, adj, adj, L1_gnn_W, L1_gnn_a1, L1_gnn_a2, L1_gnn_a_ln, L1_gnn_b_ln)
    h = jnp.maximum(_layernorm(x, axis=-1), 0.0)
    x = x + _L2_gnn_ref(h, adj, L2_gnn_W)
    h = jnp.maximum(_layernorm(x, axis=-1), 0.0)
    x = x + _L3_gnn_ref(h, adj, L3_gnn_weight, L3_gnn_bias, L3_gnn_node_w, L3_gnn_edge_w)
    return x


_drawn_inputs = setup_inputs


def setup_inputs(seed=0):
    import zlib

    import numpy as np

    out = dict(_drawn_inputs(seed))
    spreads = {'L1_gnn_a_ln': (1.0, 0.2), 'L1_gnn_b_ln': (0.0, 0.1)}
    factors = {'L2_gnn_W': 3.458,
     'L3_gnn_weight': 8.0,
     'L3_gnn_bias': 4.515,
     'L3_gnn_node_w': 8.0,
     'L3_gnn_edge_w': 8.0}
    for name, (base, spread) in spreads.items():
        noise = np.random.default_rng([zlib.crc32(name.encode()), seed]).standard_normal(out[name].shape)
        drawn = base * np.exp(spread * noise) if base else spread * noise
        out[name] = jnp.asarray(drawn.astype(out[name].dtype))
    for name, factor in factors.items():
        out[name] = (out[name] * factor).astype(out[name].dtype)
    return out
```

```python
from contextlib import ExitStack

import concourse.bass as bass
from concourse import mybir

F32 = mybir.dt.float32
F16 = mybir.dt.float16
BF16 = mybir.dt.bfloat16
ALU = mybir.AluOpType
ACT = mybir.ActivationFunctionType
AXX = mybir.AxisListType.X
RMAX = bass.bass_isa.ReduceOp.max
RADD = bass.bass_isa.ReduceOp.add

P = 128
N = 2708
T = -(-N // P)
NP = T * P
LAST = N - (T - 1) * P
D = 512
KC = D // P
H = 8
DH = D // H
IB = T // 2
BW = 2 * P
BIG = 1e30
CLAMP = 1e28
WS = 64.0
XMAX = 1.0 - 2.0 ** -23
ATMAX = 8.317766
CHUNKS = [(0, 6), (6, 6), (12, 6), (18, 4)]


def free(t):
    return t + 1


def done(t):
    return t + 3


def ds(start, size):
    return bass.ds(start, size)


def wait_count(eng, sem, count, gate):
    eng.wait_ge(sem, count)
    eng.sem_inc(gate, 1)


class Kit:

    def __init__(self, nc, stack, prefix):
        self.nc, self.stack, self.prefix, self.semaphores = nc, stack, prefix, []

    def sb(self, name, shape, dt=F32):
        return self.stack.enter_context(self.nc.sbuf_tensor(f"{self.prefix}_{name}", [P] + list(shape), dt))

    def ps(self, name, shape, dt=F32):
        return self.stack.enter_context(self.nc.psum_tensor(f"{self.prefix}_{name}", [P] + list(shape), dt))

    def sems(self, names):
        made = [self.nc.alloc_semaphore(f"{self.prefix}_{n}") for n in names.split()]
        self.semaphores += made
        return made

    def close(self):
        self.nc.clear_and_free_semaphores(self.semaphores)
        self.nc.all_engine_barrier()


def flat(ap):
    return ap.rearrange("p o d -> p (o d)")


def tiles(ap):
    return ap.rearrange("(t p) d -> p t d", p=P)


def norm_statistics(dve, x_all, stats, mv, std, rstd, nmr, x_here, s):
    for c, (t0, n) in enumerate(CHUNKS):
        x_here(c)
        for t in range(t0, t0 + n):
            last = dve.bn_stats(stats[:, t, :], x_all[:, t, :])
    last.then_inc(s["stats"], 1)
    dve.wait_ge(s["stats"], 1)
    for t in range(T):
        last = dve.bn_aggr(mv[:, t, :], stats[:, t, :])
    last.then_inc(s["mv"], 1)
    dve.wait_ge(s["mv"], 1)
    dve.tensor_scalar(std[:], mv[:, :, 1], 1e-5, None, ALU.add).then_inc(s["var"], 1)
    dve.wait_ge(s["std"], 1)
    dve.reciprocal(rstd[:], std[:]).then_inc(s["rstd"], 1)
    dve.wait_ge(s["rstd"], 1)
    dve.scalar_tensor_tensor(nmr[:], mv[:, :, 0], -1.0, rstd[:], ALU.mult, ALU.mult).then_inc(s["nmr"], 1)


def split_weights(dve, w, w_hi, w_lo, s):
    dve.tensor_scalar(w_hi[:], w[:], WS, None, ALU.mult).then_inc(s["w_hi"], 1)
    dve.wait_ge(s["w_hi"], 1)
    dve.scalar_tensor_tensor(w_lo[:], w[:], WS, w_hi[:], ALU.mult, ALU.subtract).then_inc(s["w_lo"], 1)


def split_product(pe, out, a_hi, a_lo, b_hi, b_lo, columns):
    for k in range(KC):
        pe.matmul(out, a_hi[:, k, :], b_hi[:, k, columns], start=(k == 0), stop=False, skip_group_check=True)
        pe.matmul(out, a_hi[:, k, :], b_lo[:, k, columns], start=False, stop=False, skip_group_check=True)
        last = pe.matmul(out, a_lo[:, k, :], b_hi[:, k, columns], start=False, stop=(k == KC - 1), skip_group_check=True)
    return last


def loop_with_next(eng, now, ahead):
    ahead(0, 0)
    with eng.Fori(0, T - 2, 2) as t:
        for b in range(2):
            ahead(t + b + 1, 1 - b)
            now(t + b, b)
    ahead(T - 1, 1)
    now(T - 2, 0)
    now(T - 1, 1)


def loop_with_two_next(eng, now, ahead, far_ahead):
    far_ahead(0, 0)
    far_ahead(1, 1)
    ahead(0, 0)
    with eng.Fori(0, T - 3, 2) as t:
        for b in range(2):
            far_ahead(t + b + 2, b)
            ahead(t + b + 1, 1 - b)
            now(t + b, b)
    ahead(T - 1, 1)
    now(T - 2, 0)
    now(T - 1, 1)


def loop_tiles(eng, step):
    with eng.Fori(0, T - 1, 2) as t:
        for b in range(2):
            step(t + b, b)


class Chain:

    def __init__(self, dve, link, asked, answered):
        self.dve, self.link, self.asked, self.answered = dve, link, asked, answered
        self.steps = self.questions = 0

    def then(self, instruction):
        self.steps += 1
        instruction.then_inc(self.link, 1)
        self.dve.wait_ge(self.link, self.steps)

    def ask(self):
        self.questions += 1
        self.dve.sem_inc(self.asked, 1)
        self.dve.wait_ge(self.answered, self.questions)

    def scale(self, out, a, s1, op0=ALU.mult, s2=None, op1=ALU.bypass):
        if s2 is None:
            self.then(self.dve.tensor_scalar(out, a, s1, None, op0))
        else:
            self.then(self.dve.tensor_scalar(out, a, s1, s2, op0, op1))

    def pair(self, out, a, b, op=ALU.mult):
        self.then(self.dve.tensor_tensor(out, a, b, op))

    def fused(self, out, a, s, b, op0, op1):
        self.then(self.dve.scalar_tensor_tensor(out, a, s, b, op0, op1))

    def invert(self, out, a):
        self.then(self.dve.reciprocal(out, a))

    def choose(self, out, small, is_small):
        self.pair(small, small, out, ALU.subtract)
        self.pair(small, small, is_small)
        self.pair(out, out, small, ALU.add)

    def atanh(self, out, x, t1, t2, ln):
        self.scale(x, x, XMAX, ALU.min)
        self.scale(t1, x, -1.0, ALU.mult, 1.0, ALU.add)
        self.invert(t1, t1)
        self.fused(ln, x, 1.0, t1, ALU.add, ALU.mult)
        self.ask()
        self.scale(out, ln, 0.5)
        self.pair(t1, x, x)
        self.scale(t2, t1, 1 / 7, ALU.mult, 1 / 5, ALU.add)
        self.pair(t2, t2, t1)
        self.scale(t2, t2, 1 / 3, ALU.add)
        self.pair(t2, t2, t1)
        self.fused(t2, t2, 1.0, x, ALU.add, ALU.mult)
        self.scale(t1, x, 0.05, ALU.is_lt)
        self.choose(out, t2, t1)

    def tanh(self, out, x, t1, t2, e):
        self.ask()
        self.scale(t1, e, 1.0, ALU.add)
        self.invert(t1, t1)
        self.scale(t2, e, -1.0, ALU.mult, 1.0, ALU.add)
        self.pair(out, t2, t1)
        self.pair(t1, x, x)
        self.scale(t2, t1, 2 / 15, ALU.mult, -1 / 3, ALU.add)
        self.pair(t2, t2, t1)
        self.fused(t2, t2, 1.0, x, ALU.add, ALU.mult)
        self.scale(t1, x, 0.02, ALU.is_lt)
        self.choose(out, t2, t1)


def answers(act, asked, answered, questions):
    for n, (out, function, of, scale) in enumerate(questions):
        act.wait_ge(asked, n + 1)
        act.activation(out, of, function, scale=scale).then_inc(answered, 1)


def setup(nc, dram, keep):
    with ExitStack() as stack:
        kit = Kit(nc, stack, "setup")
        (loaded, made) = kit.sems("loaded made")
        with nc.Block() as block:
            @block.sync
            def _(sp):
                sp.dma_start(keep["ident"][:], dram["ident"]).then_inc(loaded, 16)
                sp.wait_ge(loaded, 16)

            @block.vector
            def _(dve):
                dve.wait_ge(loaded, 16)
                dve.tensor_copy(keep["ident16"][:], keep["ident"][:]).then_inc(made, 1)

            @block.gpsimd
            def _(pool):
                pool.memset(keep["ones16"][:], 1.0).then_inc(made, 1)
                pool.wait_ge(made, 2)

        kit.close()

def prep0(nc, dram, keep):
    with ExitStack() as stack:
        kit = Kit(nc, stack, "p0")
        x_all, h = kit.sb("x_all", [T, D]), kit.sb("h", [2, D])
        hT_hi, hT_lo = kit.sb("hT_hi", [2, KC, P], F16), kit.sb("hT_lo", [2, KC, P], F16)
        NX = 2 * D + 2
        w = kit.sb("w", [KC, NX])
        w_hi, w_lo = kit.sb("w_hi", [KC, NX], F16), kit.sb("w_lo", [KC, NX], F16)
        wt, avec = kit.sb("wt", [KC, D]), kit.sb("avec", [KC, 2])
        stats, mv = kit.sb("stats", [T, 6]), kit.sb("mv", [T, 2])
        std, rstd, nmr = kit.sb("std", [T]), kit.sb("rstd", [T]), kit.sb("nmr", [T])
        uvT = kit.sb("uvT", [P])
        tp = kit.ps("tp", [2, KC, P])
        main = kit.ps("main", [2, 2 * D])
        small = kit.ps("small", [2, 256])
        z_hi, z_lo, uv, cs = keep["z_hi"], keep["z_lo"], keep["uv"], keep["cs0"]
        x_in = kit.sems(" ".join(f"x_in{c}" for c in range(len(CHUNKS))))
        s = dict(zip("stats mv var std rstd nmr w_hi w_lo".split(),
                     kit.sems("stats mv var std rstd nmr w_hi w_lo")))
        (w_in, a_in, wa_made, wa_copied, h_ready, tp_ready, hi_ready, lo_done, prod_done, z_hi_done,
         z_lo_done, uv_done, uvt_ready, uvt_copied, cs_ready, rows_out, used) = kit.sems(
            "w_in a_in wa_made wa_copied h_ready tp_ready hi_ready lo_done prod_done z_hi_done "
            "z_lo_done uv_done uvt_ready uvt_copied cs_ready rows_out used")
        x_t = tiles(dram["x0"])

        with nc.Block() as block:
            @block.sync
            def _(sp):
                for ring in (lo_done, prod_done, z_lo_done, uv_done):
                    sp.sem_inc(ring, 2)
                sp.dma_start(wt[:], dram["w0t"].rearrange("(k p) n -> p k n", p=P)).then_inc(a_in, 16)
                sp.dma_start(avec[:], dram["a0"]).then_inc(a_in, 16)
                for c, (t0, n) in enumerate(CHUNKS):
                    sp.dma_start(x_all[:, t0:t0 + n, :], x_t[:, t0:t0 + n, :]).then_inc(x_in[c], 16)
                    if c < 2:
                        sp.dma_start(w[:, :, c * D:(c + 1) * D],
                                     dram["wtr0"][c * D:(c + 1) * D, :].rearrange("(k p) n -> p k n", p=P)).then_inc(w_in, 16)
                sp.wait_ge(uvt_copied, 1)
                sp.dma_start(dram["rows"][0:2 * T, :], uvT[0:2 * T, :]).then_inc(rows_out, 16)
                sp.wait_ge(rows_out, 16)

            @block.scalar
            def _(act):
                act.wait_ge(s["var"], 1)
                act.activation(std[:], std[:], ACT.Sqrt).then_inc(s["std"], 1)
                act.wait_ge(s["nmr"], 1)

                def normalise(t, b):
                    act.wait_ge(tp_ready, free(t))
                    act.activation(h[:, b, :], flat(x_all[:, ds(t, 1), :]), ACT.Relu,
                                   bias=nmr[:, ds(t, 1)], scale=rstd[:, ds(t, 1)]).then_inc(h_ready, 1)

                def high(t, b):
                    act.wait_ge(tp_ready, done(t))
                    act.wait_ge(prod_done, free(t))
                    act.activation(hT_hi[:, b], tp[:, b], ACT.Copy).then_inc(hi_ready, 1)

                def finish(t, b):
                    act.wait_ge(prod_done, done(t))
                    act.activation(flat(z_hi[:, ds(t, 1), :]), main[:, b, :], ACT.Copy, scale=1 / WS).then_inc(z_hi_done, 1)

                act.sem_inc(tp_ready, 2)
                loop_with_two_next(act, finish, high, normalise)

            @block.tensor
            def _(pe):
                pe.wait_ge(a_in, 32)
                for m in range(KC):
                    for k in range(KC):
                        last = pe.matmul(small[:, 0, 2 * m:2 * m + 2], wt[:, k, m * P:(m + 1) * P], avec[:, k, :],
                                         start=(k == 0), stop=(k == KC - 1))
                last.then_inc(wa_made, 1)
                pe.wait_ge(s["w_lo"], 1)

                def transpose(t, b):
                    pe.wait_ge(h_ready, t + 1)
                    pe.wait_ge(lo_done, free(t))
                    for k in range(KC):
                        last = pe.transpose(tp[:, b, k, :], h[:, b, k * P:(k + 1) * P], keep["ident"][:])
                    last.then_inc(tp_ready, 1)

                def products(t, b):
                    pe.wait_ge(hi_ready, t + 1)
                    pe.wait_ge(lo_done, done(t))
                    pe.wait_ge(z_lo_done, free(t))
                    for half in range(2):
                        cols = slice(half * D, (half + 1) * D)
                        split_product(pe, main[:, b, cols], hT_hi[:, b], hT_lo[:, b], w_hi, w_lo, cols)
                    pe.wait_ge(uv_done, done(t - 1))
                    last = split_product(pe, small[:, b, 0:2], hT_hi[:, b], hT_lo[:, b], w_hi, w_lo, slice(2 * D, NX))
                    last.then_inc(prod_done, 1)

                loop_with_next(pe, products, transpose)
                pe.wait_ge(uv_done, done(T - 1))
                pe.transpose(tp[0:2 * T, 0, 0, :], uv[:].rearrange("p s t -> p (s t)"), keep["ident"][:]).then_inc(uvt_ready, 1)
                pe.wait_ge(z_lo_done, done(T - 1))

                def column_sums(t, rows, start, stop):
                    for half in range(2):
                        for part in (z_hi, z_lo):
                            last = pe.matmul(main[:, 0, half * D:(half + 1) * D], keep["ones16"][0:rows, :],
                                             flat(part[0:rows, ds(t, 1), half * D:(half + 1) * D]),
                                             start=start and part is z_hi, stop=stop and part is z_lo,
                                             skip_group_check=True)
                    return last

                column_sums(0, P, True, False)
                with pe.Fori(1, T - 1) as t:
                    column_sums(t, P, False, False)
                column_sums(T - 1, LAST, False, True).then_inc(cs_ready, 1)

            @block.vector
            def _(dve):
                dve.wait_ge(wa_made, 1)
                dve.tensor_copy(w[:, :, 2 * D:NX], small[:, 0, 0:2 * KC].rearrange("p (m s) -> p m s", s=2)).then_inc(wa_copied, 1)
                dve.wait_ge(wa_copied, 1)
                dve.wait_ge(w_in, 32)
                split_weights(dve, w, w_hi, w_lo, s)
                norm_statistics(dve, x_all, stats, mv, std, rstd, nmr, lambda c: dve.wait_ge(x_in[c], 16), s)

                def split(t, b):
                    dve.wait_ge(hi_ready, t + 1)
                    dve.tensor_tensor(hT_lo[:, b], tp[:, b], hT_hi[:, b], ALU.subtract).then_inc(lo_done, 1)

                def finish(t, b):
                    dve.wait_ge(prod_done, done(t))
                    dve.tensor_scalar(uv[:, :, ds(t, 1)], small[:, b, 0:2].unsqueeze(2), 1 / WS, None, ALU.mult).then_inc(uv_done, 1)
                    dve.wait_ge(z_hi_done, t + 1)
                    dve.scalar_tensor_tensor(flat(z_lo[:, ds(t, 1), :]), main[:, b, :], 1 / WS, flat(z_hi[:, ds(t, 1), :]),
                                             ALU.mult, ALU.subtract).then_inc(z_lo_done, 1)

                loop_with_next(dve, finish, split)
                dve.wait_ge(uvt_ready, 1)
                dve.tensor_copy(uvT[0:2 * T, :], tp[0:2 * T, 0, 0, :]).then_inc(uvt_copied, 1)
                dve.wait_ge(cs_ready, 1)
                dve.tensor_copy(cs[:], main[:, 0, :]).then_inc(used, 1)

        kit.close()


def extremes0(nc, dram, keep):
    with ExitStack() as stack:
        kit = Kit(nc, stack, "e0")
        v_row = kit.sb("v_row", [NP])
        a_rows = kit.sb("a_rows", [2, NP])
        am = kit.sb("am", [2, NP])
        scratch = kit.sb("scratch", [2, NP])
        vmax, nvmin = kit.sb("vmax", [T]), kit.sb("nvmin", [T])
        s1, s2, g = kit.sb("s1", [T]), kit.sb("s2", [T]), kit.sb("g", [2, T])
        gT = kit.sb("gT", [P])
        gps = kit.ps("gps", [P])
        uv, iso = keep["uv"], keep["iso"]
        a_in = kit.sems("a_in0 a_in1")
        (row_in, am_ready, used, link, g_ready, gt_ready, gt_copied, rows_out) = kit.sems(
            "row_in am_ready used link g_ready gt_ready gt_copied rows_out")

        with nc.Block() as block:
            @block.sync
            def _(sp):
                v = dram["rows"][T:2 * T, :].rearrange("(o t) p -> o (t p)", o=1)
                sp.dma_start(v_row[:], v.broadcast_to([P, NP])).then_inc(row_in, 16)
                for t in range(T):
                    if t >= 2:
                        sp.wait_ge(am_ready, t - 1)
                    sp.dma_start(a_rows[:, t % 2, :], dram["adj"][t * P:(t + 1) * P, :]).then_inc(a_in[t % 2], 16)
                sp.wait_ge(gt_copied, 1)
                sp.dma_start(dram["rows"][2 * T:4 * T, :], gT[0:2 * T, :]).then_inc(rows_out, 16)
                sp.wait_ge(rows_out, 16)

            @block.scalar
            def _(act):
                for t in range(T):
                    act.wait_ge(a_in[t % 2], 16 * (t // 2 + 1))
                    if t >= 2:
                        act.wait_ge(used, 2 * (t - 1))
                    act.activation(am[:, t % 2, :], a_rows[:, t % 2, :], ACT.Copy, scale=BIG, bias=-BIG).then_inc(am_ready, 1)

            @block.vector
            def _(dve):
                dve.wait_ge(row_in, 16)
                for t in range(T):
                    dve.wait_ge(am_ready, t + 1)
                    if t >= 1:
                        dve.wait_ge(used, 2 * t)
                    dve.tensor_tensor_reduce(scratch[:, 0, :], v_row[:], am[:, t % 2, :], 1.0, -3e38,
                                             ALU.add, ALU.max, vmax[:, t:t + 1]).then_inc(used, 1)
                    dve.tensor_tensor_reduce(scratch[:, 1, :], am[:, t % 2, :], v_row[:], 1.0, -3e38,
                                             ALU.subtract, ALU.max, nvmin[:, t:t + 1]).then_inc(used, 1)
                dve.wait_ge(used, 2 * T)
                step = [0]

                def then(ins):
                    step[0] += 1
                    ins.then_inc(link, 1)
                    dve.wait_ge(link, step[0])

                u = uv[:, 0, :]
                then(dve.tensor_scalar(iso[:], vmax[:], -CLAMP, None, ALU.is_lt))
                then(dve.tensor_scalar(keep["v08"][:], uv[:, 1, :], 0.8, None, ALU.mult))
                then(dve.tensor_scalar(keep["v02"][:], uv[:, 1, :], 0.2, None, ALU.mult))
                then(dve.scalar_tensor_tensor(s1[:], vmax[:], -CLAMP, u, ALU.max, ALU.add))
                then(dve.scalar_tensor_tensor(s2[:], s1[:], 0.2, s1[:], ALU.mult, ALU.max))
                then(dve.scalar_tensor_tensor(g[:, 0, :], u, 0.2, s2[:], ALU.mult, ALU.subtract))
                then(dve.tensor_scalar(s1[:], nvmin[:], -CLAMP, -1.0, ALU.max, ALU.mult))
                then(dve.tensor_tensor(s1[:], s1[:], u, ALU.add))
                then(dve.scalar_tensor_tensor(s2[:], s1[:], 0.2, s1[:], ALU.mult, ALU.max))
                then(dve.scalar_tensor_tensor(g[:, 1, :], u, -0.2, s2[:], ALU.mult, ALU.add))
                then(dve.tensor_scalar(s1[:], iso[:], -1.0, 1.0, ALU.mult, ALU.add))
                dve.tensor_tensor(g[:], g[:], s1[:].unsqueeze(1).broadcast_to([P, 2, T]), ALU.mult).then_inc(g_ready, 1)
                dve.wait_ge(gt_ready, 1)
                dve.tensor_copy(gT[0:2 * T, :], gps[0:2 * T, :]).then_inc(gt_copied, 1)

            @block.tensor
            def _(pe):
                pe.wait_ge(g_ready, 1)
                pe.transpose(gps[0:2 * T, :], g[:].rearrange("p s t -> p (s t)"), keep["ident"][:]).then_inc(gt_ready, 1)

        kit.close()


def attention0(nc, dram, keep):
    with ExitStack() as stack:
        kit = Kit(nc, stack, "m0")
        HJ = T // 2
        at32 = kit.sb("at32", [2, HJ, BW])
        at16 = kit.sb("at16", [2, HJ, BW], F16)
        u_row, g_row = kit.sb("u_row", [NP]), kit.sb("g_row", [2, NP])
        r = kit.sb("r", [2, BW])
        sc, e, pm = kit.sb("sc", [2, 2, BW]), kit.sb("e", [2, 2, BW]), kit.sb("pm", [2, 2, BW])
        p_hi, p_lo = kit.sb("p_hi", [2, 2, BW], F16), kit.sb("p_lo", [2, 2, BW], F16)
        o = kit.sb("o", [2, 2, D])
        x, ym, ye, yp = kit.sb("x", [2, D]), kit.sb("ym", [2, D]), kit.sb("ye", [2, D]), kit.sb("yp", [2, D])
        sums, den, rden = kit.sb("sums", [2, 2]), kit.sb("den", [2, 2]), kit.sb("rden", [2, 2])
        acc = kit.ps("acc", [2, 2, D])
        rowsum = kit.ps("rowsum", [512])
        z, cs = (keep["z_hi"], keep["z_lo"]), keep["cs0"]
        ones, iso = keep["ones16"], keep["iso"]
        at_in, at_used, at16_ready, at16_out = ([kit.sems(f"{n}{i}")[0] for i in range(2)] for n in
                                                ("at_in", "at_used", "at16_ready", "at16_out"))
        (rows_in, x_in, r_ready, sc_done, e_done, pm_done, hi_done, lo_done, p_done, acc_ready, acc_free, link,
         y_ready, ye_ready, yp_ready, x_ready, x_out, gate) = kit.sems(
            "rows_in x_in r_ready sc_done e_done pm_done hi_done lo_done p_done acc_ready acc_free link "
            "y_ready ye_ready yp_ready x_ready x_out gate")
        x_blocks = lambda name: dram[name].rearrange("(i q p) d -> i p q d", q=2, p=P)
        block_of = lambda ap, ib: ap[ds(ib, 1)].rearrange("o p q d -> p (o q) d")

        with nc.Block() as block:
            @block.sync
            def _(sp):
                for ring in (sc_done, e_done, pm_done, hi_done, lo_done, p_done):
                    sp.sem_inc(ring, 2)
                for single in (*at_used, *at16_ready, acc_free, ye_ready, x_ready):
                    sp.sem_inc(single, 1)
                for out in (*at16_out, x_out):
                    sp.sem_inc(out, 16)
                for n, row in enumerate((u_row[:], g_row[:, 0, :], g_row[:, 1, :])):
                    t0 = (0, 2 * T, 3 * T)[n]
                    src = dram["rows"][t0:t0 + T, :].rearrange("(o t) p -> o (t p)", o=1)
                    sp.dma_start(row, src.broadcast_to([P, NP])).then_inc(rows_in, 16)
                def mask_block(ib):
                    for half in range(2):
                        js = slice(half * HJ, (half + 1) * HJ)
                        sp.wait_ge(at_used[half], ib + 1)
                        wait_count(sp, at16_ready[half], ib + 1, gate)
                        sp.dma_start(at32[:, half], block_of(dram["adjT"][:, :, js, :], ib)).then_inc(at_in[half], 16)
                    for half in range(2):
                        js = slice(half * HJ, (half + 1) * HJ)
                        wait_count(sp, at16_ready[half], ib + 2, gate)
                        sp.dma_start(block_of(dram["at16"][:, :, js, :], ib), at16[:, half]).then_inc(at16_out[half], 16)

                def residual(ib):
                    wait_count(sp, x_out, ib * 16 + 16, gate)
                    sp.dma_start(x[:], block_of(x_blocks("x0"), ib)).then_inc(x_in, 16)
                    wait_count(sp, x_ready, ib + 2, gate)
                    sp.dma_start(block_of(x_blocks("x1"), ib), x[:]).then_inc(x_out, 16)

                mask_block(0)
                with sp.Fori(1, IB) as ib:
                    mask_block(ib)
                    residual(ib - 1)
                residual(IB - 1)
                sp.wait_ge(x_out, 16 * (IB + 1))
                for half in range(2):
                    sp.wait_ge(at16_out[half], 16 * (IB + 1))

            @block.gpsimd
            def _(pool):
                def convert(ib):
                    for half in range(2):
                        pool.wait_ge(at16_out[half], ib * 16 + 16)
                        wait_count(pool, at_in[half], ib * 16 + 16, gate)
                        pool.tensor_copy(at16[:, half], at32[:, half]).then_inc(at16_ready[half], 1)

                def finish(ib):
                    pool.wait_ge(x_in, ib * 16 + 16)
                    pool.wait_ge(y_ready, ib + 1)
                    pool.tensor_tensor(yp[:], yp[:], x[:], ALU.add).then_inc(yp_ready, 1)
                    pool.wait_ge(yp_ready, ib + 1)
                    pool.wait_ge(ye_ready, ib + 2)
                    pool.tensor_tensor(x[:], yp[:], ye[:], ALU.add).then_inc(x_ready, 1)

                convert(0)
                with pool.Fori(1, IB) as ib:
                    convert(ib)
                    finish(ib - 1)
                finish(IB - 1)

            @block.scalar
            def _(act):
                act.wait_ge(rows_in, 48)

                def relu(ib, j):
                    wait_count(act, sc_done, free(ib * T + j), gate)
                    act.activation(r[:, j % 2, :], u_row[:, ds(ib * BW, BW)], ACT.Relu,
                                   bias=keep["v08"][:, j:j + 1], scale=0.8).then_inc(r_ready, 1)

                def exp(ib, j):
                    act.wait_ge(sc_done, done(ib * T + j))
                    act.wait_ge(pm_done, free(ib * T + j))
                    act.activation(e[:, j % 2], sc[:, j % 2], ACT.Exp).then_inc(e_done, 1)

                def high(ib, j):
                    act.wait_ge(pm_done, done(ib * T + j))
                    act.wait_ge(p_done, free(ib * T + j))
                    act.activation(p_hi[:, j % 2], pm[:, j % 2], ACT.Copy).then_inc(hi_done, 1)

                def elu(ib):
                    act.wait_ge(y_ready, ib + 1)
                    act.wait_ge(x_ready, ib + 1)
                    act.activation(ye[:], ym[:], ACT.Exp).then_inc(ye_ready, 1)

                def one_block(ib, first):
                    relu(ib, 0)
                    relu(ib, 1)
                    exp(ib, 0)
                    for j in range(T):
                        if j + 2 < T:
                            relu(ib, j + 2)
                        if j + 1 < T:
                            exp(ib, j + 1)
                        high(ib, j)
                        if j == 5 and not first:
                            elu(ib - 1)

                one_block(0, True)
                with act.Fori(1, IB) as ib:
                    one_block(ib, False)
                elu(IB - 1)

            @block.vector
            def _(dve):
                dve.wait_ge(rows_in, 48)

                def scores(ib, j):
                    i = slice(None)
                    dve.wait_ge(r_ready, ib * T + j + 1)
                    dve.wait_ge(e_done, free(ib * T + j))
                    dve.scalar_tensor_tensor(sc[:, j % 2, 0, i], r[:, j % 2, :], keep["v02"][:, j:j + 1],
                                             g_row[:, 0, ds(ib * BW, BW)], ALU.add, ALU.add)
                    dve.scalar_tensor_tensor(sc[:, j % 2, 1, i], r[:, j % 2, :], keep["v02"][:, j:j + 1],
                                             g_row[:, 1, ds(ib * BW, BW)], ALU.add, ALU.subtract,
                                             reverse1=True).then_inc(sc_done, 1)

                def mask(ib, j):
                    if j % HJ == 0:
                        dve.wait_ge(at_in[j // HJ], ib * 16 + 16)
                    dve.wait_ge(e_done, done(ib * T + j))
                    dve.wait_ge(hi_done, free(ib * T + j))
                    dve.wait_ge(lo_done, free(ib * T + j))
                    m = at32[:, j // HJ, j % HJ, :].unsqueeze(1).broadcast_to([P, 2, BW])
                    last = dve.scalar_tensor_tensor(pm[:, j % 2], e[:, j % 2], 1.0, m, ALU.min, ALU.mult)
                    last.then_inc(pm_done, 1)
                    if j % HJ == HJ - 1:
                        dve.wait_ge(pm_done, done(ib * T + j))
                        dve.sem_inc(at_used[j // HJ], 1)

                def low(ib, j):
                    dve.wait_ge(hi_done, done(ib * T + j))
                    dve.wait_ge(p_done, free(ib * T + j))
                    dve.tensor_tensor(p_lo[:, j % 2], pm[:, j % 2], p_hi[:, j % 2], ALU.subtract).then_inc(lo_done, 1)

                def evacuate(ib):
                    dve.wait_ge(acc_ready, ib + 1)
                    dve.tensor_copy(sums[:].rearrange("p q s -> p (q s)"), rowsum[:, 0:4]).then_inc(link, 1)
                    for q in range(2):
                        for s in range(2):
                            last = dve.scalar_tensor_tensor(o[:, q, s, :], cs[:, s * D:(s + 1) * D], iso[:, ds(ib * 2 + q, 1)],
                                                            acc[:, q, s, :], ALU.mult, ALU.add)
                    last.then_inc(acc_free, 1)
                    dve.wait_ge(link, ib * 7 + 1)
                    for q in range(2):
                        dve.scalar_tensor_tensor(den[:, q, :], iso[:, ds(ib * 2 + q, 1)].broadcast_to([P, 2]), float(N),
                                                 sums[:, q, :], ALU.mult, ALU.add).then_inc(link, 1)
                    dve.wait_ge(link, ib * 7 + 3)
                    dve.reciprocal(rden[:], den[:]).then_inc(link, 1)
                    dve.wait_ge(link, ib * 7 + 4)
                    dve.wait_ge(acc_free, ib + 2)
                    for q in range(2):
                        last = dve.tensor_scalar(o[:, q, 1, :], o[:, q, 1, :], rden[:, q, 1:2], None, ALU.mult)
                    last.then_inc(link, 1)
                    dve.wait_ge(link, ib * 7 + 5)
                    for q in range(2):
                        last = dve.scalar_tensor_tensor(o[:, q, 0, :], o[:, q, 0, :], rden[:, q, 0:1], o[:, q, 1, :],
                                                        ALU.mult, ALU.subtract)
                    last.then_inc(link, 1)
                    dve.wait_ge(link, ib * 7 + 6)
                    dve.wait_ge(x_ready, ib + 1)
                    dve.tensor_scalar(ym[:], o[:, :, 0, :], 0.0, None, ALU.min).then_inc(link, 1)
                    dve.tensor_scalar(yp[:], o[:, :, 0, :], 0.0, -1.0, ALU.max, ALU.add).then_inc(y_ready, 1)
                    dve.wait_ge(link, ib * 7 + 7)

                def one_block(ib, first):
                    scores(ib, 0)
                    for j in range(T):
                        if j + 1 < T:
                            scores(ib, j + 1)
                        mask(ib, j)
                        if j > 0:
                            low(ib, j - 1)
                        if j == 1 and not first:
                            evacuate(ib - 1)
                    low(ib, T - 1)

                one_block(0, True)
                with dve.Fori(1, IB) as ib:
                    one_block(ib, False)
                evacuate(IB - 1)

            @block.tensor
            def _(pe):
                def products(ib, j):
                    if j == 0:
                        pe.wait_ge(acc_free, ib + 1)
                    pe.wait_ge(lo_done, done(ib * T + j))
                    for q in range(2):
                        i = slice(q * P, (q + 1) * P)
                        for s in range(2):
                            zs = [part[:, j, s * D:(s + 1) * D] for part in z]
                            col = rowsum[:, 2 * q + s:2 * q + s + 1]
                            hi, lo = p_hi[:, j % 2, s, i], p_lo[:, j % 2, s, i]
                            pe.matmul(acc[:, q, s, :], hi, zs[0], start=(j == 0), stop=False, skip_group_check=True)
                            pe.matmul(acc[:, q, s, :], hi, zs[1], start=False, stop=False, skip_group_check=True)
                            pe.matmul(col, hi, ones[:, 0:1], start=(j == 0 and q == 0 and s == 0), stop=False,
                                      skip_group_check=True)
                            pe.matmul(acc[:, q, s, :], lo, zs[0], start=False, stop=(j == T - 1), skip_group_check=True)
                            last = pe.matmul(col, lo, ones[:, 0:1], start=False, stop=(j == T - 1), skip_group_check=True)
                    last.then_inc(p_done, 1)
                    if j == T - 1:
                        pe.wait_ge(p_done, done(ib * T + j))
                        pe.sem_inc(acc_ready, 1)

                with pe.Fori(0, IB) as ib:
                    for j in range(T):
                        products(ib, j)

        kit.close()

def prep1(nc, dram, keep):
    with ExitStack() as stack:
        kit = Kit(nc, stack, "p1")
        x_all, h = kit.sb("x_all", [T, D]), kit.sb("h", [2, D])
        hT_hi, hT_lo = kit.sb("hT_hi", [2, KC, P], F16), kit.sb("hT_lo", [2, KC, P], F16)
        NX = D + 2 * H
        w = kit.sb("w", [KC, NX])
        w_hi, w_lo = kit.sb("w_hi", [KC, NX], F16), kit.sb("w_lo", [KC, NX], F16)
        a12, a12s, prod = kit.sb("a12", [2 * H, DH]), kit.sb("a12s", [2 * H, DH]), kit.sb("prod", [2 * H, DH])
        aln, bln, wsum = kit.sb("aln", [DH]), kit.sb("bln", [DH]), kit.sb("wsum", [H])
        ab = kit.sb("ab", [2 * H])
        stats, mv = kit.sb("stats", [T, 6]), kit.sb("mv", [T, 2])
        std, rstd, nmr = kit.sb("std", [T]), kit.sb("rstd", [T]), kit.sb("nmr", [T])
        sq, c_out = kit.sb("sq", [2, D]), kit.sb("c_out", [2, D])
        ss, at = kit.sb("ss", [H, T]), kit.sb("at", [2 * H, T])
        valid, gm, gall = kit.sb("valid", [T]), kit.sb("gm", [H]), kit.sb("gall", [H])
        t1, t2 = kit.sb("t1", [H, T]), kit.sb("t2", [H, T])
        upT = kit.sb("upT", [2, P])
        tp = kit.ps("tp", [2, KC, P])
        main = kit.ps("main", [2, D])
        small = kit.ps("small", [2, 256])
        r, f1, f2, d1, d2, nv = (keep[n] for n in ("r1", "f1", "f2", "d1", "d2", "nv"))
        x_in = kit.sems(" ".join(f"x_in{c}" for c in range(len(CHUNKS))))
        s = dict(zip("stats mv var std rstd nmr w_hi w_lo".split(),
                     kit.sems("stats mv var std rstd nmr w_hi w_lo")))
        c_stored = kit.sems("c_stored0 c_stored1")
        (w_in, a_in, link, h_ready, tp_ready, hi_ready, lo_done, prod_done, c_made, sq_made, ss_done,
         dots_done, sd_need, sd_made, g_made, g_all, e_need, e_made, up_ready, upt_made, upt_copied,
         rows_out) = kit.sems(
            "w_in a_in link h_ready tp_ready hi_ready lo_done prod_done c_made sq_made ss_done "
            "dots_done sd_need sd_made g_made g_all e_need e_made up_ready upt_made upt_copied rows_out")
        x_t = tiles(dram["x1"])

        with nc.Block() as block:
            @block.sync
            def _(sp):
                for ring in (lo_done, prod_done, c_made, sq_made, ss_done, dots_done):
                    sp.sem_inc(ring, 2)
                for stored in c_stored:
                    sp.sem_inc(stored, 16)
                sp.dma_start(w[:, :, 0:D], dram["w1"].rearrange("(k p) n -> p k n", p=P)).then_inc(w_in, 16)
                for n, name in enumerate(("a1", "a2")):
                    sp.dma_start(a12[:, n * H:(n + 1) * H, :].rearrange("p g e -> p (g e)"),
                                 dram[name].broadcast_to([P, D])).then_inc(a_in, 16)
                sp.dma_start(aln[:], dram["aln"].broadcast_to([P, DH])).then_inc(a_in, 16)
                sp.dma_start(bln[:], dram["bln"].broadcast_to([P, DH])).then_inc(a_in, 16)
                sp.dma_start(valid[:], dram["valid"]).then_inc(a_in, 16)
                for c, (t0, n) in enumerate(CHUNKS):
                    sp.dma_start(x_all[:, t0:t0 + n, :], x_t[:, t0:t0 + n, :]).then_inc(x_in[c], 16)

                def store(t, b):
                    sp.wait_ge(c_made, done(t))
                    sp.dma_start(dram["c1"].rearrange("(t p) d -> t p d", p=P)[ds(t, 1)].rearrange("o p d -> p (o d)"),
                                 c_out[:, b, :]).then_inc(c_stored[b], 16)

                loop_tiles(sp, store)
                for stored in c_stored:
                    sp.wait_ge(stored, 16 * (T // 2 + 1))
                sp.wait_ge(upt_copied, 1)
                for n in range(2):
                    sp.dma_start(dram["rows1"][n * 4 * T:(n + 1) * 4 * T, :], upT[0:4 * T, n, :]).then_inc(rows_out, 16)
                sp.wait_ge(rows_out, 32)

            @block.scalar
            def _(act):
                act.wait_ge(s["var"], 1)
                act.activation(std[:], std[:], ACT.Sqrt).then_inc(s["std"], 1)
                act.wait_ge(s["nmr"], 1)

                def normalise(t, b):
                    act.wait_ge(tp_ready, free(t))
                    act.activation(h[:, b, :], flat(x_all[:, ds(t, 1), :]), ACT.Relu,
                                   bias=nmr[:, ds(t, 1)], scale=rstd[:, ds(t, 1)]).then_inc(h_ready, 1)

                def high(t, b):
                    act.wait_ge(tp_ready, done(t))
                    act.wait_ge(prod_done, free(t))
                    act.activation(hT_hi[:, b], tp[:, b], ACT.Copy).then_inc(hi_ready, 1)

                def finish(t, b):
                    act.wait_ge(prod_done, done(t))
                    act.wait_ge(c_stored[b], 8 * (t - b) + 16)
                    act.activation(c_out[:, b, :], main[:, b, :], ACT.Copy, scale=1 / WS).then_inc(c_made, 1)
                    act.wait_ge(ss_done, free(t))
                    act.activation(sq[:, b, :], main[:, b, :], ACT.Square, scale=1 / WS).then_inc(sq_made, 1)

                act.sem_inc(tp_ready, 2)
                loop_with_two_next(act, finish, high, normalise)
                act.wait_ge(sd_need, 1)
                act.activation(ss[:], ss[:], ACT.Sqrt, scale=1 / (DH - 1)).then_inc(sd_made, 1)
                act.wait_ge(e_need, 1)
                for n, (to, of, by) in enumerate(((d1, nv, -1.0), (d2, nv, -0.2), (f1, t1, 0.8), (f2, t2, -0.8))):
                    act.activation(to[:], of[:], ACT.Exp, scale=by).then_inc(e_made, 1)

            @block.tensor
            def _(pe):
                pe.wait_ge(s["w_lo"], 1)

                def transpose(t, b):
                    pe.wait_ge(h_ready, t + 1)
                    pe.wait_ge(lo_done, free(t))
                    for k in range(KC):
                        last = pe.transpose(tp[:, b, k, :], h[:, b, k * P:(k + 1) * P], keep["ident"][:])
                    last.then_inc(tp_ready, 1)

                def products(t, b):
                    pe.wait_ge(lo_done, done(t))
                    pe.wait_ge(sq_made, free(t))
                    split_product(pe, main[:, b, :], hT_hi[:, b], hT_lo[:, b], w_hi, w_lo, slice(0, D))
                    pe.wait_ge(dots_done, done(t - 1))
                    last = split_product(pe, small[:, b, 0:2 * H], hT_hi[:, b], hT_lo[:, b], w_hi, w_lo, slice(D, NX))
                    last.then_inc(prod_done, 1)

                loop_with_next(pe, products, transpose)
                pe.wait_ge(up_ready, 1)
                for n in range(2):
                    last = pe.transpose(tp[0:4 * T, n, 0, :], t1[:, 4 * n:4 * n + 4, :].rearrange("p h t -> p (h t)"), keep["ident"][:])
                last.then_inc(upt_made, 1)

            @block.gpsimd
            def _(pool):
                pool.wait_ge(g_made, 1)
                pool.partition_all_reduce(gall[:], gm[:], P, RMAX).then_inc(g_all, 1)

            @block.vector
            def _(dve):
                step = [0]

                def then(ins):
                    step[0] += 1
                    ins.then_inc(link, 1)
                    dve.wait_ge(link, step[0])

                heads = lambda ap: ap.rearrange("p (h e) -> p h e", e=DH)
                dve.wait_ge(a_in, 80)
                then(dve.tensor_tensor(prod[:], a12[:], bln[:].unsqueeze(1).broadcast_to([P, 2 * H, DH]), ALU.mult))
                then(dve.tensor_reduce(ab[:], prod[:], AXX, ALU.add))
                then(dve.tensor_tensor(a12s[:], a12[:], aln[:].unsqueeze(1).broadcast_to([P, 2 * H, DH]), ALU.mult))
                dve.wait_ge(w_in, 16)
                for k in range(KC):
                    then(dve.tensor_reduce(wsum[:], heads(w[:, k, 0:D]), AXX, ALU.add))
                    then(dve.scalar_tensor_tensor(heads(w[:, k, 0:D]), wsum[:].unsqueeze(2).broadcast_to([P, H, DH]), -1.0 / DH,
                                                  heads(w[:, k, 0:D]), ALU.mult, ALU.add))
                    for n in range(2):
                        then(dve.tensor_tensor(prod[:, 0:H, :], heads(w[:, k, 0:D]), a12s[:, n * H:(n + 1) * H, :], ALU.mult))
                        then(dve.tensor_reduce(w[:, k, D + n * H:D + (n + 1) * H], prod[:, 0:H, :], AXX, ALU.add))
                split_weights(dve, w, w_hi, w_lo, s)
                norm_statistics(dve, x_all, stats, mv, std, rstd, nmr, lambda c: dve.wait_ge(x_in[c], 16), s)

                def split(t, b):
                    dve.wait_ge(hi_ready, t + 1)
                    dve.tensor_tensor(hT_lo[:, b], tp[:, b], hT_hi[:, b], ALU.subtract).then_inc(lo_done, 1)

                def finish(t, b):
                    dve.wait_ge(prod_done, done(t))
                    dve.tensor_scalar(at[:, :, ds(t, 1)], small[:, b, 0:2 * H].unsqueeze(2), 1 / WS, None,
                                      ALU.mult).then_inc(dots_done, 1)
                    dve.wait_ge(sq_made, done(t))
                    dve.tensor_reduce(ss[:, :, ds(t, 1)], heads(sq[:, b, :]), AXX, ALU.add).then_inc(ss_done, 1)

                loop_with_next(dve, finish, split)
                dve.wait_ge(ss_done, done(T - 1))
                dve.sem_inc(sd_need, 1)
                dve.wait_ge(sd_made, 1)
                then(dve.tensor_scalar(ss[:], ss[:], 1e-6, None, ALU.add))
                then(dve.reciprocal(r[:], ss[:]))
                for n in range(2):
                    then(dve.tensor_tensor(at[:, n * H:(n + 1) * H, :], at[:, n * H:(n + 1) * H, :], r[:], ALU.mult))
                then(dve.tensor_tensor(at[:], at[:], ab[:].unsqueeze(2).broadcast_to([P, 2 * H, T]), ALU.add))
                then(dve.tensor_tensor(r[:], r[:], valid[:].unsqueeze(1).broadcast_to([P, H, T]), ALU.mult))
                dve.tensor_reduce(gm[:], at[:, H:2 * H, :], AXX, ALU.max).then_inc(g_made, 1)
                dve.wait_ge(g_all, 1)
                g = gall[:].unsqueeze(2).broadcast_to([P, H, T])
                then(dve.tensor_tensor(nv[:], g, at[:, H:2 * H, :], ALU.subtract))
                then(dve.tensor_tensor(t1[:], at[:, 0:H, :], g, ALU.add))
                dve.sem_inc(up_ready, 1)
                dve.wait_ge(upt_made, 1)
                for n in range(2):
                    last = dve.tensor_copy(upT[0:4 * T, n, :], tp[0:4 * T, n, 0, :])
                last.then_inc(upt_copied, 1)
                then(dve.tensor_scalar(t2[:], t1[:], 0.0, None, ALU.max))
                then(dve.tensor_scalar(t1[:], t1[:], 0.0, None, ALU.min))
                dve.sem_inc(e_need, 1)
                dve.wait_ge(e_made, 4)
                then(dve.tensor_scalar(d1[:], d1[:], YS, None, ALU.mult))
                then(dve.tensor_scalar(d2[:], d2[:], YS, None, ALU.mult))

        kit.close()


YS = 4096.0
STEEP = 2.0 ** 80
LS = 2048.0
YW = DH + 1
BLOCKS = [(2 * i, min(2, IB - 2 * i)) for i in range(-(-IB // 2))]


def attention1(nc, dram, keep):
    with ExitStack() as stack:
        kit = Kit(nc, stack, "m1")
        NB = len(BLOCKS)
        at = kit.sb("at", [IB, T, BW], F16)
        u = kit.sb("u", [2, 2, BW])
        c = kit.sb("c", [2, T, DH])
        yf = kit.sb("yf", [T, YW])
        y12 = kit.sb("y12", [2, T, 2, 2, YW], F16)
        y2 = kit.sb("y2", [2, T, 2, YW], F16)
        nvk, nvs = kit.sb("nvk", [2, T]), kit.sb("nvs", [2, T])
        above = kit.sb("above", [2, 2, BW], BF16)
        b01 = kit.sb("b01", [4, 2, BW], F16)
        lowp, both = kit.sb("lowp", [4, 2, YW]), kit.sb("both", [2, 4, 2, YW])
        num, part = kit.sb("num", [4, YW]), kit.sb("part", [4, YW])
        rden, yo = kit.sb("rden", [4]), kit.sb("yo", [2, 4, DH])
        csp, cs = kit.sb("csp", [2, DH]), kit.sb("cs", [2, YW])
        acc = kit.ps("acc", [2, 4, 512])
        r, f1, f2, d1, d2, nv = (keep[n] for n in ("r1", "f1", "f2", "d1", "d2", "nv"))
        iso = keep["iso"]
        at_in, u_in, c_in, y_out = (kit.sems(n) for n in
                                    (" ".join(f"at_in{i}" for i in range(NB)), "u_in0 u_in1", "c_in0 c_in1", "y_out0 y_out1"))
        (u_done, nvk_made, nvs_made, above_made, chat_made, yf_made, yhi_made, diff_made, ylo_made, b_ready, b_used, acc_free,
         low_made, both_made, den_made, rden_made, y_made, csp_made, cs_made, head_done, link, gate) = kit.sems(
            "u_done nvk_made nvs_made above_made chat_made yf_made yhi_made diff_made ylo_made b_ready b_used acc_free "
            "low_made both_made den_made rden_made y_made csp_made cs_made head_done link gate")

        SHARED = [list(range({2: T, 3: T, 4: 7}.get(n, 3), T, 2)) for n in range(NB)]
        EARLY = (0, 1, 4, 5)
        shares = [(n, j) for n in range(NB) for j in SHARED[n]]

        def acc_view(bank, nt):
            return acc[:, bank, 0:nt, 0:4 * YW].rearrange("p t (l y e) -> p t l y e", l=2, y=2)

        with nc.Block() as block:
            @block.sync
            def _(sp):
                sp.sem_inc(b_used, 4)
                sp.sem_inc(acc_free, 2)
                sp.sem_inc(head_done, 2)
                for out in y_out:
                    sp.sem_inc(out, 16)

                def load_c(k, b):
                    sp.dma_start(c[:, b], dram["c1"].rearrange("(t p) (k e) -> k p t e", p=P, e=DH)[ds(k, 1)].rearrange(
                        "o p t e -> p (o t) e")).then_inc(c_in[b], 16)

                def load_u(k, n):
                    i0, nb = BLOCKS[n]
                    src = dram["rows1"].rearrange("(k t) p -> k (t p)", k=H)[ds(k, 1), i0 * BW:(i0 + nb) * BW]
                    sp.dma_start(u[:, n % 2, 0:nb, :].rearrange("p n c -> p (n c)"),
                                 src.broadcast_to([P, nb * BW])).then_inc(u_in[n % 2], 16)

                def head(k, b, more, last):
                    for n, (i0, nb) in enumerate(BLOCKS):
                        g = k * NB + n
                        if n + 2 < NB or not last:
                            sp.wait_ge(u_done, g + 1)
                            load_u(k if n + 2 < NB else k + 1, (n + 2) % NB)
                        wait_count(sp, y_made, g + 1, gate)
                        sp.dma_start(dram["y1"].rearrange("(t p) (k e) -> k p t e", p=P, e=DH)[ds(k, 1), :, 2 * i0:2 * (i0 + nb), :].rearrange(
                            "o p t e -> p (o t) e"), yo[:, n % 2, 0:2 * nb, :]).then_inc(y_out[n % 2], 16)
                    if more:
                        load_c(k + 2, b)

                load_c(0, 0)
                load_u(0, 0)
                for i, (i0, nb) in enumerate(BLOCKS):
                    sp.dma_start(at[:, i0:i0 + nb], dram["at16"].rearrange("i p t c -> p i t c")[:, i0:i0 + nb]).then_inc(at_in[i], 16)
                    if i == 0:
                        load_u(0, 1)
                        load_c(1, 1)
                with sp.Fori(0, H - 3, 2) as k:
                    for b in range(2):
                        head(k + b, b, True, False)
                head(H - 2, 0, False, False)
                head(H - 1, 1, False, True)
                for out in y_out:
                    sp.wait_ge(out, 16 * (H * NB // 2 + 1))

            @block.gpsimd
            def _(pool):
                def scale_head(k, b):
                    pool.wait_ge(head_done, free(k))
                    wait_count(pool, c_in[b], (k - b) * 8 + 16, gate)
                    pool.tensor_copy(nvk[:, b, :].unsqueeze(1), nv[:, ds(k, 1), :]).then_inc(nvk_made, 1)
                    wait_count(pool, nvk_made, k + 1, gate)
                    pool.tensor_scalar(nvs[:, b, :], nvk[:, b, :], -STEEP, None, ALU.mult).then_inc(nvs_made, 1)
                    pool.tensor_tensor(c[:, b], c[:, b], r[:, ds(k, 1), :].rearrange("p o t -> p (o t)").unsqueeze(2).broadcast_to([P, T, DH]),
                                       ALU.mult).then_inc(chat_made, 1)

                def build(k, b, n):
                    if n == 0:
                        wait_count(pool, chat_made, k + 1, gate)
                    dk = (d1, d2)[n][:, ds(k, 1), :].rearrange("p o t -> p (o t)").unsqueeze(2)
                    if not (isinstance(k, int) and k == 0 and n == 0):
                        wait_count(pool, ylo_made, 2 * k + n, gate)
                    pool.tensor_tensor(yf[:, :, 0:DH], c[:, b], dk.broadcast_to([P, T, DH]), ALU.mult).then_inc(yf_made, 1)
                    pool.tensor_copy(yf[:, :, DH:YW], dk).then_inc(yf_made, 1)
                    hi = y12[:, b, :, 0, 0, :] if n == 0 else y2[:, b, :, 0, :]
                    pool.wait_ge(yhi_made, 2 * k + n + 1)
                    pool.tensor_tensor(yf[:], yf[:], hi, ALU.subtract).then_inc(diff_made, 1)

                def column_sums(k, b):
                    wait_count(pool, csp_made, k + 1, gate)
                    pool.partition_all_reduce(cs[:, 0, 0:DH], csp[:, 0, :], P, RADD).then_inc(cs_made, 1)
                    wait_count(pool, cs_made, k + 1, gate)
                    pool.tensor_scalar(cs[:, 0, 0:DH], cs[:, 0, 0:DH], YS, None, ALU.mult).then_inc(link, 1)

                def numerator(k, b, n):
                    i0, nb = BLOCKS[n]
                    nt, t0, g = 2 * nb, 2 * i0, k * NB + n
                    steps = g * 6 + k + 2
                    of = lambda f: f[:, ds(k, 1), t0:t0 + nt].rearrange("p o t -> p (o t)").unsqueeze(2).broadcast_to([P, nt, YW])
                    pool.wait_ge(both_made, g + 1)
                    pool.wait_ge(link, steps)
                    pool.tensor_tensor(num[:, 0:nt], both[:, n % 2, 0:nt, 0, :], of(f1), ALU.mult).then_inc(link, 1)
                    pool.tensor_tensor(part[:, 0:nt], both[:, n % 2, 0:nt, 1, :], of(f2), ALU.mult).then_inc(link, 1)
                    pool.wait_ge(link, steps + 2)
                    pool.tensor_tensor(num[:, 0:nt], num[:, 0:nt], part[:, 0:nt], ALU.add).then_inc(link, 1)
                    pool.wait_ge(link, steps + 3)
                    pool.tensor_tensor(part[:, 0:nt], cs[:, 0, :].unsqueeze(1).broadcast_to([P, nt, YW]),
                                       iso[:, t0:t0 + nt].unsqueeze(2).broadcast_to([P, nt, YW]), ALU.mult).then_inc(link, 1)
                    pool.wait_ge(link, steps + 4)
                    pool.tensor_tensor(num[:, 0:nt], num[:, 0:nt], part[:, 0:nt], ALU.add).then_inc(den_made, 1)

                def quotient(k, b, n):
                    i0, nb = BLOCKS[n]
                    nt, t0, g = 2 * nb, 2 * i0, k * NB + n
                    steps = g * 6 + k + 2
                    pool.wait_ge(rden_made, g + 1)
                    pool.wait_ge(y_out[n % 2], (k * NB + n - n % 2) * 8 + 16)
                    pool.tensor_tensor(yo[:, n % 2, 0:nt], num[:, 0:nt, 0:DH], rden[:, 0:nt].unsqueeze(2).broadcast_to([P, nt, DH]),
                                       ALU.mult).then_inc(link, 1)
                    pool.wait_ge(link, steps + 5)
                    pool.tensor_tensor(yo[:, n % 2, 0:nt], yo[:, n % 2, 0:nt], c[:, b, t0:t0 + nt], ALU.add).then_inc(y_made, 1)
                    pool.wait_ge(y_made, g + 1)
                    pool.sem_inc(link, 1)

                def head(k, b, more):
                    column_sums(k, b)
                    for n in range(NB):
                        numerator(k, b, n)
                        if more and n == 0:
                            scale_head(k + 1, 1 - b)
                        if more and n in (1, 2):
                            build(k + 1, 1 - b, n - 1)
                        quotient(k, b, n)

                pool.memset(cs[:], float(N) * YS).then_inc(link, 1)
                pool.wait_ge(link, 1)
                scale_head(0, 0)
                build(0, 0, 0)
                build(0, 0, 1)
                with pool.Fori(0, H - 3, 2) as k:
                    for b in range(2):
                        head(k + b, b, True)
                head(H - 2, 0, True)
                head(H - 1, 1, False)

            @block.scalar
            def _(act):
                def split(k, b, n):
                    hi = y12[:, b, :, 0, 0, :] if n == 0 else y2[:, b, :, 0, :]
                    lo = y12[:, b, :, 1, 0, :] if n == 0 else y2[:, b, :, 1, :]
                    if n == 0:
                        act.wait_ge(head_done, free(k))
                    act.wait_ge(yf_made, 4 * k + 2 * n + 2)
                    act.activation(hi, yf[:], ACT.Copy).then_inc(yhi_made, 1)
                    if n == 1:
                        act.wait_ge(yhi_made, 2 * k + 2)
                        act.activation(y12[:, b, :, 0, 1, :], hi, ACT.Copy, scale=-1.0)
                    act.wait_ge(diff_made, 2 * k + n + 1)
                    if n == 1:
                        act.activation(y12[:, b, :, 1, 1, :], yf[:], ACT.Copy, scale=-LS)
                    act.activation(lo, yf[:], ACT.Copy, scale=LS).then_inc(ylo_made, 1)

                def low(k, n):
                    i0, nb = BLOCKS[n]
                    g = k * NB + n
                    act.wait_ge(b_used, (g + 1) * T + 4)
                    act.wait_ge(both_made, g) if not (isinstance(g, int) and g == 0) else None
                    act.activation(lowp[:, 0:2 * nb], acc_view(n % 2, 2 * nb)[:, :, 1], ACT.Copy, scale=1 / LS).then_inc(low_made, 1)

                def compare(k, b, n, j):
                    i = shares.index((n, j))
                    n2, j2 = shares[i - 2]
                    if i >= 2:
                        act.wait_ge(b_ready, (k * NB + n2) * T + j2 + 1)
                    elif not (isinstance(k, int) and k == 0):
                        act.wait_ge(b_ready, ((k - 1) * NB + n2) * T + j2 + 1)
                    nb = BLOCKS[n][1]
                    act.activation(above[:, i % 2, 0:nb], u[:, n % 2, 0:nb], ACT.Relu, bias=nvs[:, b, j:j + 1],
                                   scale=STEEP).then_inc(above_made, 1)

                def early(k, b, n):
                    if n == 0:
                        act.wait_ge(nvs_made, k + 1)
                    act.wait_ge(u_in[n % 2], (k * NB + n - n % 2) * 8 + 16)
                    for j in SHARED[n][:2]:
                        compare(k, b, n, j)

                def head(k, b, more):
                    for n in range(NB):
                        if SHARED[n] and n not in EARLY:
                            act.wait_ge(u_in[n % 2], (k * NB + n - n % 2) * 8 + 16)
                        for j in SHARED[n][2:] if n in EARLY else SHARED[n]:
                            compare(k, b, n, j)
                        if n + 1 in EARLY:
                            early(k, b, n + 1)
                        elif n == NB - 1 and more:
                            early(k + 1, 1 - b, 0)
                        low(k, n)
                        if more and n in (1, 2):
                            split(k + 1, 1 - b, n - 1)

                early(0, 0, 0)
                split(0, 0, 0)
                split(0, 0, 1)
                with act.Fori(0, H - 3, 2) as k:
                    for b in range(2):
                        head(k + b, b, True)
                head(H - 2, 0, True)
                head(H - 1, 1, False)

            @block.vector
            def _(dve):
                def combine(k, n):
                    i0, nb = BLOCKS[n]
                    g = k * NB + n
                    dve.wait_ge(low_made, g + 1)
                    dve.tensor_tensor(both[:, n % 2, 0:2 * nb], acc_view(n % 2, 2 * nb)[:, :, 0], lowp[:, 0:2 * nb],
                                      ALU.add).then_inc(both_made, 1)
                    dve.wait_ge(both_made, g + 1)
                    dve.sem_inc(acc_free, 1)

                def divide(k, n):
                    i0, nb = BLOCKS[n]
                    dve.wait_ge(den_made, k * NB + n + 1)
                    dve.reciprocal(rden[:, 0:2 * nb], num[:, 0:2 * nb, DH]).then_inc(rden_made, 1)

                def sum_head(k, b):
                    dve.wait_ge(chat_made, k + 1)
                    dve.tensor_reduce(csp[:, 0, :], c[:, b].rearrange("p t e -> p e t"), AXX, ALU.add).then_inc(csp_made, 1)

                def head(k, b, first=False, last=False):
                    dve.wait_ge(nvk_made, k + 1)
                    for n, (i0, nb) in enumerate(BLOCKS):
                        g = k * NB + n
                        before = (k, n - 1) if n > 0 else (k - 1, NB - 1)
                        if first:
                            dve.wait_ge(at_in[n], 16)
                        dve.wait_ge(u_in[n % 2], (g - n % 2) * 8 + 16)
                        for j in range(T):
                            m = g * T + j
                            dve.wait_ge(b_used, m + 1)
                            to, mask = b01[:, (n * T + j) % 4, 0:nb], at[:, i0:i0 + nb, j, :]
                            if j in SHARED[n]:
                                i = shares.index((n, j))
                                dve.wait_ge(above_made, k * len(shares) + i + 1)
                                dve.tensor_tensor(to, above[:, i % 2, 0:nb], mask, ALU.min).then_inc(b_ready, 1)
                            else:
                                dve.scalar_tensor_tensor(to, u[:, n % 2, 0:nb], nvk[:, b, j:j + 1], mask,
                                                         ALU.is_gt, ALU.mult).then_inc(b_ready, 1)
                            if j == 5 and not (first and n == 0):
                                combine(*before)
                            if j == 13 and not (first and n == 0):
                                divide(*before)
                            if j == 17 and n == NB - 2 and not last:
                                sum_head(k + 1, 1 - b)
                        dve.wait_ge(b_ready, (g + 1) * T)
                        dve.sem_inc(u_done, 1)

                sum_head(0, 0)
                head(0, 0, first=True)
                with dve.Fori(1, H - 2, 2) as k:
                    for b in range(2):
                        head(k + b, 1 - b)
                head(H - 1, 1, last=True)
                combine(H - 1, NB - 1)
                divide(H - 1, NB - 1)

            @block.tensor
            def _(pe):
                def head(k, b, first=False):
                    pe.wait_ge(ylo_made, 2 * k + 2)
                    for n, (i0, nb) in enumerate(BLOCKS):
                        g = k * NB + n
                        pe.wait_ge(acc_free, free(g))
                        if first:
                            pe.wait_ge(at_in[n], 16)
                        for j in range(T):
                            pe.wait_ge(b_ready, g * T + j + 1)
                            for q in range(2 * nb):
                                half = slice((q % 2) * P, (q % 2 + 1) * P)
                                full = acc_view(n % 2, 2 * nb)[:, q]
                                pe.matmul(full.rearrange("p l y e -> p (l y e)"), b01[:, (n * T + j) % 4, q // 2, half],
                                          y12[:, b, j].rearrange("p l y e -> p (l y e)"), start=(j == 0), stop=False,
                                          skip_group_check=True)
                                last = pe.matmul(full[:, :, 1, :], at[:, i0 + q // 2, j, half], y2[:, b, j],
                                                 start=False, stop=(j == T - 1), skip_group_check=True)
                            last.then_inc(b_used, 1)
                    pe.sem_inc(head_done, 1)

                head(0, 0, first=True)
                with pe.Fori(1, H - 2, 2) as k:
                    for b in range(2):
                        head(k + b, 1 - b)
                head(H - 1, 1)

        kit.close()

XS = 2.0 ** -10
EMIN = 2.0 ** -25


def prep2(nc, dram, keep):
    with ExitStack() as stack:
        kit = Kit(nc, stack, "p2")
        x_all, h = kit.sb("x_all", [T, D]), kit.sb("h", [2, D])
        hT_hi, hT_lo = kit.sb("hT_hi", [2, KC, P], F16), kit.sb("hT_lo", [2, KC, P], F16)
        w = kit.sb("w", [KC, D])
        w_hi, w_lo = kit.sb("w_hi", [KC, D], F16), kit.sb("w_lo", [KC, D], F16)
        y, low, el = kit.sb("y", [2, 6, D]), kit.sb("low", [6, D]), kit.sb("el", [6, D])
        aln, bln = kit.sb("aln", [DH]), kit.sb("bln", [DH])
        stats, mv = kit.sb("stats", [T, 6]), kit.sb("mv", [T, 2])
        std, rstd, nmr = kit.sb("std", [T]), kit.sb("rstd", [T]), kit.sb("nmr", [T])
        sq = kit.sb("sq", [2, 2, D])
        ssq = kit.sb("ssq", [2, T])
        v = kit.sb("v", [10, T])
        tp = kit.ps("tp", [2, KC, P])
        main = kit.ps("main", [2, D])
        xs_hi, xs_lo, gcol = keep["xs_hi"], keep["xs_lo"], keep["gcol"]
        x_in = kit.sems(" ".join(f"x_in{c}" for c in range(len(CHUNKS))))
        y_in = kit.sems(" ".join(f"y_in{c}" for c in range(len(CHUNKS))))
        s = dict(zip("stats mv var std rstd nmr w_hi w_lo".split(),
                     kit.sems("stats mv var std rstd nmr w_hi w_lo")))
        (w_in, a_in, bln_made, scaled, y_made, low_made, el_made, plus_made, sum_made, x_made, x_out, h_ready, hsq_made, hss_done, tp_ready,
         hi_ready, lo_done, prod_done, m_made, msq_made, ssq_done, link, asked, answered, xs_made, hi_made, diff_made,
         g_made, used) = kit.sems(
            "w_in a_in bln_made scaled y_made low_made el_made plus_made sum_made x_made x_out h_ready hsq_made hss_done tp_ready "
            "hi_ready lo_done prod_done m_made msq_made ssq_done link asked answered xs_made hi_made diff_made "
            "g_made used")
        x_t, y_t = tiles(dram["x1"]), tiles(dram["y1"])
        hn, mn, t1, t2, ln, tt, ee, th, ga, co = (v[:, i, :] for i in range(10))

        with nc.Block() as block:
            @block.sync
            def _(sp):
                for ring in (lo_done, prod_done, msq_made, ssq_done, hss_done):
                    sp.sem_inc(ring, 2)
                sp.dma_start(aln[:], dram["aln"].broadcast_to([P, DH])).then_inc(a_in, 16)
                sp.dma_start(bln[:], dram["bln"].broadcast_to([P, DH])).then_inc(a_in, 16)
                for c, (t0, n) in enumerate(CHUNKS):
                    if c >= 2:
                        sp.wait_ge(x_made, c - 1)
                    sp.dma_start(y[:, c % 2, 0:n, :], y_t[:, t0:t0 + n, :]).then_inc(y_in[c], 16)
                    sp.dma_start(x_all[:, t0:t0 + n, :], x_t[:, t0:t0 + n, :]).then_inc(x_in[c], 16)
                    if c == 0:
                        sp.dma_start(w[:], dram["w2"].rearrange("(k p) n -> p k n", p=P)).then_inc(w_in, 16)
                for c, (t0, n) in enumerate(CHUNKS):
                    sp.wait_ge(x_made, c + 1)
                    sp.dma_start(tiles(dram["x2"])[:, t0:t0 + n, :], x_all[:, t0:t0 + n, :]).then_inc(x_out, 16)
                sp.wait_ge(x_out, 16 * len(CHUNKS))

            @block.gpsimd
            def _(pool):
                pool.wait_ge(a_in, 32)
                pool.tensor_tensor(bln[:], bln[:], bln[:], ALU.add).then_inc(bln_made, 1)
                pool.wait_ge(bln_made, 1)
                for c, (t0, n) in enumerate(CHUNKS):
                    yc = y[:, c % 2, 0:n, :].rearrange("p n (h e) -> p (n h) e", e=DH)
                    pool.wait_ge(y_in[c], 16)
                    pool.tensor_tensor(yc, yc, aln[:].unsqueeze(1).broadcast_to([P, n * H, DH]), ALU.mult).then_inc(scaled, 1)
                    pool.wait_ge(scaled, c + 1)
                    pool.tensor_tensor(yc, yc, bln[:].unsqueeze(1).broadcast_to([P, n * H, DH]), ALU.add).then_inc(y_made, 1)

            @block.scalar
            def _(act):
                for c, (t0, n) in enumerate(CHUNKS):
                    act.wait_ge(low_made, c + 1)
                    act.activation(el[:, 0:n, :], low[:, 0:n, :], ACT.Exp).then_inc(el_made, 1)
                act.wait_ge(s["var"], 1)
                act.activation(std[:], std[:], ACT.Sqrt).then_inc(s["std"], 1)
                act.wait_ge(s["nmr"], 1)
                act.wait_ge(x_out, 16 * len(CHUNKS))

                def normalise(t, b):
                    act.wait_ge(tp_ready, free(t))
                    act.wait_ge(hss_done, free(t))
                    act.activation(h[:, b, :], flat(x_all[:, ds(t, 1), :]), ACT.Relu,
                                   bias=nmr[:, ds(t, 1)], scale=rstd[:, ds(t, 1)]).then_inc(h_ready, 1)
                    act.wait_ge(h_ready, t + 1)
                    act.activation(sq[:, b, 0, :], h[:, b, :], ACT.Square).then_inc(hsq_made, 1)

                def high(t, b):
                    act.wait_ge(tp_ready, done(t))
                    act.wait_ge(prod_done, free(t))
                    act.activation(hT_hi[:, b], tp[:, b], ACT.Copy).then_inc(hi_ready, 1)

                def finish(t, b):
                    act.wait_ge(prod_done, done(t))
                    act.activation(flat(x_all[:, ds(t, 1), :]), main[:, b, :], ACT.Copy, scale=1 / WS).then_inc(m_made, 1)
                    act.wait_ge(ssq_done, free(t))
                    act.activation(sq[:, b, 1, :], main[:, b, :], ACT.Square, scale=1 / WS).then_inc(msq_made, 1)

                act.sem_inc(tp_ready, 2)
                loop_with_two_next(act, finish, high, normalise)
                answers(act, asked, answered, [(v[:, 0:2, :], ACT.Sqrt, ssq[:], 1.0), (ln, ACT.Ln, ln, 1.0),
                                               (ee, ACT.Exp, tt, -2.0)])
                for c, (t0, n) in enumerate(CHUNKS):
                    act.wait_ge(xs_made, c + 1)
                    act.activation(xs_hi[:, t0:t0 + n, :], x_all[:, t0:t0 + n, :], ACT.Copy).then_inc(hi_made, 1)
                    act.wait_ge(diff_made, c + 1)
                    act.activation(xs_lo[:, t0:t0 + n, :], x_all[:, t0:t0 + n, :], ACT.Copy, scale=LS).then_inc(used, 1)
                act.wait_ge(g_made, 1)
                act.activation(gcol[:, :, 1], ga, ACT.Copy, scale=LS).then_inc(used, 1)

            @block.tensor
            def _(pe):
                pe.wait_ge(s["w_lo"], 1)

                def transpose(t, b):
                    pe.wait_ge(h_ready, t + 1)
                    pe.wait_ge(lo_done, free(t))
                    for k in range(KC):
                        last = pe.transpose(tp[:, b, k, :], h[:, b, k * P:(k + 1) * P], keep["ident"][:])
                    last.then_inc(tp_ready, 1)

                def products(t, b):
                    pe.wait_ge(lo_done, done(t))
                    pe.wait_ge(msq_made, free(t))
                    split_product(pe, main[:, b, :], hT_hi[:, b], hT_lo[:, b], w_hi, w_lo, slice(0, D)).then_inc(prod_done, 1)

                loop_with_next(pe, products, transpose)

            @block.vector
            def _(dve):
                dve.wait_ge(w_in, 16)
                split_weights(dve, w, w_hi, w_lo, s)

                def residual(c):
                    t0, n = CHUNKS[c]
                    yc, xc = y[:, c % 2, 0:n, :], x_all[:, t0:t0 + n, :]
                    dve.wait_ge(y_made, c + 1)
                    dve.tensor_scalar(low[:, 0:n, :], yc, 0.0, None, ALU.min).then_inc(low_made, 1)
                    dve.wait_ge(low_made, c + 1)
                    dve.tensor_scalar(yc, yc, 0.0, -1.0, ALU.max, ALU.add).then_inc(plus_made, 1)
                    dve.wait_ge(plus_made, c + 1)
                    dve.wait_ge(x_in[c], 16)
                    dve.tensor_tensor(xc, xc, yc, ALU.add).then_inc(sum_made, 1)
                    dve.wait_ge(sum_made, c + 1)
                    dve.wait_ge(el_made, c + 1)
                    dve.tensor_tensor(xc, xc, el[:, 0:n, :], ALU.add).then_inc(x_made, 1)
                    dve.wait_ge(x_made, c + 1)

                norm_statistics(dve, x_all, stats, mv, std, rstd, nmr, residual, s)

                def split(t, b):
                    dve.wait_ge(hi_ready, t + 1)
                    dve.tensor_tensor(hT_lo[:, b], tp[:, b], hT_hi[:, b], ALU.subtract).then_inc(lo_done, 1)
                    dve.wait_ge(hsq_made, t + 1)
                    dve.tensor_reduce(ssq[:, 0, ds(t, 1)], sq[:, b, 0, :], AXX, ALU.add).then_inc(hss_done, 1)

                def finish(t, b):
                    dve.wait_ge(msq_made, done(t))
                    dve.tensor_reduce(ssq[:, 1, ds(t, 1)], sq[:, b, 1, :], AXX, ALU.add).then_inc(ssq_done, 1)

                loop_with_next(dve, finish, split)
                dve.wait_ge(ssq_done, done(T - 1))
                dve.wait_ge(hss_done, done(T - 1))
                ch = Chain(dve, link, asked, answered)
                ch.scale(ssq[:], ssq[:], 1e-20, ALU.max)
                ch.ask()
                ch.invert(co, mn)
                ch.invert(ga, hn)
                ch.pair(ga, ga, mn)
                ch.scale(th, mn, 1e-10, ALU.is_gt)
                ch.pair(co, co, th)
                ch.atanh(tt, hn, t1, t2, ln)
                ch.pair(tt, tt, ga)
                ch.tanh(th, tt, t1, t2, ee)
                ch.pair(co, co, th)
                ch.scale(ee, ee, EMIN, ALU.max)
                ch.scale(t1, ee, 2.0)
                ch.invert(t1, t1)
                ch.fused(t2, ee, 1.0, t1, ALU.add, ALU.mult)
                ch.fused(ga, ee, 1.0, t2, ALU.add, ALU.mult)
                ch.pair(t2, ga, co)
                ch.scale(co, t2, XS)
                ch.scale(ga, ga, -1.0, ALU.add, XS, ALU.mult)
                for c, (t0, n) in enumerate(CHUNKS):
                    dve.tensor_tensor(x_all[:, t0:t0 + n, :], x_all[:, t0:t0 + n, :],
                                      co[:, t0:t0 + n].unsqueeze(2).broadcast_to([P, n, D]), ALU.mult).then_inc(xs_made, 1)
                ch.then(dve.tensor_copy(gcol[:, :, 0], ga))
                ch.pair(ga, ga, gcol[:, :, 0], ALU.subtract)
                dve.sem_inc(g_made, 1)
                dve.memset(gcol[:, :, 2], 1.0).then_inc(used, 1)
                for c, (t0, n) in enumerate(CHUNKS):
                    dve.wait_ge(hi_made, c + 1)
                    dve.tensor_tensor(x_all[:, t0:t0 + n, :], x_all[:, t0:t0 + n, :], xs_hi[:, t0:t0 + n, :],
                                      ALU.subtract).then_inc(diff_made, 1)

        kit.close()


def midpoint2(nc, dram, keep):
    with ExitStack() as stack:
        kit = Kit(nc, stack, "m2")
        HJ = T // 2
        at = kit.sb("at", [2, HJ, BW], F16)
        lowp, nom, rel = kit.sb("lowp", [2, D]), kit.sb("nom", [2, D]), kit.sb("rel", [2, D])
        sq = kit.sb("sq", [2, 2, D])
        ss, sm, v = kit.sb("ss", [2, T]), kit.sb("sm", [3, T]), kit.sb("v", [10, T])
        hi = kit.ps("hi", [2, D])
        lo = kit.ps("lo", [2, D])
        small = kit.ps("small", [2, 512])
        xs_hi, xs_lo, gcol, factor = keep["xs_hi"], keep["xs_lo"], keep["gcol"], keep["factor"]
        at_in, r_out = kit.sems("at_in0 at_in1"), kit.sems("r_out0 r_out1")
        (prod_done, half_used, low_made, nom_made, sm_made, acc_free, nsq_made, rel_made, rsq_made, ss_done, link, asked,
         answered, gate) = kit.sems(
            "prod_done half_used low_made nom_made sm_made acc_free nsq_made rel_made rsq_made ss_done link asked "
            "answered gate")
        den, nn, rr, t1, t2, ln, ee, un, xn, th = (v[:, i, :] for i in range(10))

        def loop_blocks(eng, step):
            with eng.Fori(0, IB) as ib:
                for q in range(2):
                    step(ib, q)

        with nc.Block() as block:
            @block.sync
            def _(sp):
                for ring in (acc_free, nom_made, rsq_made, ss_done):
                    sp.sem_inc(ring, 2)
                for out in r_out:
                    sp.sem_inc(out, 16)
                for half in range(2):
                    sp.sem_inc(half_used, 1)

                def load(ib, half):
                    wait_count(sp, half_used, 2 * ib + half + 1, gate)
                    sp.dma_start(at[:, half], dram["at16"][ds(ib, 1), :, half * HJ:(half + 1) * HJ, :].rearrange(
                        "o p t c -> p (o t) c")).then_inc(at_in[half], 16)

                def store(ib):
                    for q in range(2):
                        wait_count(sp, rel_made, 2 * ib + q + 1, gate)
                        sp.dma_start(dram["part2"].rearrange("(t p) d -> t p d", p=P)[ds(2 * ib + q, 1)].rearrange(
                            "o p d -> p (o d)"), rel[:, q, :]).then_inc(r_out[q], 16)

                load(0, 0)
                load(0, 1)
                with sp.Fori(1, IB) as ib:
                    load(ib, 0)
                    load(ib, 1)
                    store(ib - 1)
                store(IB - 1)
                for out in r_out:
                    sp.wait_ge(out, 16 * (IB + 1))

            @block.tensor
            def _(pe):
                def tile(ib, q):
                    pe.wait_ge(acc_free, free(2 * ib + q))
                    for j in range(T):
                        if q == 0 and j % HJ == 0:
                            pe.wait_ge(at_in[j // HJ], ib * 16 + 16)
                        a = at[:, j // HJ, j % HJ, q * P:(q + 1) * P]
                        ends = dict(start=(j == 0), stop=(j == T - 1))
                        pe.matmul(hi[:, q, :], a, xs_hi[:, j, :], **ends)
                        pe.matmul(lo[:, q, :], a, xs_lo[:, j, :], **ends)
                        last = pe.matmul(small[:, q, 0:3], a, gcol[:, j, :], **ends)
                        if j == HJ - 1 and q == 1:
                            last.then_inc(half_used, 1)
                        if j == T - 1:
                            last.then_inc(prod_done, 1)
                            if q == 1:
                                pe.wait_ge(prod_done, 2 * ib + 2)
                                pe.sem_inc(half_used, 1)

                loop_blocks(pe, tile)

            @block.scalar
            def _(act):
                def tile(ib, q):
                    t = 2 * ib + q
                    act.wait_ge(prod_done, t + 1)
                    act.wait_ge(nom_made, free(t))
                    act.activation(lowp[:, q, :], lo[:, q, :], ACT.Copy, scale=1 / LS).then_inc(low_made, 1)
                    act.wait_ge(nom_made, done(t))
                    act.wait_ge(ss_done, free(t))
                    act.activation(sq[:, q, 0, :], nom[:, q, :], ACT.Square).then_inc(nsq_made, 1)
                    act.wait_ge(rel_made, t + 1)
                    act.activation(sq[:, q, 1, :], rel[:, q, :], ACT.Square).then_inc(rsq_made, 1)

                loop_blocks(act, tile)
                answers(act, asked, answered, [(v[:, 1:3, :], ACT.Sqrt, ss[:], 1.0), (t1, ACT.Sqrt, t1, 1.0),
                                               (ln, ACT.Ln, ln, 1.0), (ee, ACT.Exp, un, -2.0)])

            @block.vector
            def _(dve):
                def tile(ib, q):
                    t = 2 * ib + q
                    dve.wait_ge(prod_done, t + 1)
                    dve.tensor_copy(sm[:, :, ds(t, 1)], small[:, q, 0:3].unsqueeze(2)).then_inc(sm_made, 1)
                    dve.wait_ge(low_made, t + 1)
                    dve.wait_ge(rsq_made, free(t))
                    dve.tensor_tensor(nom[:, q, :], hi[:, q, :], lowp[:, q, :], ALU.add).then_inc(nom_made, 1)
                    dve.wait_ge(nom_made, done(t))
                    dve.wait_ge(sm_made, t + 1)
                    dve.sem_inc(acc_free, 1)
                    dve.wait_ge(r_out[q], ib * 16 + 16)
                    dve.tensor_scalar(rel[:, q, :], nom[:, q, :], 0.0, None, ALU.max).then_inc(rel_made, 1)
                    dve.wait_ge(nsq_made, t + 1)
                    dve.wait_ge(rsq_made, done(t))
                    dve.tensor_reduce(ss[:, :, ds(t, 1)], sq[:, q], AXX, ALU.add).then_inc(ss_done, 1)

                loop_blocks(dve, tile)
                dve.wait_ge(ss_done, done(T - 1))
                dve.wait_ge(sm_made, T)
                ch = Chain(dve, link, asked, answered)
                alpha = sm[:, 2, :]
                ch.fused(den, sm[:, 1, :], 1 / LS, sm[:, 0, :], ALU.mult, ALU.add)
                ch.scale(den, den, 1e-10 * XS, ALU.max)
                ch.invert(den, den)
                ch.ask()
                ch.pair(xn, nn, den)
                ch.pair(t2, xn, xn)
                ch.scale(t1, t2, -1.0, ALU.mult, 1.0, ALU.add)
                ch.scale(t1, t1, 1e-10, ALU.max)
                ch.ask()
                ch.scale(t1, t1, 1.0, ALU.add)
                ch.invert(t1, t1)
                ch.pair(xn, xn, t1)
                ch.scale(xn, xn, 1e-10, ALU.max)
                ch.atanh(un, xn, t1, t2, ln)
                ch.pair(un, un, alpha)
                ch.scale(un, un, ATMAX, ALU.min)
                ch.scale(nn, nn, 1e-30, ALU.max)
                ch.invert(nn, nn)
                ch.pair(un, un, nn)
                ch.pair(un, un, rr)
                ch.tanh(th, un, t1, t2, ee)
                ch.scale(rr, rr, 1e-30, ALU.max)
                ch.invert(rr, rr)
                ch.pair(factor[:], th, rr)

        kit.close()

def prep3(nc, dram, keep):
    with ExitStack() as stack:
        kit = Kit(nc, stack, "p3")
        x_all, h = kit.sb("x_all", [T, D]), kit.sb("h", [2, D])
        hT_hi, hT_lo = kit.sb("hT_hi", [2, KC, P], F16), kit.sb("hT_lo", [2, KC, P], F16)
        NX = 2 * D + 1
        w = kit.sb("w", [KC, NX])
        w_hi, w_lo = kit.sb("w_hi", [KC, NX], F16), kit.sb("w_lo", [KC, NX], F16)
        r = kit.sb("r", [6, D])
        stats, mv = kit.sb("stats", [T, 6]), kit.sb("mv", [T, 2])
        std, rstd, nmr = kit.sb("std", [T]), kit.sb("rstd", [T]), kit.sb("nmr", [T])
        valid, nl, ne = kit.sb("valid", [T]), kit.sb("nl", [T]), kit.sb("ne", [T])
        one = kit.sb("one", [4, 1])
        tp = kit.ps("tp", [2, KC, P])
        main = kit.ps("main", [2, D])
        edge = kit.ps("edge", [2, KC, P])
        small = kit.ps("small", [2, 256])
        s_hi, s_lo, e_hi, e_lo, node = (keep[n] for n in ("s_hi", "s_lo", "e_hi", "e_lo", "node"))
        x_in = kit.sems(" ".join(f"x_in{c}" for c in range(len(CHUNKS))))
        s = dict(zip("stats mv var std rstd nmr w_hi w_lo".split(),
                     kit.sems("stats mv var std rstd nmr w_hi w_lo")))
        (w_in, r_in, v_in, x_made, x_out, h_ready, tp_ready, hi_ready, lo_done, prod_done, s_hi_made, s_lo_done,
         e_hi_made, e_lo_done, nl_done, link, asked, answered, m_made, m_all, z_all) = kit.sems(
            "w_in r_in v_in x_made x_out h_ready tp_ready hi_ready lo_done prod_done s_hi_made s_lo_done "
            "e_hi_made e_lo_done nl_done link asked answered m_made m_all z_all")
        x_t, r_t = tiles(dram["x2"]), tiles(dram["part2"])
        gm, gmall, gz, gzall = (one[:, i, :] for i in range(4))

        with nc.Block() as block:
            @block.sync
            def _(sp):
                for ring in (lo_done, prod_done, s_lo_done, e_lo_done, nl_done):
                    sp.sem_inc(ring, 2)
                for c, (t0, n) in enumerate(CHUNKS):
                    sp.dma_start(x_all[:, t0:t0 + n, :], x_t[:, t0:t0 + n, :]).then_inc(x_in[c], 16)
                    if c >= 1:
                        sp.wait_ge(x_made, c)
                    sp.dma_start(r[:, 0:n, :], r_t[:, t0:t0 + n, :]).then_inc(r_in, 16)
                    if c == 0:
                        sp.dma_start(w[:], dram["w3"].rearrange("(k p) n -> p k n", p=P)).then_inc(w_in, 16)
                        sp.dma_start(valid[:], dram["valid"]).then_inc(v_in, 16)
                for c, (t0, n) in enumerate(CHUNKS):
                    sp.wait_ge(x_made, c + 1)
                    sp.dma_start(tiles(dram["x3"])[:, t0:t0 + n, :], x_all[:, t0:t0 + n, :]).then_inc(x_out, 16)
                sp.wait_ge(x_out, 16 * len(CHUNKS))

            @block.gpsimd
            def _(pool):
                pool.wait_ge(m_made, 1)
                pool.partition_all_reduce(gmall, gm, P, RMAX).then_inc(m_all, 1)
                pool.wait_ge(answered, 1)
                pool.partition_all_reduce(gzall, gz, P, RADD).then_inc(z_all, 1)

            @block.scalar
            def _(act):
                act.wait_ge(s["var"], 1)
                act.activation(std[:], std[:], ACT.Sqrt).then_inc(s["std"], 1)
                act.wait_ge(s["nmr"], 1)

                def normalise(t, b):
                    act.wait_ge(tp_ready, free(t))
                    act.activation(h[:, b, :], flat(x_all[:, ds(t, 1), :]), ACT.Relu,
                                   bias=nmr[:, ds(t, 1)], scale=rstd[:, ds(t, 1)]).then_inc(h_ready, 1)

                def high(t, b):
                    act.wait_ge(tp_ready, done(t))
                    act.wait_ge(prod_done, free(t))
                    act.activation(hT_hi[:, b], tp[:, b], ACT.Copy).then_inc(hi_ready, 1)

                def finish(t, b):
                    act.wait_ge(prod_done, done(t))
                    act.activation(flat(s_hi[:, ds(t, 1), :]), main[:, b, :], ACT.Copy, scale=1 / WS).then_inc(s_hi_made, 1)
                    act.activation(e_hi[:, :, ds(t * P, P)], edge[:, b], ACT.Copy, scale=1 / WS).then_inc(e_hi_made, 1)

                act.sem_inc(tp_ready, 2)
                loop_with_two_next(act, finish, high, normalise)
                act.wait_ge(asked, 1)
                act.activation(ne[:], nl[:], ACT.Exp, accum_out=gz).then_inc(answered, 1)

            @block.tensor
            def _(pe):
                pe.wait_ge(s["w_lo"], 1)

                def transpose(t, b):
                    pe.wait_ge(h_ready, t + 1)
                    pe.wait_ge(lo_done, free(t))
                    for k in range(KC):
                        last = pe.transpose(tp[:, b, k, :], h[:, b, k * P:(k + 1) * P], keep["ident"][:])
                    last.then_inc(tp_ready, 1)

                def products(t, b):
                    pe.wait_ge(lo_done, done(t))
                    pe.wait_ge(s_lo_done, free(t))
                    split_product(pe, main[:, b, :], hT_hi[:, b], hT_lo[:, b], w_hi, w_lo, slice(0, D))
                    pe.wait_ge(e_lo_done, free(t))
                    for m in range(KC):
                        of = slice(D + m * P, D + (m + 1) * P)
                        for k in range(KC):
                            for n, (a, b_) in enumerate(((w_hi, hT_hi), (w_lo, hT_hi), (w_hi, hT_lo))):
                                pe.matmul(edge[:, b, m, :], a[:, k, of], b_[:, b, k, :], start=(m == 0 and k == 0 and n == 0),
                                          stop=(k == KC - 1 and n == 2), skip_group_check=True)
                    pe.wait_ge(nl_done, done(t - 1))
                    split_product(pe, small[:, b, 0:1], hT_hi[:, b], hT_lo[:, b], w_hi, w_lo, slice(2 * D, NX)).then_inc(prod_done, 1)

                loop_with_next(pe, products, transpose)

            @block.vector
            def _(dve):
                dve.wait_ge(w_in, 16)
                split_weights(dve, w, w_hi, w_lo, s)

                def residual(c):
                    t0, n = CHUNKS[c]
                    dve.wait_ge(x_in[c], 16)
                    dve.wait_ge(r_in, 16 * (c + 1))
                    for t in range(n):
                        last = dve.scalar_tensor_tensor(x_all[:, t0 + t, :], r[:, t, :], keep["factor"][:, t0 + t:t0 + t + 1],
                                                        x_all[:, t0 + t, :], ALU.mult, ALU.add)
                    last.then_inc(x_made, 1)
                    dve.wait_ge(x_made, c + 1)

                norm_statistics(dve, x_all, stats, mv, std, rstd, nmr, residual, s)

                def split(t, b):
                    dve.wait_ge(hi_ready, t + 1)
                    dve.tensor_tensor(hT_lo[:, b], tp[:, b], hT_hi[:, b], ALU.subtract).then_inc(lo_done, 1)

                def finish(t, b):
                    dve.wait_ge(prod_done, done(t))
                    dve.tensor_scalar(nl[:, ds(t, 1)], small[:, b, 0:1], 1 / WS, None, ALU.mult).then_inc(nl_done, 1)
                    dve.wait_ge(s_hi_made, t + 1)
                    dve.scalar_tensor_tensor(flat(s_lo[:, ds(t, 1), :]), main[:, b, :], 1 / WS, flat(s_hi[:, ds(t, 1), :]),
                                             ALU.mult, ALU.subtract).then_inc(s_lo_done, 1)
                    dve.wait_ge(e_hi_made, t + 1)
                    dve.scalar_tensor_tensor(e_lo[:, :, ds(t * P, P)], edge[:, b], 1 / WS, e_hi[:, :, ds(t * P, P)],
                                             ALU.mult, ALU.subtract).then_inc(e_lo_done, 1)

                loop_with_next(dve, finish, split)
                dve.wait_ge(nl_done, done(T - 1))
                dve.wait_ge(v_in, 16)
                ch = Chain(dve, link, asked, answered)
                ch.scale(valid[:], valid[:], BIG, ALU.mult, -BIG, ALU.add)
                ch.pair(nl[:], nl[:], valid[:], ALU.add)
                dve.tensor_reduce(gm, nl[:], AXX, ALU.max).then_inc(m_made, 1)
                dve.wait_ge(m_all, 1)
                ch.scale(nl[:], nl[:], gmall, ALU.subtract)
                ch.ask()
                dve.wait_ge(z_all, 1)
                ch.invert(gzall, gzall)
                ch.scale(nl[:], keep["iso"][:], -1.0, ALU.mult, 1.0, ALU.add)
                ch.fused(node[:], ne[:], gzall, nl[:], ALU.mult, ALU.mult)

        kit.close()


def attention3(nc, dram, keep):
    with ExitStack() as stack:
        kit = Kit(nc, stack, "m3")
        EC = [(c * 512, min(512, NP - c * 512)) for c in range(-(-NP // 512))]
        GROUPS = [(g, min(8, T - g)) for g in range(0, T, 8)]
        a = kit.sb("a", [2, NP])
        am = kit.sb("am", [2, NP], BF16)
        em = kit.sb("em", [2, NP])
        w_hi, w_lo = kit.sb("w_hi", [NP], F16), kit.sb("w_lo", [NP], F16)
        wT_hi, wT_lo = kit.sb("wT_hi", [T, P], F16), kit.sb("wT_lo", [T, P], F16)
        mx, nm, rs, co = kit.sb("mx", [2, len(EC)]), kit.sb("nm", [2, 1]), kit.sb("rs", [2, 1]), kit.sb("co", [2, 1])
        x, o, bias = kit.sb("x", [2, D]), kit.sb("o", [2, D]), kit.sb("bias", [D])
        sc = kit.ps("sc", [4, 512])
        tw = kit.ps("tw", [2, 8, P], F16)
        acc = kit.ps("acc", [2, D])
        s_hi, s_lo, e_hi, e_lo, node = (keep[n] for n in ("s_hi", "s_lo", "e_hi", "e_lo", "node"))
        a_in, x_in, out_done = kit.sems("a_in0 a_in1"), kit.sems("x_in0 x_in1"), kit.sems("out_done0 out_done1")
        (bias_in, am_made, sc_made, sc_used, max_made, exp_made, hi_made, lo_made, t_hi, t_lo, wt_hi, wt_lo,
         acc_made, acc_used, o_made, out_made, link, gate) = kit.sems(
            "bias_in am_made sc_made sc_used max_made exp_made hi_made lo_made t_hi t_lo wt_hi wt_lo "
            "acc_made acc_used o_made out_made link gate")
        NE, NG = len(EC), len(GROUPS)
        AFTER = (0, 2, 4)
        bank = lambda b, c: (NE * b + c) % 4

        with nc.Block() as block:
            @block.sync
            def _(sp):
                for ring in (am_made, max_made, acc_used, out_made, lo_made):
                    sp.sem_inc(ring, 2)
                sp.sem_inc(sc_used, 4)
                for done_ in out_done:
                    sp.sem_inc(done_, 16)
                sp.dma_start(bias[:], dram["bias3"].broadcast_to([P, D])).then_inc(bias_in, 16)

                def load_mask(t, b):
                    wait_count(sp, am_made, free(t), gate)
                    sp.dma_start(a[:, b, :], dram["adj"].rearrange("(t p) n -> t p n", p=P)[ds(t, 1)].rearrange(
                        "o p n -> p (o n)")).then_inc(a_in[b], 16)

                def load_x(t, b):
                    wait_count(sp, out_done[b], (t - b) * 8 + 16, gate)
                    sp.dma_start(x[:, b, :], dram["x3"].rearrange("(t p) d -> t p d", p=P)[ds(t, 1)].rearrange(
                        "o p d -> p (o d)")).then_inc(x_in[b], 16)

                def store(t, b):
                    wait_count(sp, out_made, done(t), gate)
                    rows = LAST if isinstance(t, int) and t == T - 1 else P
                    sp.dma_start(dram["out"][ds(t * P, rows), :], x[0:rows, b, :]).then_inc(out_done[b], 16)

                for t in range(2):
                    load_mask(t, t)
                    load_x(t, t)
                load_mask(2, 0)
                with sp.Fori(3, T - 1, 2) as t:
                    for b in range(2):
                        load_mask(t + b, 1 - b)
                        store(t + b - 3, b)
                        load_x(t + b - 1, b)
                load_mask(T - 1, 1)
                store(T - 4, 0)
                load_x(T - 2, 0)
                store(T - 3, 1)
                load_x(T - 1, 1)
                store(T - 2, 0)
                store(T - 1, 1)
                for done_ in out_done:
                    sp.wait_ge(done_, 16 * (T // 2 + 1))

            @block.tensor
            def _(pe):
                def chunk(t, b, c):
                    n0, n = EC[c]
                    pe.wait_ge(sc_used, t * NE + c + 1)
                    for k in range(KC):
                        for i, (l, r) in enumerate(((e_hi, e_hi), (e_hi, e_lo), (e_lo, e_hi))):
                            last = pe.matmul(sc[:, bank(b, c), 0:n], l[:, k, ds(t * P, P)], r[:, k, n0:n0 + n],
                                             start=(k == 0 and i == 0), stop=(k == KC - 1 and i == 2))
                    last.then_inc(sc_made, 1)

                def transposes(t, g):
                    j0, nj = GROUPS[g]
                    if g == 0:
                        pe.wait_ge(lo_made, done(t))
                    for part, half, made, moved in ((w_hi, 0, t_hi, wt_hi), (w_lo, 1, t_lo, wt_lo)):
                        if not (isinstance(t, int) and t == 0 and g == 0):
                            pe.wait_ge(moved, t * NG + g)
                        for j in range(nj):
                            last = pe.transpose(tw[:, half, j, :], part[:, (j0 + j) * P:(j0 + j + 1) * P], keep["ident16"][:])
                        last.then_inc(made, 1)

                def products(t, b):
                    pe.wait_ge(acc_used, free(t))
                    for g, (j0, nj) in enumerate(GROUPS):
                        pe.wait_ge(wt_hi, t * NG + g + 1)
                        pe.wait_ge(wt_lo, t * NG + g + 1)
                        for j in range(j0, j0 + nj):
                            pe.matmul(acc[:, b, :], wT_hi[:, j, :], s_hi[:, j, :], start=(j == 0), stop=False)
                            pe.matmul(acc[:, b, :], wT_hi[:, j, :], s_lo[:, j, :], start=False, stop=False)
                            last = pe.matmul(acc[:, b, :], wT_lo[:, j, :], s_hi[:, j, :], start=False, stop=(j == T - 1))
                    last.then_inc(acc_made, 1)

                def step(t, b):
                    for c in range(NE):
                        chunk(t + 1, 1 - b, c)
                        if c in AFTER:
                            transposes(t, AFTER.index(c))
                    products(t, b)

                for c in range(NE):
                    chunk(0, 0, c)
                with pe.Fori(0, T - 2, 2) as t:
                    for b in range(2):
                        step(t + b, b)
                step(T - 2, 0)
                for g in range(NG):
                    transposes(T - 1, g)
                products(T - 1, 1)

            @block.vector
            def _(dve):
                dve.wait_ge(bias_in, 16)

                def chunk_max(t, b, c):
                    n0, n = EC[c]
                    if c == 0:
                        dve.wait_ge(am_made, done(t))
                        dve.wait_ge(lo_made, free(t))
                    wait_count(dve, sc_made, t * NE + c + 1, gate)
                    dve.tensor_tensor_reduce(em[:, b, n0:n0 + n], sc[:, bank(b, c), 0:n], am[:, b, n0:n0 + n], 1.0, -3e38,
                                             ALU.add, ALU.max, mx[:, b, c:c + 1]).then_inc(sc_used, 1)

                def row_max(t, b):
                    dve.wait_ge(sc_used, (t + 1) * NE + 4)
                    dve.tensor_reduce(nm[:, b, :], mx[:, b, :], AXX, ALU.max, negate=True).then_inc(max_made, 1)

                def low(t, b):
                    dve.wait_ge(hi_made, t + 1)
                    dve.tensor_tensor(w_lo[:], em[:, b, :], w_hi[:], ALU.subtract).then_inc(lo_made, 1)

                def move(t, g):
                    j0, nj = GROUPS[g]
                    dve.wait_ge(t_lo, t * NG + g + 1)
                    if g == 0 and not (isinstance(t, int) and t == 0):
                        dve.wait_ge(acc_made, t)
                    dve.tensor_copy(wT_lo[:, j0:j0 + nj, :], tw[:, 1, 0:nj, :]).then_inc(wt_lo, 1)

                def finish(t, b):
                    dve.wait_ge(exp_made, t + 1)
                    dve.reciprocal(co[:, b, :], rs[:, b, :]).then_inc(link, 1)
                    dve.wait_ge(link, 2 * t + 1)
                    dve.tensor_tensor(co[:, b, :], co[:, b, :], node[:, ds(t, 1)], ALU.mult).then_inc(link, 1)
                    dve.wait_ge(link, 2 * t + 2)
                    dve.wait_ge(acc_made, t + 1)
                    dve.wait_ge(out_made, free(t))
                    dve.scalar_tensor_tensor(o[:, b, :], acc[:, b, :], co[:, b, :], bias[:], ALU.mult, ALU.add).then_inc(acc_used, 1)

                def step(t, b, first=False):
                    low(t, b)
                    for c in range(NE):
                        chunk_max(t + 1, 1 - b, c)
                        if c in AFTER:
                            move(t, AFTER.index(c))
                        if c == 1 and not first:
                            finish(t - 1, 1 - b)
                    row_max(t + 1, 1 - b)

                for c in range(NE):
                    chunk_max(0, 0, c)
                row_max(0, 0)
                step(0, 0, True)
                with dve.Fori(1, T - 2, 2) as t:
                    for b in range(2):
                        step(t + b, 1 - b)
                low(T - 1, 1)
                finish(T - 2, 0)
                for g in range(NG):
                    move(T - 1, g)
                finish(T - 1, 1)

            @block.scalar
            def _(act):
                def mask(t, b):
                    act.wait_ge(a_in[b], (t - b) * 8 + 16)
                    act.wait_ge(max_made, free(t))
                    act.activation(am[:, b, :], a[:, b, :], ACT.Copy, scale=BIG, bias=-BIG).then_inc(am_made, 1)

                def softmax(t, b):
                    act.wait_ge(max_made, done(t))
                    act.activation(em[:, b, :], em[:, b, :], ACT.Exp, bias=nm[:, b, :], accum_out=rs[:, b, :]).then_inc(exp_made, 1)
                    act.wait_ge(exp_made, t + 1)
                    if not (isinstance(t, int) and t == 0):
                        act.wait_ge(t_hi, t * NG)
                        act.wait_ge(t_lo, t * NG)
                    act.activation(w_hi[:], em[:, b, :], ACT.Copy).then_inc(hi_made, 1)

                def move(t, b):
                    for g, (j0, nj) in enumerate(GROUPS):
                        act.wait_ge(t_hi, t * NG + g + 1)
                        if g == 0 and not (isinstance(t, int) and t == 0):
                            act.wait_ge(acc_made, t)
                        act.activation(wT_hi[:, j0:j0 + nj, :], tw[:, 0, 0:nj, :], ACT.Copy).then_inc(wt_hi, 1)

                mask(0, 0)
                mask(1, 1)
                with act.Fori(0, T - 3, 2) as t:
                    for b in range(2):
                        softmax(t + b, b)
                        mask(t + b + 2, b)
                        move(t + b, b)
                for t in (T - 2, T - 1):
                    softmax(t, t % 2)
                    move(t, t % 2)

            @block.gpsimd
            def _(pool):
                def add(t, b):
                    pool.wait_ge(x_in[b], (t - b) * 8 + 16)
                    pool.wait_ge(acc_used, done(t))
                    pool.tensor_tensor(x[:, b, :], x[:, b, :], o[:, b, :], ALU.add).then_inc(out_made, 1)

                loop_tiles(pool, add)

        kit.close()

def build(nc, dram):
    with ExitStack() as stack:
        kit = Kit(nc, stack, "keep")
        keep = {"ident": kit.sb("ident", [P]), "ident16": kit.sb("ident16", [P], F16),
                "ones16": kit.sb("ones16", [P], F16), "iso": kit.sb("iso", [T]), "factor": kit.sb("factor", [T])}
        setup(nc, dram, keep)
        with ExitStack() as layer:
            kit = Kit(nc, layer, "keep0")
            keep |= {"z_hi": kit.sb("z_hi", [T, 2 * D], F16), "z_lo": kit.sb("z_lo", [T, 2 * D], F16),
                     "uv": kit.sb("uv", [2, T]), "cs0": kit.sb("cs0", [2 * D]),
                     "v08": kit.sb("v08", [T]), "v02": kit.sb("v02", [T])}
            prep0(nc, dram, keep)
            extremes0(nc, dram, keep)
            attention0(nc, dram, keep)
        with ExitStack() as layer:
            kit = Kit(nc, layer, "keep1")
            keep |= {n: kit.sb(n, [H, T]) for n in ("r1", "f1", "f2", "d1", "d2", "nv")}
            prep1(nc, dram, keep)
            attention1(nc, dram, keep)
        with ExitStack() as layer:
            kit = Kit(nc, layer, "keep2")
            keep |= {"xs_hi": kit.sb("xs_hi", [T, D], F16), "xs_lo": kit.sb("xs_lo", [T, D], F16), "gcol": kit.sb("gcol", [T, 3], F16)}
            prep2(nc, dram, keep)
            midpoint2(nc, dram, keep)
        with ExitStack() as layer:
            kit = Kit(nc, layer, "keep3")
            keep |= {n: kit.sb(n, [T, D], F16) for n in ("s_hi", "s_lo")}
            keep |= {n: kit.sb(n, [KC, NP], F16) for n in ("e_hi", "e_lo")}
            keep["node"] = kit.sb("node", [T])
            prep3(nc, dram, keep)
            attention3(nc, dram, keep)


def layouts(inputs):
    import numpy as np

    x, adj = np.asarray(inputs["x"]), np.asarray(inputs["adj"])
    f32 = x.dtype
    x0 = np.zeros((NP, D), f32)
    x0[:N] = x
    rows = np.zeros((NP, NP), f32)
    rows[:N, :N] = adj
    adjT = np.ascontiguousarray(rows.reshape(IB, BW, T, P).transpose(0, 3, 2, 1))
    get = lambda name: np.ascontiguousarray(np.asarray(inputs[name]))
    valid = np.zeros((NP,), f32)
    valid[:N] = 1
    return {
        "x0": x0, "adj": rows, "adjT": adjT, "ident": np.eye(P, dtype=f32),
        "valid": np.ascontiguousarray(valid.reshape(T, P).T),
        "w0t": np.ascontiguousarray(get("L0_gnn_W").T),
        "a0": np.ascontiguousarray(get("L0_gnn_a").reshape(2, KC, P).transpose(2, 1, 0)),
        "wtr0": get("L0_gnn_wtrans"), "w1": get("L1_gnn_W"),
        "a1": np.ascontiguousarray(get("L1_gnn_a1").T).reshape(1, -1),
        "a2": np.ascontiguousarray(get("L1_gnn_a2").T).reshape(1, -1),
        "aln": get("L1_gnn_a_ln").reshape(1, -1), "bln": get("L1_gnn_b_ln").reshape(1, -1),
        "w2": get("L2_gnn_W"), "w3": np.concatenate([get("L3_gnn_weight"), get("L3_gnn_edge_w"), get("L3_gnn_node_w")], axis=1),
        "bias3": get("L3_gnn_bias").reshape(1, -1),
    }


SCRATCH = {"rows": (4 * T, P), "rows1": (H * T, P), "at16": (IB, P, T, BW), "x1": (NP, D), "x2": (NP, D), "x3": (NP, D),
           "c1": (NP, D), "y1": (NP, D), "part2": (NP, D)}


def kernel(**inputs):
    import concourse.bacc as bacc
    from concourse.bass_utils import run_bass_kernel_spmd

    nc = bacc.Bacc("TRN2", target_bir_lowering=False, num_devices=1)
    arrays = layouts(inputs)
    dram = {name: nc.dram_tensor(name, a.shape, F32, kind="ExternalInput").ap() for name, a in arrays.items()}
    for name, shape in SCRATCH.items():
        dram[name] = nc.dram_tensor(name, shape, F16 if name == "at16" else F32).ap()
    dram["out"] = nc.dram_tensor("out", (N, D), F32, kind="ExternalOutput").ap()
    build(nc, dram)
    result = run_bass_kernel_spmd(nc, [arrays], core_ids=[0])
    return result.results[0]["out"]
```

```python
from contextlib import ExitStack

import concourse.bass as bass
from concourse import mybir

F32 = mybir.dt.float32
F16 = mybir.dt.float16
BF16 = mybir.dt.bfloat16
ALU = mybir.AluOpType
ACT = mybir.ActivationFunctionType
AXX = mybir.AxisListType.X
RMAX = bass.bass_isa.ReduceOp.max
RADD = bass.bass_isa.ReduceOp.add

P = 128
N = 2708
T = -(-N // P)
NP = T * P
LAST = N - (T - 1) * P
D = 512
KC = D // P
H = 8
DH = D // H
IB = T // 2
BW = 2 * P
BIG = 1e30
CLAMP = 1e28
WS = 64.0
XMAX = 1.0 - 2.0 ** -23
ATMAX = 8.317766
CHUNKS = [(0, 2), (2, 4), (6, 6), (12, 6), (18, 4)]


def free(t):
    return t + 1


def done(t):
    return t + 3


def ds(start, size):
    return bass.ds(start, size)


def wait_count(eng, sem, count, gate):
    eng.wait_ge(sem, count)
    eng.sem_inc(gate, 1)


class Kit:

    def __init__(self, nc, stack, prefix):
        self.nc, self.stack, self.prefix, self.semaphores = nc, stack, prefix, []

    def sb(self, name, shape, dt=F32):
        return self.stack.enter_context(self.nc.sbuf_tensor(f"{self.prefix}_{name}", [P] + list(shape), dt))

    def ps(self, name, shape, dt=F32):
        return self.stack.enter_context(self.nc.psum_tensor(f"{self.prefix}_{name}", [P] + list(shape), dt))

    def sems(self, names):
        made = [self.nc.alloc_semaphore(f"{self.prefix}_{n}") for n in names.split()]
        self.semaphores += made
        return made

    def close(self):
        self.nc.clear_and_free_semaphores(self.semaphores)
        self.nc.all_engine_barrier()


def flat(ap):
    return ap.rearrange("p o d -> p (o d)")


def tiles(ap):
    return ap.rearrange("(t p) d -> p t d", p=P)


def moments(dve, t, b, x_all, stats, mv, std, s, gate):
    if not isinstance(t, int) or t >= 2:
        wait_count(dve, s["nmr"], t - 1, gate)
    dve.bn_stats(stats[:, b, :], flat(x_all[:, ds(t, 1), :])).then_inc(s["stats"], 1)
    wait_count(dve, s["stats"], t + 1, gate)
    dve.bn_aggr(mv[:, b, :], stats[:, b, :]).then_inc(s["mv"], 1)
    wait_count(dve, s["mv"], t + 1, gate)
    dve.tensor_scalar(std[:, b:b + 1], mv[:, b, 1:2], 1e-5, None, ALU.add).then_inc(s["var"], 1)


def root(act, t, b, std, s):
    act.wait_ge(s["var"], t + 1)
    act.activation(std[:, b:b + 1], std[:, b:b + 1], ACT.Sqrt).then_inc(s["std"], 1)


def shift(dve, t, b, mv, std, rstd, nmr, h_ready, s, gate):
    if not isinstance(t, int) or t >= 2:
        wait_count(dve, h_ready, t - 1, gate)
    wait_count(dve, s["std"], t + 1, gate)
    dve.reciprocal(rstd[:, b:b + 1], std[:, b:b + 1]).then_inc(s["rstd"], 1)
    wait_count(dve, s["rstd"], t + 1, gate)
    dve.scalar_tensor_tensor(nmr[:, b:b + 1], mv[:, b, 0:1], -1.0, rstd[:, b:b + 1], ALU.mult, ALU.mult).then_inc(s["nmr"], 1)


def pipeline(eng, *stages, before=()):
    far = max(lead for lead, _ in stages)
    end = (T - far) // 2 * 2
    actions = {t: [act for at, act in before if at == t] for t, _ in before}

    def step(t):
        for lead, stage in stages:
            if 0 <= t + lead < T:
                stage(t + lead, (t + lead) % 2)

    for t in range(min(-far, *actions), 0) if actions else range(-far, 0):
        for action in actions.get(t, ()):
            action()
        step(t)
    cuts = sorted({0, end} | {t for t in actions if 0 <= t < end})
    for first, stop in zip(cuts, cuts[1:]):
        for action in actions.get(first, ()):
            action()
        with eng.Fori(first, stop - 1, 2) as t:
            for b in range(2):
                for lead, stage in stages:
                    stage(t + b + lead, (b + lead) % 2)
    for t in range(end, T):
        for action in actions.get(t, ()):
            action()
        step(t)


def split_weights(dve, w, w_hi, w_lo, s):
    dve.tensor_scalar(w_hi[:], w[:], WS, None, ALU.mult).then_inc(s["w_hi"], 1)
    dve.wait_ge(s["w_hi"], 1)
    dve.scalar_tensor_tensor(w_lo[:], w[:], WS, w_hi[:], ALU.mult, ALU.subtract).then_inc(s["w_lo"], 1)


def split_product(pe, out, a_hi, a_lo, b_hi, b_lo, columns):
    for k in range(KC):
        pe.matmul(out, a_hi[:, k, :], b_hi[:, k, columns], start=(k == 0), stop=False, skip_group_check=True)
        pe.matmul(out, a_hi[:, k, :], b_lo[:, k, columns], start=False, stop=False, skip_group_check=True)
        last = pe.matmul(out, a_lo[:, k, :], b_hi[:, k, columns], start=False, stop=(k == KC - 1), skip_group_check=True)
    return last


def loop_tiles(eng, step):
    with eng.Fori(0, T - 1, 2) as t:
        for b in range(2):
            step(t + b, b)


class Chain:

    def __init__(self, dve, link, asked, answered):
        self.dve, self.link, self.asked, self.answered = dve, link, asked, answered
        self.steps = self.questions = 0

    def then(self, instruction):
        self.steps += 1
        instruction.then_inc(self.link, 1)
        self.dve.wait_ge(self.link, self.steps)

    def ask(self):
        self.questions += 1
        self.dve.sem_inc(self.asked, 1)
        self.dve.wait_ge(self.answered, self.questions)

    def scale(self, out, a, s1, op0=ALU.mult, s2=None, op1=ALU.bypass):
        if s2 is None:
            self.then(self.dve.tensor_scalar(out, a, s1, None, op0))
        else:
            self.then(self.dve.tensor_scalar(out, a, s1, s2, op0, op1))

    def pair(self, out, a, b, op=ALU.mult):
        self.then(self.dve.tensor_tensor(out, a, b, op))

    def fused(self, out, a, s, b, op0, op1):
        self.then(self.dve.scalar_tensor_tensor(out, a, s, b, op0, op1))

    def invert(self, out, a):
        self.then(self.dve.reciprocal(out, a))

    def choose(self, out, small, is_small):
        self.pair(small, small, out, ALU.subtract)
        self.pair(small, small, is_small)
        self.pair(out, out, small, ALU.add)

    def atanh(self, out, x, t1, t2, ln):
        self.scale(x, x, XMAX, ALU.min)
        self.scale(t1, x, -1.0, ALU.mult, 1.0, ALU.add)
        self.invert(t1, t1)
        self.fused(ln, x, 1.0, t1, ALU.add, ALU.mult)
        self.ask()
        self.scale(out, ln, 0.5)
        self.pair(t1, x, x)
        self.scale(t2, t1, 1 / 7, ALU.mult, 1 / 5, ALU.add)
        self.pair(t2, t2, t1)
        self.scale(t2, t2, 1 / 3, ALU.add)
        self.pair(t2, t2, t1)
        self.fused(t2, t2, 1.0, x, ALU.add, ALU.mult)
        self.scale(t1, x, 0.05, ALU.is_lt)
        self.choose(out, t2, t1)

    def tanh(self, out, x, t1, t2, e):
        self.ask()
        self.scale(t1, e, 1.0, ALU.add)
        self.invert(t1, t1)
        self.scale(t2, e, -1.0, ALU.mult, 1.0, ALU.add)
        self.pair(out, t2, t1)
        self.pair(t1, x, x)
        self.scale(t2, t1, 2 / 15, ALU.mult, -1 / 3, ALU.add)
        self.pair(t2, t2, t1)
        self.fused(t2, t2, 1.0, x, ALU.add, ALU.mult)
        self.scale(t1, x, 0.02, ALU.is_lt)
        self.choose(out, t2, t1)


def answers(act, asked, answered, questions):
    for n, (out, function, of, scale) in enumerate(questions):
        act.wait_ge(asked, n + 1)
        act.activation(out, of, function, scale=scale).then_inc(answered, 1)


def setup(nc, dram, keep):
    with ExitStack() as stack:
        kit = Kit(nc, stack, "setup")
        (loaded, made) = kit.sems("loaded made")
        with nc.Block() as block:
            @block.sync
            def _(sp):
                sp.dma_start(keep["ident"][:], dram["ident"]).then_inc(loaded, 16)
                sp.wait_ge(loaded, 16)

            @block.vector
            def _(dve):
                dve.wait_ge(loaded, 16)
                dve.tensor_copy(keep["ident16"][:], keep["ident"][:]).then_inc(made, 1)

            @block.gpsimd
            def _(pool):
                pool.memset(keep["ones16"][:], 1.0).then_inc(made, 1)
                pool.wait_ge(made, 2)

        kit.close()

def prep0(nc, dram, keep):
    with ExitStack() as stack:
        kit = Kit(nc, stack, "p0")
        x_all, h = kit.sb("x_all", [T, D]), kit.sb("h", [2, D])
        hT_hi, hT_lo = kit.sb("hT_hi", [2, KC, P], F16), kit.sb("hT_lo", [2, KC, P], F16)
        NX = 2 * D + 2
        w = kit.sb("w", [KC, NX])
        w_hi, w_lo = kit.sb("w_hi", [KC, NX], F16), kit.sb("w_lo", [KC, NX], F16)
        wt, avec = kit.sb("wt", [KC, D]), kit.sb("avec", [KC, 2])
        stats, mv = kit.sb("stats", [2, 6]), kit.sb("mv", [2, 2])
        std, rstd, nmr = kit.sb("std", [2]), kit.sb("rstd", [2]), kit.sb("nmr", [2])
        uvT = kit.sb("uvT", [P])
        zsum, ones32 = kit.sb("zsum", [2 * D]), kit.sb("ones32", [P])
        tp = kit.ps("tp", [2, KC, P])
        main = kit.ps("main", [2, 2 * D])
        small = kit.ps("small", [2, 256])
        z_hi, z_lo, uv, cs = keep["z_hi"], keep["z_lo"], keep["uv"], keep["cs0"]
        x_in = kit.sems(" ".join(f"x_in{c}" for c in range(len(CHUNKS))))
        s = dict(zip("stats mv var std rstd nmr w_hi w_lo".split(),
                     kit.sems("stats mv var std rstd nmr w_hi w_lo")))
        (w_in, gate, a_in, wa_made, wa_copied, h_ready, tp_ready, hi_ready, lo_done, prod_done, z_hi_done,
         z_lo_done, uv_done, uvt_ready, uvt_copied, cs_ready, rows_out, used, zsum_made, zero_made) = kit.sems(
            "w_in gate a_in wa_made wa_copied h_ready tp_ready hi_ready lo_done prod_done z_hi_done "
            "z_lo_done uv_done uvt_ready uvt_copied cs_ready rows_out used zsum_made zero_made")
        x_t = tiles(dram["x0"])

        with nc.Block() as block:
            @block.sync
            def _(sp):
                for ring in (lo_done, prod_done, z_lo_done, uv_done):
                    sp.sem_inc(ring, 2)
                for c, (t0, n) in enumerate(CHUNKS):
                    sp.dma_start(x_all[:, t0:t0 + n, :], x_t[:, t0:t0 + n, :]).then_inc(x_in[c], 16)
                    if c == 0:
                        sp.dma_start(wt[:], dram["w0t"].rearrange("(k p) n -> p k n", p=P)).then_inc(a_in, 16)
                        sp.dma_start(avec[:], dram["a0"]).then_inc(a_in, 16)
                    if c < 2:
                        sp.dma_start(w[:, :, c * D:(c + 1) * D],
                                     dram["wtr0"][c * D:(c + 1) * D, :].rearrange("(k p) n -> p k n", p=P)).then_inc(w_in, 16)
                sp.wait_ge(uvt_copied, 1)
                sp.dma_start(dram["rows"][0:2 * T, :], uvT[0:2 * T, :]).then_inc(rows_out, 16)
                sp.wait_ge(rows_out, 16)

            @block.scalar
            def _(act):

                def normalise(t, b):
                    act.wait_ge(s["nmr"], t + 1)
                    act.wait_ge(tp_ready, free(t))
                    act.activation(h[:, b, :], flat(x_all[:, ds(t, 1), :]), ACT.Relu,
                                   bias=nmr[:, b:b + 1], scale=rstd[:, b:b + 1]).then_inc(h_ready, 1)

                def high(t, b):
                    act.wait_ge(tp_ready, done(t))
                    act.wait_ge(prod_done, free(t))
                    act.activation(hT_hi[:, b], tp[:, b], ACT.Copy).then_inc(hi_ready, 1)

                def finish(t, b):
                    act.wait_ge(prod_done, done(t))
                    act.activation(flat(z_hi[:, ds(t, 1), :]), main[:, b, :], ACT.Copy, scale=1 / WS).then_inc(z_hi_done, 1)

                act.sem_inc(tp_ready, 2)
                pipeline(act, (2, high), (4, lambda t, b: root(act, t, b, std, s)), (3, normalise), (0, finish))

            @block.tensor
            def _(pe):
                pe.wait_ge(a_in, 32)
                for m in range(KC):
                    for k in range(KC):
                        last = pe.matmul(small[:, 0, 2 * m:2 * m + 2], wt[:, k, m * P:(m + 1) * P], avec[:, k, :],
                                         start=(k == 0), stop=(k == KC - 1))
                last.then_inc(wa_made, 1)

                def transpose(t, b):
                    pe.wait_ge(h_ready, t + 1)
                    pe.wait_ge(lo_done, free(t))
                    for k in range(KC):
                        last = pe.transpose(tp[:, b, k, :], h[:, b, k * P:(k + 1) * P], keep["ident"][:])
                    last.then_inc(tp_ready, 1)

                def products(t, b):
                    pe.wait_ge(hi_ready, t + 1)
                    pe.wait_ge(lo_done, done(t))
                    pe.wait_ge(z_lo_done, free(t))
                    for half in range(2):
                        cols = slice(half * D, (half + 1) * D)
                        split_product(pe, main[:, b, cols], hT_hi[:, b], hT_lo[:, b], w_hi, w_lo, cols)
                    pe.wait_ge(uv_done, done(t - 1))
                    last = split_product(pe, small[:, b, 0:2], hT_hi[:, b], hT_lo[:, b], w_hi, w_lo, slice(2 * D, NX))
                    last.then_inc(prod_done, 1)

                pipeline(pe, (2, transpose), (1, products),
                         before=[(-1, lambda: pe.wait_ge(s["w_lo"], 1))])
                pe.wait_ge(uv_done, done(T - 1))
                pe.transpose(tp[0:2 * T, 0, 0, :], uv[:].rearrange("p s t -> p (s t)"), keep["ident"][:]).then_inc(uvt_ready, 1)
                pe.wait_ge(zsum_made, 2 * T)
                for half in range(2):
                    of = slice(half * D, (half + 1) * D)
                    last = pe.matmul(main[:, 0, of], ones32[:], zsum[:, of], start=True, stop=True, skip_group_check=True)
                last.then_inc(cs_ready, 1)

            @block.gpsimd
            def _(pool):
                pool.memset(ones32[:], 1.0)
                pool.memset(zsum[:], 0.0).then_inc(zero_made, 1)
                pool.wait_ge(zero_made, 1)

                def add(t, b):
                    wait_count(pool, z_lo_done, done(t), gate)
                    for n, part in enumerate((z_hi, z_lo)):
                        if n == 1 or not isinstance(t, int) or t > 0:
                            wait_count(pool, zsum_made, 2 * t + n, gate)
                        pool.tensor_tensor(zsum[:], zsum[:], flat(part[:, ds(t, 1), :]), ALU.add).then_inc(zsum_made, 1)

                add(0, 0)
                add(1, 1)
                with pool.Fori(2, T - 1, 2) as t:
                    for b in range(2):
                        add(t + b, b)

            @block.vector
            def _(dve):
                def weights():
                    dve.wait_ge(wa_made, 1)
                    dve.tensor_copy(w[:, :, 2 * D:NX], small[:, 0, 0:2 * KC].rearrange("p (m s) -> p m s", s=2)).then_inc(wa_copied, 1)
                    dve.wait_ge(wa_copied, 1)
                    dve.wait_ge(w_in, 32)
                    split_weights(dve, w, w_hi, w_lo, s)

                def split(t, b):
                    dve.wait_ge(hi_ready, t + 1)
                    dve.tensor_tensor(hT_lo[:, b], tp[:, b], hT_hi[:, b], ALU.subtract).then_inc(lo_done, 1)

                def dots(t, b):
                    dve.wait_ge(prod_done, done(t))
                    dve.tensor_scalar(uv[:, :, ds(t, 1)], small[:, b, 0:2].unsqueeze(2), 1 / WS, None, ALU.mult).then_inc(uv_done, 1)

                def low(t, b):
                    dve.wait_ge(z_hi_done, t + 1)
                    dve.scalar_tensor_tensor(flat(z_lo[:, ds(t, 1), :]), main[:, b, :], 1 / WS, flat(z_hi[:, ds(t, 1), :]),
                                             ALU.mult, ALU.subtract).then_inc(z_lo_done, 1)

                here = lambda c: dve.wait_ge(x_in[c], 16)
                pipeline(dve, (0, dots), (2, split), (5, lambda t, b: moments(dve, t, b, x_all, stats, mv, std, s, gate)),
                         (4, lambda t, b: shift(dve, t, b, mv, std, rstd, nmr, h_ready, s, gate)), (0, low),
                         before=[(-4, weights)] + [(t0 - 6, lambda c=c: here(c)) for c, (t0, n) in enumerate(CHUNKS)])
                dve.wait_ge(uvt_ready, 1)
                dve.tensor_copy(uvT[0:2 * T, :], tp[0:2 * T, 0, 0, :]).then_inc(uvt_copied, 1)
                dve.wait_ge(cs_ready, 1)
                dve.tensor_copy(cs[:], main[:, 0, :]).then_inc(used, 1)

        kit.close()


def attention0(nc, dram, keep):
    with ExitStack() as stack:
        kit = Kit(nc, stack, "m0")
        HJ = T // 2
        at32 = kit.sb("at32", [2, HJ, BW])
        at16 = kit.sb("at16", [2, HJ, BW], F16)
        u_row, v_row, g_row = kit.sb("u_row", [2, BW]), kit.sb("v_row", [NP]), kit.sb("g_row", [2, 2, BW])
        HN = NP // 2
        a_rows, am, dropped = kit.sb("a_rows", [2, HN]), kit.sb("am", [2, HN], BF16), kit.sb("dropped", [HN], BF16)
        vx, top, sign = kit.sb("vx", [2, 2, 2]), kit.sb("top", [2, 2]), kit.sb("sign", [2, 2])
        s1, s2, g = kit.sb("s1", [2, 2]), kit.sb("s2", [2, 2]), kit.sb("g", [2, 2])
        negv = kit.sb("negv", [T])
        diag, ones32 = kit.sb("diag", [4, P]), kit.sb("ones32", [P])
        r = kit.sb("r", [2, BW])
        sc, e, pm = kit.sb("sc", [2, 2, BW]), kit.sb("e", [2, 2, BW]), kit.sb("pm", [2, 2, BW])
        p_hi, p_lo = kit.sb("p_hi", [4, 2, BW], F16), kit.sb("p_lo", [4, 2, BW], F16)
        o = kit.sb("o", [2, 2, D])
        ym, yp = o[:, :, 1, :], o[:, :, 0, :]
        x = kit.sb("x", [2, D])
        sums, den, rden = kit.sb("sums", [2, 2]), kit.sb("den", [2, 2]), kit.sb("rden", [2, 2])
        acc = kit.ps("acc", [2, 2, D])
        rowsum = kit.ps("rowsum", [512])
        g_all = kit.ps("g_all", [4, P])
        z, cs = (keep["z_hi"], keep["z_lo"]), keep["cs0"]
        ones, iso, uv = keep["ones16"], keep["iso"], keep["uv"]
        u_in = kit.sems("u_in0 u_in1")
        piece_in = kit.sems("piece_in0 piece_in1")
        at_in, at_used, at16_ready, at16_out = ([kit.sems(f"{n}{i}")[0] for i in range(2)] for n in
                                                ("at_in", "at_used", "at16_ready", "at16_out"))
        (rows_in, x_in, r_ready, sc_done, e_done, pm_done, hi_done, lo_done, p_done, acc_free, link,
         y_ready, ye_ready, yp_ready, x_ready, x_out, gate, neg_done, am_made, ext_done, ext_link, diag_made, g_made,
         g_ready, ones_made, v_made, dropped_made) = kit.sems(
            "rows_in x_in r_ready sc_done e_done pm_done hi_done lo_done p_done acc_free link "
            "y_ready ye_ready yp_ready x_ready x_out gate neg_done am_made ext_done ext_link diag_made g_made "
            "g_ready ones_made v_made dropped_made")
        ring4 = lambda gb, j: (gb * T + j) % 4
        EVACUATE_AT, DIVIDE_AT, ELU_AT, FINISH_AT = 3, 6, 6, 8
        MASK_AT, EXTREME_AT = (0, 4, 8, 11), (1, 5, 7, 9, 11, 13, 15, 16)
        SHIFTS_AT, SPREAD_AT, G_ROWS_AT = 18, 16, 19
        x_blocks = lambda name: dram[name].rearrange("(i q p) d -> i p q d", q=2, p=P)
        block_of = lambda ap, ib: ap[ds(ib, 1)].rearrange("o p q d -> p (o q) d")

        def loop_blocks(one_block, eng):
            one_block(0, 0, True, False)
            with eng.Fori(1, IB - 3, 2) as ib:
                for n in range(2):
                    one_block(ib + n, 1 - n, False, False)
            one_block(IB - 2, (IB - 2) % 2, False, False)
            one_block(IB - 1, (IB - 1) % 2, False, True)

        with nc.Block() as block:
            @block.sync
            def _(sp):
                for ring in (sc_done, neg_done, e_done, pm_done, hi_done, lo_done, ext_done):
                    sp.sem_inc(ring, 2)
                sp.sem_inc(p_done, 4)
                for single in (*at_used, *at16_ready, ye_ready, x_ready):
                    sp.sem_inc(single, 1)
                sp.sem_inc(acc_free, 4)
                for out in (*at16_out, x_out):
                    sp.sem_inc(out, 16)
                v = dram["rows"][T:2 * T, :].rearrange("(o t) p -> o (t p)", o=1)
                sp.dma_start(v_row[:], v.broadcast_to([P, NP])).then_inc(rows_in, 16)

                def load_u(ib, gb):
                    src = dram["rows"][ds(2 * ib, 2), :].rearrange("(o t) p -> o (t p)", o=1)
                    sp.dma_start(u_row[:, gb, :], src.broadcast_to([P, BW])).then_inc(u_in[gb], 16)

                def load_mask(ib, half):
                    js = slice(half * HJ, (half + 1) * HJ)
                    sp.wait_ge(at_used[half], ib + 1)
                    wait_count(sp, at16_ready[half], ib + 1, gate)
                    sp.dma_start(at32[:, half], block_of(dram["adjT"][:, :, js, :], ib)).then_inc(at_in[half], 16)

                def store_mask(ib, half):
                    js = slice(half * HJ, (half + 1) * HJ)
                    wait_count(sp, at16_ready[half], ib + 2, gate)
                    sp.dma_start(block_of(dram["at16"][:, :, js, :], ib), at16[:, half]).then_inc(at16_out[half], 16)

                def load_x(ib):
                    wait_count(sp, x_out, ib * 16 + 16, gate)
                    sp.dma_start(x[:], block_of(x_blocks("x0"), ib)).then_inc(x_in, 16)

                def store_x(ib):
                    wait_count(sp, x_ready, ib + 2, gate)
                    sp.dma_start(block_of(x_blocks("x1"), ib), x[:]).then_inc(x_out, 16)

                sp.wait_ge(piece_in[1], 16)
                load_u(0, 0)
                load_u(1, 1)
                load_mask(0, 0)
                load_mask(0, 1)
                store_mask(0, 0)
                load_mask(1, 0)
                store_mask(0, 1)
                load_mask(1, 1)
                def one_block(ib, gb):
                    load_x(ib - 1)
                    wait_count(sp, r_ready, ib * T, gate)
                    load_u(ib + 1, 1 - gb)
                    store_mask(ib, 0)
                    load_mask(ib + 1, 0)
                    store_x(ib - 1)
                    store_mask(ib, 1)
                    load_mask(ib + 1, 1)

                with sp.Fori(1, IB - 3, 2) as ib:
                    for n in range(2):
                        one_block(ib + n, 1 - n)
                one_block(IB - 2, (IB - 2) % 2)
                load_x(IB - 2)
                store_mask(IB - 1, 0)
                store_x(IB - 2)
                store_mask(IB - 1, 1)
                load_x(IB - 1)
                store_x(IB - 1)
                sp.wait_ge(x_out, 16 * (IB + 1))
                for half in range(2):
                    sp.wait_ge(at16_out[half], 16 * (IB + 1))

            @block.gpsimd
            def _(pool):
                def convert(ib, half, part):
                    if part == 0:
                        pool.wait_ge(at16_out[half], ib * 16 + 16)
                        wait_count(pool, at_in[half], ib * 16 + 16, gate)
                    last = pool.tensor_copy(at16[:, half, part], at32[:, half, part])
                    if part == HJ - 1:
                        last.then_inc(at16_ready[half], 1)

                def finish(ib, piece):
                    q, half = divmod(piece % 4, 2)
                    of = slice(half * D // 2, (half + 1) * D // 2)
                    if piece == 0:
                        wait_count(pool, x_in, ib * 16 + 16, gate)
                        wait_count(pool, y_ready, ib + 1, gate)
                    if piece == 4:
                        wait_count(pool, yp_ready, ib * 4 + 4, gate)
                        wait_count(pool, ye_ready, ib + 2, gate)
                    if piece < 4:
                        pool.tensor_tensor(yp[:, q, of], yp[:, q, of], x[:, q, of], ALU.add).then_inc(yp_ready, 1)
                    else:
                        last = pool.tensor_tensor(x[:, q, of], yp[:, q, of], ym[:, q, of], ALU.add)
                        if piece == 7:
                            last.then_inc(x_ready, 1)

                def negative(ib, gb, j):
                    if j == 0:
                        wait_count(pool, g_ready, ib + 1, gate)
                    wait_count(pool, r_ready, ib * T + j + 1, gate)
                    wait_count(pool, e_done, free(ib * T + j), gate)
                    pool.tensor_tensor(sc[:, j % 2, 1, :], g_row[:, gb, 1, :], r[:, j % 2, :], ALU.subtract).then_inc(neg_done, 1)

                def one_block(ib, gb, first, last):
                    for j in range(T):
                        negative(ib, gb, j)
                        convert(ib, j // HJ, j % HJ)
                        if FINISH_AT <= j < FINISH_AT + 8 and not first:
                            finish(ib - 1, j - FINISH_AT)

                pool.memset(ones32[:], 1.0)
                pool.memset(sign[:, 0, :], 1.0)
                pool.memset(sign[:, 1, :], -1.0).then_inc(ones_made, 1)
                loop_blocks(one_block, pool)
                for piece in range(8):
                    finish(IB - 1, piece)

            @block.scalar
            def _(act):

                def relu(ib, gb, j):
                    wait_count(act, sc_done, free(ib * T + j), gate)
                    if j == 0:
                        act.wait_ge(u_in[gb], (ib - gb) * 8 + 16)
                    act.activation(r[:, j % 2, :], u_row[:, gb, :], ACT.Relu,
                                   bias=keep["v08"][:, j:j + 1], scale=0.8).then_inc(r_ready, 1)

                def exp(ib, j):
                    act.wait_ge(sc_done, done(ib * T + j))
                    act.wait_ge(pm_done, free(ib * T + j))
                    v = keep["v02"][:, j:j + 1]
                    act.activation(e[:, j % 2, 0], sc[:, j % 2, 0], ACT.Exp, bias=v)
                    act.wait_ge(neg_done, done(ib * T + j))
                    act.activation(e[:, j % 2, 1], sc[:, j % 2, 1], ACT.Exp, bias=negv[:, j:j + 1]).then_inc(e_done, 1)

                def high(ib, gb, j):
                    act.wait_ge(pm_done, done(ib * T + j))
                    act.wait_ge(p_done, ib * T + j + 1)
                    act.activation(p_hi[:, ring4(gb, j)], pm[:, j % 2], ACT.Copy).then_inc(hi_done, 1)

                def elu(ib):
                    act.wait_ge(y_ready, ib + 1)
                    act.activation(ym, ym, ACT.Exp).then_inc(ye_ready, 1)

                def load(ib, i):
                    q, half = divmod(i, 2)
                    act.dma_start(a_rows[:, i % 2, :], dram["adj"][ds(ib * BW + q * P, P), half * HN:(half + 1) * HN]).then_inc(
                        piece_in[i % 2], 16)

                def mask_rows(ib, i):
                    c = ib * 4 + i
                    act.wait_ge(piece_in[i % 2], (c - i % 2) * 8 + 16)
                    act.wait_ge(ext_done, free(c))
                    act.activation(am[:, i % 2, :], a_rows[:, i % 2, :], ACT.Copy, scale=BIG, bias=-BIG).then_inc(am_made, 1)
                    act.wait_ge(am_made, c + 1)
                    if i < 2:
                        load(ib, i + 2)
                    elif not (isinstance(ib, int) and ib == IB - 1):
                        load(ib + 1, i - 2)

                def g_rows(ib, gb):
                    act.wait_ge(g_made, ib + 1)
                    act.activation(g_row[:, gb].rearrange("p s i -> p (s i)"), g_all[:].rearrange("p n i -> p (n i)"),
                                   ACT.Copy).then_inc(g_ready, 1)

                def one_block(ib, gb, first, last):
                    if first:
                        relu(ib, gb, 0)
                        relu(ib, gb, 1)
                        exp(ib, 0)
                    for j in range(T):
                        if j + 2 < T or not last:
                            relu(ib + (j + 2) // T, gb if j + 2 < T else 1 - gb, (j + 2) % T)
                        if j + 1 < T or not last:
                            exp(ib + (j + 1) // T, (j + 1) % T)
                        high(ib, gb, j)
                        if j == ELU_AT and not first:
                            elu(ib - 1)
                        if not last:
                            if j in MASK_AT:
                                mask_rows(ib + 1, MASK_AT.index(j))
                            if j == G_ROWS_AT:
                                g_rows(ib + 1, 1 - gb)

                load(0, 0)
                load(0, 1)
                act.wait_ge(v_made, 3)
                for i in range(4):
                    mask_rows(0, i)
                g_rows(0, 0)
                loop_blocks(one_block, act)
                elu(IB - 1)

            @block.vector
            def _(dve):

                def scores(ib, gb, j):
                    dve.wait_ge(r_ready, ib * T + j + 1)
                    dve.wait_ge(e_done, free(ib * T + j))
                    if j == 0:
                        dve.wait_ge(g_ready, ib + 1)
                    dve.tensor_tensor(sc[:, j % 2, 0, :], r[:, j % 2, :], g_row[:, gb, 0, :], ALU.add).then_inc(sc_done, 1)

                def mask(ib, j):
                    if j % HJ == 0:
                        dve.wait_ge(at_in[j // HJ], ib * 16 + 16)
                    dve.wait_ge(e_done, done(ib * T + j))
                    dve.wait_ge(hi_done, free(ib * T + j))
                    dve.wait_ge(lo_done, free(ib * T + j))
                    m = at32[:, j // HJ, j % HJ, :].unsqueeze(1).broadcast_to([P, 2, BW])
                    last = dve.scalar_tensor_tensor(pm[:, j % 2], e[:, j % 2], 1.0, m, ALU.min, ALU.mult)
                    last.then_inc(pm_done, 1)
                    if j % HJ == HJ - 1:
                        dve.wait_ge(pm_done, done(ib * T + j))
                        dve.sem_inc(at_used[j // HJ], 1)

                def low(ib, gb, j):
                    dve.wait_ge(hi_done, done(ib * T + j))
                    dve.wait_ge(p_done, ib * T + j + 1)
                    dve.tensor_tensor(p_lo[:, ring4(gb, j)], pm[:, j % 2], p_hi[:, ring4(gb, j)], ALU.subtract).then_inc(lo_done, 1)

                def evacuate(ib):
                    dve.wait_ge(p_done, (ib + 1) * T + 4)
                    dve.tensor_copy(sums[:].rearrange("p q s -> p (q s)"), rowsum[:, 0:4]).then_inc(link, 1)
                    dve.wait_ge(link, ib * 7 + 1)
                    dve.wait_ge(x_ready, ib + 1)
                    for q in range(2):
                        for s in range(2):
                            dve.scalar_tensor_tensor(o[:, q, s, :], cs[:, s * D:(s + 1) * D], iso[:, ds(ib * 2 + q, 1)],
                                                     acc[:, q, s, :], ALU.mult, ALU.add).then_inc(acc_free, 1)

                def divide(ib):
                    for q in range(2):
                        dve.scalar_tensor_tensor(den[:, q, :], iso[:, ds(ib * 2 + q, 1)].broadcast_to([P, 2]), float(N),
                                                 sums[:, q, :], ALU.mult, ALU.add).then_inc(link, 1)
                    dve.wait_ge(link, ib * 7 + 3)
                    dve.reciprocal(rden[:], den[:]).then_inc(link, 1)
                    dve.wait_ge(link, ib * 7 + 4)
                    dve.wait_ge(acc_free, ib * 4 + 8)
                    for q in range(2):
                        last = dve.tensor_scalar(o[:, q, 1, :], o[:, q, 1, :], rden[:, q, 1:2], None, ALU.mult)
                    last.then_inc(link, 1)
                    dve.wait_ge(link, ib * 7 + 5)
                    for q in range(2):
                        last = dve.scalar_tensor_tensor(o[:, q, 0, :], o[:, q, 0, :], rden[:, q, 0:1], o[:, q, 1, :],
                                                        ALU.mult, ALU.subtract)
                    last.then_inc(link, 1)
                    dve.wait_ge(link, ib * 7 + 6)
                    dve.tensor_scalar(ym, yp, 0.0, None, ALU.min).then_inc(link, 1)
                    dve.wait_ge(link, ib * 7 + 7)
                    dve.tensor_scalar(yp, yp, 0.0, -1.0, ALU.max, ALU.add).then_inc(y_ready, 1)

                def extreme(ib, i, least):
                    c = ib * 4 + i
                    wait_count(dve, am_made, c + 1, gate)
                    if least:
                        wait_count(dve, dropped_made, c + 1, gate)
                    elif not isinstance(c, int) or c > 0:
                        wait_count(dve, dropped_made, c, gate)
                    q, half = divmod(i, 2)
                    if least:
                        dve.tensor_tensor_reduce(am[:, i % 2, :], am[:, i % 2, :], v_row[:, half * HN:(half + 1) * HN], 1.0, -3e38,
                                                 ALU.subtract, ALU.max, vx[:, 1, q, half:half + 1]).then_inc(ext_done, 1)
                    else:
                        dve.tensor_tensor_reduce(dropped[:], v_row[:, half * HN:(half + 1) * HN], am[:, i % 2, :], 1.0, -3e38,
                                                 ALU.add, ALU.max, vx[:, 0, q, half:half + 1]).then_inc(dropped_made, 1)

                def shifts(ib):
                    steps = [ib * 6]

                    def then(ins):
                        steps[0] += 1
                        ins.then_inc(ext_link, 1)
                        wait_count(dve, ext_link, steps[0], gate)

                    wait_count(dve, ext_done, done(ib * 4 + 3), gate)
                    of = ds(2 * ib, 2)
                    u = uv[:, 0:1, of].broadcast_to([P, 2, 2])
                    then(dve.tensor_reduce(top[:], vx[:], AXX, ALU.max))
                    dve.tensor_scalar(iso[:, of], top[:, 0, :], -CLAMP, None, ALU.is_lt)
                    dve.tensor_scalar(s2[:], top[:, 0:1, :].broadcast_to([P, 2, 2]), -CLAMP, None, ALU.is_ge)
                    then(dve.scalar_tensor_tensor(s1[:], top[:], -CLAMP, sign[:], ALU.max, ALU.mult))
                    then(dve.tensor_tensor(s1[:], s1[:], u, ALU.add))
                    then(dve.scalar_tensor_tensor(g[:], s1[:], 0.2, s1[:], ALU.mult, ALU.max))
                    dve.tensor_tensor(s2[:], s2[:], sign[:], ALU.mult)
                    then(dve.scalar_tensor_tensor(g[:], u, 0.2, g[:], ALU.mult, ALU.subtract))
                    then(dve.tensor_tensor(g[:], g[:], s2[:], ALU.mult))
                    for n in range(4):
                        last = dve.tensor_scalar(diag[:, n, :], keep["ident"][:], g[:, n // 2, n % 2:n % 2 + 1], None, ALU.mult)
                    last.then_inc(diag_made, 1)

                def one_block(ib, gb, first, last):
                    if first:
                        scores(ib, gb, 0)
                    for j in range(T):
                        if j + 1 < T:
                            scores(ib, gb, j + 1)
                        elif not last:
                            scores(ib + 1, 1 - gb, 0)
                        mask(ib, j)
                        if j > 0:
                            low(ib, gb, j - 1)
                        elif not first:
                            low(ib - 1, 1 - gb, T - 1)
                        if j == EVACUATE_AT and not first:
                            evacuate(ib - 1)
                        if j == DIVIDE_AT and not first:
                            divide(ib - 1)
                        if not last:
                            if j in EXTREME_AT:
                                n = EXTREME_AT.index(j)
                                extreme(ib + 1, n // 2, n % 2 == 1)
                            if j == SHIFTS_AT:
                                shifts(ib + 1)

                dve.tensor_scalar(keep["v08"][:], uv[:, 1, :], 0.8, None, ALU.mult).then_inc(v_made, 1)
                dve.tensor_scalar(keep["v02"][:], uv[:, 1, :], 0.2, None, ALU.mult).then_inc(v_made, 1)
                dve.tensor_scalar(negv[:], uv[:, 1, :], -0.2, None, ALU.mult).then_inc(v_made, 1)
                dve.wait_ge(rows_in, 16)
                dve.wait_ge(ones_made, 1)
                for i in range(4):
                    for least in (False, True):
                        extreme(0, i, least)
                shifts(0)
                loop_blocks(one_block, dve)
                low(IB - 1, (IB - 1) % 2, T - 1)
                evacuate(IB - 1)
                divide(IB - 1)

            @block.tensor
            def _(pe):
                def products(ib, gb, j):
                    pe.wait_ge(lo_done, done(ib * T + j))
                    for q in range(2):
                        i = slice(q * P, (q + 1) * P)
                        for s in range(2):
                            zs = [part[:, j, s * D:(s + 1) * D] for part in z]
                            col = rowsum[:, 2 * q + s:2 * q + s + 1]
                            hi, lo = (part[:, ring4(gb, j), s, i] for part in (p_hi, p_lo))
                            if j == 0:
                                pe.wait_ge(acc_free, ib * 4 + 2 * q + s + 1)
                            pe.matmul(acc[:, q, s, :], hi, zs[0], start=(j == 0), stop=False, skip_group_check=True)
                            pe.matmul(acc[:, q, s, :], hi, zs[1], start=False, stop=False, skip_group_check=True)
                            pe.matmul(col, hi, ones[:, 0:1], start=(j == 0 and q == 0 and s == 0), stop=False,
                                      skip_group_check=True)
                            pe.matmul(acc[:, q, s, :], lo, zs[0], start=False, stop=(j == T - 1), skip_group_check=True)
                            last = pe.matmul(col, lo, ones[:, 0:1], start=False, stop=(j == T - 1), skip_group_check=True)
                    last.then_inc(p_done, 1)

                def spread(ib):
                    pe.wait_ge(diag_made, ib + 1)
                    if not isinstance(ib, int) or ib > 0:
                        pe.wait_ge(g_ready, ib)
                    for n in range(4):
                        last = pe.matmul(g_all[:, n, :], ones32[:], diag[:, n, :], start=(n == 0), stop=True, skip_group_check=True)
                    last.then_inc(g_made, 1)

                def one_block(ib, gb, first, last):
                    for j in range(T):
                        if j == SPREAD_AT and not last:
                            spread(ib + 1)
                        products(ib, gb, j)

                pe.wait_ge(ones_made, 1)
                spread(0)
                loop_blocks(one_block, pe)

        kit.close()

def prep1(nc, dram, keep):
    with ExitStack() as stack:
        kit = Kit(nc, stack, "p1")
        x_all, h = kit.sb("x_all", [T, D]), kit.sb("h", [2, D])
        hT_hi, hT_lo = kit.sb("hT_hi", [2, KC, P], F16), kit.sb("hT_lo", [2, KC, P], F16)
        NX = D + 2 * H
        w = kit.sb("w", [KC, NX])
        w_hi, w_lo = kit.sb("w_hi", [KC, NX], F16), kit.sb("w_lo", [KC, NX], F16)
        a12, a12s, prod = kit.sb("a12", [2 * H, DH]), kit.sb("a12s", [2 * H, DH]), kit.sb("prod", [2 * H, DH])
        aln, bln, wsum = kit.sb("aln", [DH]), kit.sb("bln", [DH]), kit.sb("wsum", [KC, H])
        ab, wprod = kit.sb("ab", [2 * H]), kit.sb("wprod", [2, KC, H, DH])
        stats, mv = kit.sb("stats", [2, 6]), kit.sb("mv", [2, 2])
        std, rstd, nmr = kit.sb("std", [2]), kit.sb("rstd", [2]), kit.sb("nmr", [2])
        sq, c_out = kit.sb("sq", [2, D]), kit.sb("c_out", [2, D])
        ss, at = kit.sb("ss", [H, T]), kit.sb("at", [2 * H, T])
        valid, gm, gall = kit.sb("valid", [T]), kit.sb("gm", [H]), kit.sb("gall", [H])
        t1, t2 = kit.sb("t1", [H, T]), kit.sb("t2", [H, T])
        upT = kit.sb("upT", [2, P])
        tp = kit.ps("tp", [2, KC, P])
        main = kit.ps("main", [2, D])
        small = kit.ps("small", [2, 256])
        r, f1, f2, d1, d2, nv = (keep[n] for n in ("r1", "f1", "f2", "d1", "d2", "nv"))
        x_in = kit.sems(" ".join(f"x_in{c}" for c in range(len(CHUNKS))))
        s = dict(zip("stats mv var std rstd nmr w_hi w_lo".split(),
                     kit.sems("stats mv var std rstd nmr w_hi w_lo")))
        c_stored = kit.sems("c_stored0 c_stored1")
        (w_in, gate, w_centred, wprod_made, a_in, link, h_ready, tp_ready, hi_ready, lo_done, prod_done, c_made, sq_made, ss_done,
         dots_done, sd_need, sd_made, g_made, g_all, e_need, e_made, up_ready, upt_made, upt_copied,
         rows_out) = kit.sems(
            "w_in gate w_centred wprod_made a_in link h_ready tp_ready hi_ready lo_done prod_done c_made sq_made ss_done "
            "dots_done sd_need sd_made g_made g_all e_need e_made up_ready upt_made upt_copied rows_out")
        x_t = tiles(dram["x1"])

        with nc.Block() as block:
            @block.sync
            def _(sp):
                for ring in (lo_done, prod_done, c_made, sq_made, ss_done, dots_done):
                    sp.sem_inc(ring, 2)
                for stored in c_stored:
                    sp.sem_inc(stored, 16)
                for c, (t0, n) in enumerate(CHUNKS):
                    sp.dma_start(x_all[:, t0:t0 + n, :], x_t[:, t0:t0 + n, :]).then_inc(x_in[c], 16)
                    if c == 0:
                        sp.dma_start(w[:, :, 0:D], dram["w1"].rearrange("(k p) n -> p k n", p=P)).then_inc(w_in, 16)
                        for n, name in enumerate(("a1", "a2")):
                            sp.dma_start(a12[:, n * H:(n + 1) * H, :].rearrange("p g e -> p (g e)"),
                                         dram[name].broadcast_to([P, D])).then_inc(a_in, 16)
                        sp.dma_start(aln[:], dram["aln"].broadcast_to([P, DH])).then_inc(a_in, 16)
                        sp.dma_start(bln[:], dram["bln"].broadcast_to([P, DH])).then_inc(a_in, 16)
                        sp.dma_start(valid[:], dram["valid"]).then_inc(a_in, 16)

                def store(t, b):
                    sp.wait_ge(c_made, done(t))
                    sp.dma_start(dram["c1"].rearrange("(t p) d -> t p d", p=P)[ds(t, 1)].rearrange("o p d -> p (o d)"),
                                 c_out[:, b, :]).then_inc(c_stored[b], 16)

                loop_tiles(sp, store)
                for stored in c_stored:
                    sp.wait_ge(stored, 16 * (T // 2 + 1))
                sp.wait_ge(upt_copied, 1)
                for n in range(2):
                    sp.dma_start(dram["rows1"][n * 4 * T:(n + 1) * 4 * T, :], upT[0:4 * T, n, :]).then_inc(rows_out, 16)
                sp.wait_ge(rows_out, 32)

            @block.scalar
            def _(act):

                def normalise(t, b):
                    act.wait_ge(s["nmr"], t + 1)
                    act.wait_ge(tp_ready, free(t))
                    act.activation(h[:, b, :], flat(x_all[:, ds(t, 1), :]), ACT.Relu,
                                   bias=nmr[:, b:b + 1], scale=rstd[:, b:b + 1]).then_inc(h_ready, 1)

                def high(t, b):
                    act.wait_ge(tp_ready, done(t))
                    act.wait_ge(prod_done, free(t))
                    act.activation(hT_hi[:, b], tp[:, b], ACT.Copy).then_inc(hi_ready, 1)

                def finish(t, b):
                    act.wait_ge(prod_done, done(t))
                    act.wait_ge(c_stored[b], 8 * (t - b) + 16)
                    act.activation(c_out[:, b, :], main[:, b, :], ACT.Copy, scale=1 / WS).then_inc(c_made, 1)
                    act.wait_ge(ss_done, free(t))
                    act.activation(sq[:, b, :], main[:, b, :], ACT.Square, scale=1 / WS).then_inc(sq_made, 1)

                act.sem_inc(tp_ready, 2)
                pipeline(act, (2, high), (4, lambda t, b: root(act, t, b, std, s)), (3, normalise), (0, finish))
                act.wait_ge(sd_need, 1)
                act.activation(ss[:], ss[:], ACT.Sqrt, scale=1 / (DH - 1)).then_inc(sd_made, 1)
                act.wait_ge(e_need, 1)
                for n, (to, of, by) in enumerate(((d1, nv, -1.0), (d2, nv, -0.2), (f1, t1, 0.8), (f2, t2, -0.8))):
                    act.activation(to[:], of[:], ACT.Exp, scale=by).then_inc(e_made, 1)

            @block.tensor
            def _(pe):
                def transpose(t, b):
                    pe.wait_ge(h_ready, t + 1)
                    pe.wait_ge(lo_done, free(t))
                    for k in range(KC):
                        last = pe.transpose(tp[:, b, k, :], h[:, b, k * P:(k + 1) * P], keep["ident"][:])
                    last.then_inc(tp_ready, 1)

                def products(t, b):
                    pe.wait_ge(lo_done, done(t))
                    pe.wait_ge(sq_made, free(t))
                    split_product(pe, main[:, b, :], hT_hi[:, b], hT_lo[:, b], w_hi, w_lo, slice(0, D))
                    pe.wait_ge(dots_done, done(t - 1))
                    last = split_product(pe, small[:, b, 0:2 * H], hT_hi[:, b], hT_lo[:, b], w_hi, w_lo, slice(D, NX))
                    last.then_inc(prod_done, 1)

                pipeline(pe, (2, transpose), (1, products),
                         before=[(-1, lambda: pe.wait_ge(s["w_lo"], 1))])
                pe.wait_ge(up_ready, 1)
                for n in range(2):
                    last = pe.transpose(tp[0:4 * T, n, 0, :], t1[:, 4 * n:4 * n + 4, :].rearrange("p h t -> p (h t)"), keep["ident"][:])
                last.then_inc(upt_made, 1)

            @block.gpsimd
            def _(pool):
                pool.wait_ge(w_centred, 1)
                for k in range(KC):
                    last = pool.tensor_tensor(wprod[:, 1, k], w[:, k, 0:D].rearrange("p (h e) -> p h e", e=DH),
                                              a12s[:, H:2 * H, :], ALU.mult)
                last.then_inc(wprod_made, 1)
                pool.wait_ge(g_made, 1)
                pool.partition_all_reduce(gall[:], gm[:], P, RMAX).then_inc(g_all, 1)

            @block.vector
            def _(dve):
                step = [0]

                def then(ins):
                    step[0] += 1
                    ins.then_inc(link, 1)
                    dve.wait_ge(link, step[0])

                heads = lambda ap: ap.rearrange("p (h e) -> p h e", e=DH)
                def weights():
                    dve.wait_ge(a_in, 80)
                    then(dve.tensor_tensor(prod[:], a12[:], bln[:].unsqueeze(1).broadcast_to([P, 2 * H, DH]), ALU.mult))
                    then(dve.tensor_reduce(ab[:], prod[:], AXX, ALU.add))
                    then(dve.tensor_tensor(a12s[:], a12[:], aln[:].unsqueeze(1).broadcast_to([P, 2 * H, DH]), ALU.mult))
                    dve.wait_ge(w_in, 16)
                    w_heads = w[:, :, 0:D].rearrange("p k (h e) -> p k h e", e=DH)
                    for k in range(KC):
                        last = dve.tensor_reduce(wsum[:, k], w_heads[:, k], AXX, ALU.add)
                    then(last)
                    for k in range(KC):
                        last = dve.scalar_tensor_tensor(w_heads[:, k], wsum[:, k].unsqueeze(2).broadcast_to([P, H, DH]), -1.0 / DH,
                                                        w_heads[:, k], ALU.mult, ALU.add)
                    then(last)
                    dve.sem_inc(w_centred, 1)
                    for k in range(KC):
                        last = dve.tensor_tensor(wprod[:, 0, k], w_heads[:, k], a12s[:, 0:H, :], ALU.mult)
                    then(last)
                    for n in range(2):
                        if n == 1:
                            dve.wait_ge(wprod_made, 1)
                        for k in range(KC):
                            last = dve.tensor_reduce(w[:, k, D + n * H:D + (n + 1) * H], wprod[:, n, k], AXX, ALU.add)
                    then(last)
                    split_weights(dve, w, w_hi, w_lo, s)

                def split(t, b):
                    dve.wait_ge(hi_ready, t + 1)
                    dve.tensor_tensor(hT_lo[:, b], tp[:, b], hT_hi[:, b], ALU.subtract).then_inc(lo_done, 1)

                def dots(t, b):
                    dve.wait_ge(prod_done, done(t))
                    dve.tensor_scalar(at[:, :, ds(t, 1)], small[:, b, 0:2 * H].unsqueeze(2), 1 / WS, None,
                                      ALU.mult).then_inc(dots_done, 1)

                def sum_squares(t, b):
                    dve.wait_ge(sq_made, done(t))
                    dve.tensor_reduce(ss[:, :, ds(t, 1)], heads(sq[:, b, :]), AXX, ALU.add).then_inc(ss_done, 1)

                here = lambda c: dve.wait_ge(x_in[c], 16)
                pipeline(dve, (0, dots), (2, split), (5, lambda t, b: moments(dve, t, b, x_all, stats, mv, std, s, gate)),
                         (4, lambda t, b: shift(dve, t, b, mv, std, rstd, nmr, h_ready, s, gate)), (0, sum_squares),
                         before=[(-4, weights)] + [(t0 - 6, lambda c=c: here(c)) for c, (t0, n) in enumerate(CHUNKS)])
                dve.wait_ge(ss_done, done(T - 1))
                dve.sem_inc(sd_need, 1)
                dve.wait_ge(sd_made, 1)
                then(dve.tensor_scalar(ss[:], ss[:], 1e-6, None, ALU.add))
                then(dve.reciprocal(r[:], ss[:]))
                for n in range(2):
                    then(dve.tensor_tensor(at[:, n * H:(n + 1) * H, :], at[:, n * H:(n + 1) * H, :], r[:], ALU.mult))
                then(dve.tensor_tensor(at[:], at[:], ab[:].unsqueeze(2).broadcast_to([P, 2 * H, T]), ALU.add))
                then(dve.tensor_tensor(r[:], r[:], valid[:].unsqueeze(1).broadcast_to([P, H, T]), ALU.mult))
                dve.tensor_reduce(gm[:], at[:, H:2 * H, :], AXX, ALU.max).then_inc(g_made, 1)
                dve.wait_ge(g_all, 1)
                g = gall[:].unsqueeze(2).broadcast_to([P, H, T])
                then(dve.tensor_tensor(nv[:], g, at[:, H:2 * H, :], ALU.subtract))
                then(dve.tensor_tensor(t1[:], at[:, 0:H, :], g, ALU.add))
                dve.sem_inc(up_ready, 1)
                dve.wait_ge(upt_made, 1)
                for n in range(2):
                    last = dve.tensor_copy(upT[0:4 * T, n, :], tp[0:4 * T, n, 0, :])
                last.then_inc(upt_copied, 1)
                then(dve.tensor_scalar(t2[:], t1[:], 0.0, None, ALU.max))
                then(dve.tensor_scalar(t1[:], t1[:], 0.0, None, ALU.min))
                dve.sem_inc(e_need, 1)
                dve.wait_ge(e_made, 4)
                then(dve.tensor_scalar(d1[:], d1[:], YS, None, ALU.mult))
                then(dve.tensor_scalar(d2[:], d2[:], YS, None, ALU.mult))

        kit.close()


YS = 4096.0
STEEP = 2.0 ** 80
LS = 2048.0
YW = DH + 1
BLOCKS = [(2 * i, min(2, IB - 2 * i)) for i in range(-(-IB // 2))]


def attention1(nc, dram, keep):
    with ExitStack() as stack:
        kit = Kit(nc, stack, "m1")
        NB = len(BLOCKS)
        COMBINE_AT, DIVIDE_AT, SUM_AT = 6, 15, 17
        RB = 8
        ring = lambda b, n, j: ((b * NB + n) * T + j) % RB
        at = kit.sb("at", [IB, T, BW], F16)
        u = kit.sb("u", [2, 2, BW])
        c = kit.sb("c", [2, T, DH])
        yf = kit.sb("yf", [T, YW])
        y12 = kit.sb("y12", [2, T, 2, 2, YW], F16)
        y2 = kit.sb("y2", [2, T, 2, YW], F16)
        nvk, nvs = kit.sb("nvk", [2, T]), kit.sb("nvs", [2, T])
        above = kit.sb("above", [2, 2, BW], BF16)
        b01 = kit.sb("b01", [RB, 2, BW], F16)
        lowp, both = kit.sb("lowp", [4, 2, YW]), kit.sb("both", [2, 4, 2, YW])
        num, part = kit.sb("num", [4, YW]), kit.sb("part", [4, YW])
        rden, yo = kit.sb("rden", [4]), kit.sb("yo", [2, 4, DH])
        csp, cs = kit.sb("csp", [2, DH]), kit.sb("cs", [2, YW])
        acc = kit.ps("acc", [2, 4, 512])
        r, f1, f2, d1, d2, nv = (keep[n] for n in ("r1", "f1", "f2", "d1", "d2", "nv"))
        iso = keep["iso"]
        at_in, u_in, c_in, y_out = (kit.sems(n) for n in
                                    (" ".join(f"at_in{i}" for i in range(NB)), "u_in0 u_in1", "c_in0 c_in1", "y_out0 y_out1"))
        (u_done, nvk_made, nvs_made, above_made, chat_made, yf_made, yhi_made, diff_made, ylo_made, b_ready, b_used, acc_free,
         low_made, both_made, den_made, rden_made, y_made, csp_made, cs_made, head_done, link, gate) = kit.sems(
            "u_done nvk_made nvs_made above_made chat_made yf_made yhi_made diff_made ylo_made b_ready b_used acc_free "
            "low_made both_made den_made rden_made y_made csp_made cs_made head_done link gate")

        SHARED = [list(range({1: 3, 2: T, 3: T, 4: 7, 5: 3}.get(n, 3), T, 2)) for n in range(NB)]
        EARLY = (0, 1, 4, 5)
        shares = [(n, j) for n in range(NB) for j in SHARED[n]]

        def acc_view(bank, nt):
            return acc[:, bank, 0:nt, 0:4 * YW].rearrange("p t (l y e) -> p t l y e", l=2, y=2)

        def scale_head(eng, k, b):
            eng.wait_ge(head_done, free(k))
            wait_count(eng, c_in[b], (k - b) * 8 + 16, gate)
            eng.tensor_copy(nvk[:, b, :].unsqueeze(1), nv[:, ds(k, 1), :]).then_inc(nvk_made, 1)
            wait_count(eng, nvk_made, k + 1, gate)
            eng.tensor_scalar(nvs[:, b, :], nvk[:, b, :], -STEEP, None, ALU.mult).then_inc(nvs_made, 1)
            eng.tensor_tensor(c[:, b], c[:, b], r[:, ds(k, 1), :].rearrange("p o t -> p (o t)").unsqueeze(2).broadcast_to([P, T, DH]),
                               ALU.mult).then_inc(chat_made, 1)

        def build(eng, k, b, n):
            if n == 0:
                wait_count(eng, chat_made, k + 1, gate)
            dk = (d1, d2)[n][:, ds(k, 1), :].rearrange("p o t -> p (o t)").unsqueeze(2)
            if not (isinstance(k, int) and k == 0 and n == 0):
                wait_count(eng, ylo_made, 2 * k + n, gate)
            eng.tensor_tensor(yf[:, :, 0:DH], c[:, b], dk.broadcast_to([P, T, DH]), ALU.mult).then_inc(yf_made, 1)
            eng.tensor_copy(yf[:, :, DH:YW], dk).then_inc(yf_made, 1)
            hi = y12[:, b, :, 0, 0, :] if n == 0 else y2[:, b, :, 0, :]
            eng.wait_ge(yhi_made, 2 * k + n + 1)
            eng.tensor_tensor(yf[:], yf[:], hi, ALU.subtract).then_inc(diff_made, 1)

        with nc.Block() as block:
            @block.sync
            def _(sp):
                sp.sem_inc(b_used, RB)
                sp.sem_inc(acc_free, 2)
                sp.sem_inc(head_done, 2)
                for out in y_out:
                    sp.sem_inc(out, 16)

                def load_c(k, b):
                    sp.dma_start(c[:, b], dram["c1"].rearrange("(t p) (k e) -> k p t e", p=P, e=DH)[ds(k, 1)].rearrange(
                        "o p t e -> p (o t) e")).then_inc(c_in[b], 16)

                def load_u(k, n):
                    i0, nb = BLOCKS[n]
                    src = dram["rows1"].rearrange("(k t) p -> k (t p)", k=H)[ds(k, 1), i0 * BW:(i0 + nb) * BW]
                    sp.dma_start(u[:, n % 2, 0:nb, :].rearrange("p n c -> p (n c)"),
                                 src.broadcast_to([P, nb * BW])).then_inc(u_in[n % 2], 16)

                def head(k, b, more, last):
                    for n, (i0, nb) in enumerate(BLOCKS):
                        g = k * NB + n
                        if n + 2 < NB or not last:
                            sp.wait_ge(u_done, g + 1)
                            load_u(k if n + 2 < NB else k + 1, (n + 2) % NB)
                        wait_count(sp, y_made, g + 1, gate)
                        sp.dma_start(dram["y1"].rearrange("(t p) (k e) -> k p t e", p=P, e=DH)[ds(k, 1), :, 2 * i0:2 * (i0 + nb), :].rearrange(
                            "o p t e -> p (o t) e"), yo[:, n % 2, 0:2 * nb, :]).then_inc(y_out[n % 2], 16)
                    if more:
                        load_c(k + 2, b)

                load_c(0, 0)
                load_u(0, 0)
                for i, (i0, nb) in enumerate(BLOCKS):
                    sp.dma_start(at[:, i0:i0 + nb], dram["at16"].rearrange("i p t c -> p i t c")[:, i0:i0 + nb]).then_inc(at_in[i], 16)
                    if i == 0:
                        load_u(0, 1)
                        load_c(1, 1)
                with sp.Fori(0, H - 3, 2) as k:
                    for b in range(2):
                        head(k + b, b, True, False)
                head(H - 2, 0, False, False)
                head(H - 1, 1, False, True)
                for out in y_out:
                    sp.wait_ge(out, 16 * (H * NB // 2 + 1))

            @block.gpsimd
            def _(pool):
                def column_sums(k, b):
                    wait_count(pool, csp_made, k + 1, gate)
                    pool.partition_all_reduce(cs[:, 0, 0:DH], csp[:, 0, :], P, RADD).then_inc(cs_made, 1)
                    wait_count(pool, cs_made, k + 1, gate)
                    pool.tensor_scalar(cs[:, 0, 0:DH], cs[:, 0, 0:DH], YS, None, ALU.mult).then_inc(link, 1)

                def numerator(k, b, n):
                    i0, nb = BLOCKS[n]
                    nt, t0, g = 2 * nb, 2 * i0, k * NB + n
                    steps = g * 6 + k + 2
                    of = lambda f: f[:, ds(k, 1), t0:t0 + nt].rearrange("p o t -> p (o t)").unsqueeze(2).broadcast_to([P, nt, YW])
                    pool.wait_ge(both_made, g + 1)
                    pool.wait_ge(link, steps)
                    pool.tensor_tensor(num[:, 0:nt], both[:, n % 2, 0:nt, 0, :], of(f1), ALU.mult).then_inc(link, 1)
                    pool.tensor_tensor(part[:, 0:nt], both[:, n % 2, 0:nt, 1, :], of(f2), ALU.mult).then_inc(link, 1)
                    pool.wait_ge(link, steps + 2)
                    pool.tensor_tensor(num[:, 0:nt], num[:, 0:nt], part[:, 0:nt], ALU.add).then_inc(link, 1)
                    pool.wait_ge(link, steps + 3)
                    pool.tensor_tensor(part[:, 0:nt], cs[:, 0, :].unsqueeze(1).broadcast_to([P, nt, YW]),
                                       iso[:, t0:t0 + nt].unsqueeze(2).broadcast_to([P, nt, YW]), ALU.mult).then_inc(link, 1)
                    pool.wait_ge(link, steps + 4)
                    pool.tensor_tensor(num[:, 0:nt], num[:, 0:nt], part[:, 0:nt], ALU.add).then_inc(den_made, 1)

                def quotient(k, b, n):
                    i0, nb = BLOCKS[n]
                    nt, t0, g = 2 * nb, 2 * i0, k * NB + n
                    steps = g * 6 + k + 2
                    pool.wait_ge(rden_made, g + 1)
                    pool.wait_ge(y_out[n % 2], (k * NB + n - n % 2) * 8 + 16)
                    pool.tensor_tensor(yo[:, n % 2, 0:nt], num[:, 0:nt, 0:DH], rden[:, 0:nt].unsqueeze(2).broadcast_to([P, nt, DH]),
                                       ALU.mult).then_inc(link, 1)
                    pool.wait_ge(link, steps + 5)
                    pool.tensor_tensor(yo[:, n % 2, 0:nt], yo[:, n % 2, 0:nt], c[:, b, t0:t0 + nt], ALU.add).then_inc(y_made, 1)
                    pool.wait_ge(y_made, g + 1)
                    pool.sem_inc(link, 1)

                def head(k, b, more):
                    column_sums(k, b)
                    for n in range(NB):
                        numerator(k, b, n)
                        if more and n == 0:
                            scale_head(pool, k + 1, 1 - b)
                        if more and n in (1, 2):
                            build(pool, k + 1, 1 - b, n - 1)
                        quotient(k, b, n)

                pool.memset(cs[:], float(N) * YS).then_inc(link, 1)
                pool.wait_ge(link, 1)
                with pool.Fori(0, H - 3, 2) as k:
                    for b in range(2):
                        head(k + b, b, True)
                head(H - 2, 0, True)
                head(H - 1, 1, False)

            @block.scalar
            def _(act):
                def split(k, b, n):
                    hi = y12[:, b, :, 0, 0, :] if n == 0 else y2[:, b, :, 0, :]
                    lo = y12[:, b, :, 1, 0, :] if n == 0 else y2[:, b, :, 1, :]
                    if n == 0:
                        act.wait_ge(head_done, free(k))
                    act.wait_ge(yf_made, 4 * k + 2 * n + 2)
                    act.activation(hi, yf[:], ACT.Copy).then_inc(yhi_made, 1)
                    if n == 1:
                        act.wait_ge(yhi_made, 2 * k + 2)
                        act.activation(y12[:, b, :, 0, 1, :], hi, ACT.Copy, scale=-1.0)
                    act.wait_ge(diff_made, 2 * k + n + 1)
                    if n == 1:
                        act.activation(y12[:, b, :, 1, 1, :], yf[:], ACT.Copy, scale=-LS)
                    act.activation(lo, yf[:], ACT.Copy, scale=LS).then_inc(ylo_made, 1)

                def low(k, n):
                    i0, nb = BLOCKS[n]
                    g = k * NB + n
                    act.wait_ge(b_used, (g + 1) * T + RB)
                    if not isinstance(g, int) or g > 0:
                        act.wait_ge(both_made, g)
                    act.activation(lowp[:, 0:2 * nb], acc_view(n % 2, 2 * nb)[:, :, 1], ACT.Copy, scale=1 / LS).then_inc(low_made, 1)

                def compare(k, b, n, j):
                    i = shares.index((n, j))
                    n2, j2 = shares[i - 2]
                    if i >= 2:
                        act.wait_ge(b_ready, (k * NB + n2) * T + j2 + 1)
                    elif not (isinstance(k, int) and k == 0):
                        act.wait_ge(b_ready, ((k - 1) * NB + n2) * T + j2 + 1)
                    nb = BLOCKS[n][1]
                    act.activation(above[:, i % 2, 0:nb], u[:, n % 2, 0:nb], ACT.Relu, bias=nvs[:, b, j:j + 1],
                                   scale=STEEP).then_inc(above_made, 1)

                def early(k, b, n):
                    if n == 0:
                        act.wait_ge(nvs_made, k + 1)
                    act.wait_ge(u_in[n % 2], (k * NB + n - n % 2) * 8 + 16)
                    for j in SHARED[n][:2]:
                        compare(k, b, n, j)

                def head(k, b, more):
                    for n in range(NB):
                        if SHARED[n] and n not in EARLY:
                            act.wait_ge(u_in[n % 2], (k * NB + n - n % 2) * 8 + 16)
                        for j in SHARED[n][2:] if n in EARLY else SHARED[n]:
                            compare(k, b, n, j)
                        if n + 1 in EARLY:
                            early(k, b, n + 1)
                        elif n == NB - 1 and more:
                            early(k + 1, 1 - b, 0)
                        low(k, n)
                        if more and n in (1, 2):
                            split(k + 1, 1 - b, n - 1)

                early(0, 0, 0)
                split(0, 0, 0)
                split(0, 0, 1)
                with act.Fori(0, H - 3, 2) as k:
                    for b in range(2):
                        head(k + b, b, True)
                head(H - 2, 0, True)
                head(H - 1, 1, False)

            @block.vector
            def _(dve):
                def combine(k, n):
                    i0, nb = BLOCKS[n]
                    g = k * NB + n
                    dve.wait_ge(low_made, g + 1)
                    dve.tensor_tensor(both[:, n % 2, 0:2 * nb], acc_view(n % 2, 2 * nb)[:, :, 0], lowp[:, 0:2 * nb],
                                      ALU.add).then_inc(both_made, 1)
                    dve.wait_ge(both_made, g + 1)
                    dve.sem_inc(acc_free, 1)

                def divide(k, n):
                    i0, nb = BLOCKS[n]
                    dve.wait_ge(den_made, k * NB + n + 1)
                    dve.reciprocal(rden[:, 0:2 * nb], num[:, 0:2 * nb, DH]).then_inc(rden_made, 1)

                def sum_head(k, b):
                    dve.wait_ge(chat_made, k + 1)
                    dve.tensor_reduce(csp[:, 0, :], c[:, b].rearrange("p t e -> p e t"), AXX, ALU.add).then_inc(csp_made, 1)

                def head(k, b, first=False, last=False):
                    dve.wait_ge(nvk_made, k + 1)
                    for n, (i0, nb) in enumerate(BLOCKS):
                        g = k * NB + n
                        before = (k, n - 1) if n > 0 else (k - 1, NB - 1)
                        if first:
                            dve.wait_ge(at_in[n], 16)
                        dve.wait_ge(u_in[n % 2], (g - n % 2) * 8 + 16)
                        for j in range(T):
                            m = g * T + j
                            dve.wait_ge(b_used, m + 1)
                            to, mask = b01[:, ring(b, n, j), 0:nb], at[:, i0:i0 + nb, j, :]
                            if j in SHARED[n]:
                                i = shares.index((n, j))
                                dve.wait_ge(above_made, k * len(shares) + i + 1)
                                dve.tensor_tensor(to, above[:, i % 2, 0:nb], mask, ALU.min).then_inc(b_ready, 1)
                            else:
                                dve.scalar_tensor_tensor(to, u[:, n % 2, 0:nb], nvk[:, b, j:j + 1], mask,
                                                         ALU.is_gt, ALU.mult).then_inc(b_ready, 1)
                            if j == COMBINE_AT and not (first and n == 0):
                                combine(*before)
                            if j == DIVIDE_AT and not (first and n == 0):
                                divide(*before)
                            if j == SUM_AT and n == NB - 2 and not last:
                                sum_head(k + 1, 1 - b)
                        dve.wait_ge(b_ready, (g + 1) * T)
                        dve.sem_inc(u_done, 1)

                scale_head(dve, 0, 0)
                build(dve, 0, 0, 0)
                build(dve, 0, 0, 1)
                sum_head(0, 0)
                head(0, 0, first=True)
                with dve.Fori(1, H - 2, 2) as k:
                    for b in range(2):
                        head(k + b, 1 - b)
                head(H - 1, 1, last=True)
                combine(H - 1, NB - 1)
                divide(H - 1, NB - 1)

            @block.tensor
            def _(pe):
                def head(k, b, first=False):
                    pe.wait_ge(ylo_made, 2 * k + 2)
                    for n, (i0, nb) in enumerate(BLOCKS):
                        g = k * NB + n
                        pe.wait_ge(acc_free, free(g))
                        if first:
                            pe.wait_ge(at_in[n], 16)
                        for j in range(T):
                            pe.wait_ge(b_ready, g * T + j + 1)
                            for q in range(2 * nb):
                                half = slice((q % 2) * P, (q % 2 + 1) * P)
                                full = acc_view(n % 2, 2 * nb)[:, q]
                                pe.matmul(full.rearrange("p l y e -> p (l y e)"), b01[:, ring(b, n, j), q // 2, half],
                                          y12[:, b, j].rearrange("p l y e -> p (l y e)"), start=(j == 0), stop=False,
                                          skip_group_check=True)
                                last = pe.matmul(full[:, :, 1, :], at[:, i0 + q // 2, j, half], y2[:, b, j],
                                                 start=False, stop=(j == T - 1), skip_group_check=True)
                            last.then_inc(b_used, 1)
                    pe.sem_inc(head_done, 1)

                head(0, 0, first=True)
                with pe.Fori(1, H - 2, 2) as k:
                    for b in range(2):
                        head(k + b, 1 - b)
                head(H - 1, 1)

        kit.close()

XS = 2.0 ** -10
EMIN = 2.0 ** -25


def prep2(nc, dram, keep):
    with ExitStack() as stack:
        kit = Kit(nc, stack, "p2")
        x_all, h = kit.sb("x_all", [T, D]), kit.sb("h", [2, D])
        hT_hi, hT_lo = kit.sb("hT_hi", [2, KC, P], F16), kit.sb("hT_lo", [2, KC, P], F16)
        w = kit.sb("w", [KC, D])
        w_hi, w_lo = kit.sb("w_hi", [KC, D], F16), kit.sb("w_lo", [KC, D], F16)
        y, low, el = kit.sb("y", [2, 6, D]), kit.sb("low", [6, D]), kit.sb("el", [6, D])
        aln, bln = kit.sb("aln", [DH]), kit.sb("bln", [DH])
        stats, mv = kit.sb("stats", [2, 6]), kit.sb("mv", [2, 2])
        std, rstd, nmr = kit.sb("std", [2]), kit.sb("rstd", [2]), kit.sb("nmr", [2])
        sq = kit.sb("sq", [2, 2, D])
        ssq = kit.sb("ssq", [2, T])
        v = kit.sb("v", [10, T])
        tp = kit.ps("tp", [2, KC, P])
        main = kit.ps("main", [2, D])
        xs_hi, xs_lo, gcol = keep["xs_hi"], keep["xs_lo"], keep["gcol"]
        x_in = kit.sems(" ".join(f"x_in{c}" for c in range(len(CHUNKS))))
        x_out = kit.sems(" ".join(f"x_out{c}" for c in range(len(CHUNKS))))
        y_in = kit.sems(" ".join(f"y_in{c}" for c in range(len(CHUNKS))))
        s = dict(zip("stats mv var std rstd nmr w_hi w_lo".split(),
                     kit.sems("stats mv var std rstd nmr w_hi w_lo")))
        (w_in, gate, a_in, bln_made, scaled, y_made, low_made, el_made, plus_made, sum_made, x_made, h_ready, hsq_made, hss_done, tp_ready,
         hi_ready, lo_done, prod_done, m_made, msq_made, ssq_done, link, asked, answered, co_made, hi_made, diff_made,
         g_made, used) = kit.sems(
            "w_in gate a_in bln_made scaled y_made low_made el_made plus_made sum_made x_made h_ready hsq_made hss_done tp_ready "
            "hi_ready lo_done prod_done m_made msq_made ssq_done link asked answered co_made hi_made diff_made "
            "g_made used")
        LOW_BY_ACT = (2, 3)
        x_t, y_t = tiles(dram["x1"]), tiles(dram["y1"])
        hn, mn, t1, t2, ln, tt, ee, th, ga, co = (v[:, i, :] for i in range(10))

        with nc.Block() as block:
            @block.sync
            def _(sp):
                for ring in (lo_done, prod_done, msq_made, ssq_done, hss_done):
                    sp.sem_inc(ring, 2)
                sp.dma_start(aln[:], dram["aln"].broadcast_to([P, DH])).then_inc(a_in, 16)
                sp.dma_start(bln[:], dram["bln"].broadcast_to([P, DH])).then_inc(a_in, 16)
                def store(c):
                    t0, n = CHUNKS[c]
                    sp.dma_start(tiles(dram["x2"])[:, t0:t0 + n, :], x_all[:, t0:t0 + n, :]).then_inc(x_out[c], 16)

                for c, (t0, n) in enumerate(CHUNKS):
                    if c >= 2:
                        sp.wait_ge(x_made, c - 1)
                    sp.dma_start(y[:, c % 2, 0:n, :], y_t[:, t0:t0 + n, :]).then_inc(y_in[c], 16)
                    sp.dma_start(x_all[:, t0:t0 + n, :], x_t[:, t0:t0 + n, :]).then_inc(x_in[c], 16)
                    if c == 0:
                        sp.dma_start(w[:], dram["w2"].rearrange("(k p) n -> p k n", p=P)).then_inc(w_in, 16)
                    if c >= 2:
                        store(c - 2)
                for c in range(len(CHUNKS) - 2, len(CHUNKS)):
                    sp.wait_ge(x_made, c + 1)
                    store(c)
                for out in x_out:
                    sp.wait_ge(out, 16)

            @block.gpsimd
            def _(pool):
                pool.wait_ge(a_in, 32)
                pool.tensor_tensor(bln[:], bln[:], bln[:], ALU.add).then_inc(bln_made, 1)
                pool.wait_ge(bln_made, 1)
                for c, (t0, n) in enumerate(CHUNKS):
                    yc = y[:, c % 2, 0:n, :].rearrange("p n (h e) -> p (n h) e", e=DH)
                    pool.wait_ge(y_in[c], 16)
                    pool.tensor_tensor(yc, yc, aln[:].unsqueeze(1).broadcast_to([P, n * H, DH]), ALU.mult).then_inc(scaled, 1)
                    pool.wait_ge(scaled, c + 1)
                    pool.tensor_tensor(yc, yc, bln[:].unsqueeze(1).broadcast_to([P, n * H, DH]), ALU.add).then_inc(y_made, 1)

            @block.scalar
            def _(act):
                def exp(c):
                    act.wait_ge(low_made, c + 1)
                    n = CHUNKS[c][1]
                    act.activation(el[:, 0:n, :], low[:, 0:n, :], ACT.Exp).then_inc(el_made, 1)


                def normalise(t, b):
                    act.wait_ge(s["nmr"], t + 1)
                    act.wait_ge(tp_ready, free(t))
                    act.wait_ge(hss_done, free(t))
                    act.activation(h[:, b, :], flat(x_all[:, ds(t, 1), :]), ACT.Relu,
                                   bias=nmr[:, b:b + 1], scale=rstd[:, b:b + 1]).then_inc(h_ready, 1)
                    act.wait_ge(h_ready, t + 1)
                    act.activation(sq[:, b, 0, :], h[:, b, :], ACT.Square).then_inc(hsq_made, 1)

                def high(t, b):
                    act.wait_ge(tp_ready, done(t))
                    act.wait_ge(prod_done, free(t))
                    act.activation(hT_hi[:, b], tp[:, b], ACT.Copy).then_inc(hi_ready, 1)

                def finish(t, b):
                    act.wait_ge(prod_done, done(t))
                    act.activation(flat(x_all[:, ds(t, 1), :]), main[:, b, :], ACT.Copy, scale=1 / WS).then_inc(m_made, 1)
                    act.wait_ge(ssq_done, free(t))
                    act.activation(sq[:, b, 1, :], main[:, b, :], ACT.Square, scale=1 / WS).then_inc(msq_made, 1)

                act.sem_inc(tp_ready, 2)
                pipeline(act, (2, high), (4, lambda t, b: root(act, t, b, std, s)), (3, normalise), (0, finish),
                         before=[(-4 if c == 1 else t0 - 8, lambda c=c: exp(c)) for c, (t0, n) in enumerate(CHUNKS)] +
                                [(t0, lambda c=c: act.wait_ge(x_out[c], 16)) for c, (t0, n) in enumerate(CHUNKS)])
                answers(act, asked, answered, [(v[:, 0:2, :], ACT.Sqrt, ssq[:], 1.0), (ln, ACT.Ln, ln, 1.0),
                                               (ee, ACT.Exp, tt, -2.0)])
                act.wait_ge(co_made, 1)

                def high_part(t, b):
                    act.activation(flat(xs_hi[:, ds(t, 1), :]), flat(x_all[:, ds(t, 1), :]), ACT.Copy,
                                   scale=co[:, ds(t, 1)]).then_inc(hi_made, 1)

                loop_tiles(act, high_part)
                for c in LOW_BY_ACT:
                    t0, n = CHUNKS[c]
                    act.wait_ge(diff_made, t0 + n)
                    act.activation(xs_lo[:, t0:t0 + n, :], x_all[:, t0:t0 + n, :], ACT.Copy, scale=LS).then_inc(used, 1)
                act.wait_ge(g_made, 1)
                act.activation(gcol[:, :, 1], ga, ACT.Copy, scale=LS).then_inc(used, 1)

            @block.tensor
            def _(pe):
                def transpose(t, b):
                    pe.wait_ge(h_ready, t + 1)
                    pe.wait_ge(lo_done, free(t))
                    for k in range(KC):
                        last = pe.transpose(tp[:, b, k, :], h[:, b, k * P:(k + 1) * P], keep["ident"][:])
                    last.then_inc(tp_ready, 1)

                def products(t, b):
                    pe.wait_ge(lo_done, done(t))
                    pe.wait_ge(msq_made, free(t))
                    split_product(pe, main[:, b, :], hT_hi[:, b], hT_lo[:, b], w_hi, w_lo, slice(0, D)).then_inc(prod_done, 1)

                pipeline(pe, (2, transpose), (1, products),
                         before=[(-1, lambda: pe.wait_ge(s["w_lo"], 1))])

            @block.vector
            def _(dve):
                def weights():
                    dve.wait_ge(w_in, 16)
                    split_weights(dve, w, w_hi, w_lo, s)

                def elu(c):
                    t0, n = CHUNKS[c]
                    yc, xc = y[:, c % 2, 0:n, :], x_all[:, t0:t0 + n, :]
                    dve.wait_ge(y_made, c + 1)
                    dve.tensor_scalar(low[:, 0:n, :], yc, 0.0, None, ALU.min).then_inc(low_made, 1)
                    dve.wait_ge(low_made, c + 1)
                    dve.tensor_scalar(yc, yc, 0.0, -1.0, ALU.max, ALU.add).then_inc(plus_made, 1)
                    dve.wait_ge(plus_made, c + 1)
                    dve.wait_ge(x_in[c], 16)
                    dve.tensor_tensor(xc, xc, yc, ALU.add).then_inc(sum_made, 1)

                def residual(c):
                    t0, n = CHUNKS[c]
                    xc = x_all[:, t0:t0 + n, :]
                    dve.wait_ge(sum_made, c + 1)
                    dve.wait_ge(el_made, c + 1)
                    dve.tensor_tensor(xc, xc, el[:, 0:n, :], ALU.add).then_inc(x_made, 1)
                    dve.wait_ge(x_made, c + 1)


                def split(t, b):
                    dve.wait_ge(hi_ready, t + 1)
                    dve.tensor_tensor(hT_lo[:, b], tp[:, b], hT_hi[:, b], ALU.subtract).then_inc(lo_done, 1)
                    dve.wait_ge(hsq_made, t + 1)
                    dve.tensor_reduce(ssq[:, 0, ds(t, 1)], sq[:, b, 0, :], AXX, ALU.add).then_inc(hss_done, 1)

                def finish(t, b):
                    dve.wait_ge(msq_made, done(t))
                    dve.tensor_reduce(ssq[:, 1, ds(t, 1)], sq[:, b, 1, :], AXX, ALU.add).then_inc(ssq_done, 1)

                pipeline(dve, (2, split), (5, lambda t, b: moments(dve, t, b, x_all, stats, mv, std, s, gate)),
                         (4, lambda t, b: shift(dve, t, b, mv, std, rstd, nmr, h_ready, s, gate)), (0, finish),
                         before=[(-4, weights)] + [(-3 if c == 1 else t0 - 6, lambda c=c: residual(c)) for c, (t0, n) in enumerate(CHUNKS)] +
                                [(-4 if c == 1 else t0 - 8, lambda c=c: elu(c)) for c, (t0, n) in enumerate(CHUNKS)])
                dve.wait_ge(ssq_done, done(T - 1))
                dve.wait_ge(hss_done, done(T - 1))
                ch = Chain(dve, link, asked, answered)
                ch.scale(ssq[:], ssq[:], 1e-20, ALU.max)
                ch.ask()
                ch.invert(co, mn)
                ch.invert(ga, hn)
                ch.pair(ga, ga, mn)
                ch.scale(th, mn, 1e-10, ALU.is_gt)
                ch.pair(co, co, th)
                ch.atanh(tt, hn, t1, t2, ln)
                ch.pair(tt, tt, ga)
                ch.tanh(th, tt, t1, t2, ee)
                ch.pair(co, co, th)
                ch.scale(ee, ee, EMIN, ALU.max)
                ch.scale(t1, ee, 2.0)
                ch.invert(t1, t1)
                ch.fused(t2, ee, 1.0, t1, ALU.add, ALU.mult)
                ch.fused(ga, ee, 1.0, t2, ALU.add, ALU.mult)
                ch.pair(t2, ga, co)
                ch.scale(co, t2, XS)
                ch.scale(ga, ga, -1.0, ALU.add, XS, ALU.mult)
                dve.sem_inc(co_made, 1)
                ch.then(dve.tensor_copy(gcol[:, :, 0], ga))
                ch.pair(ga, ga, gcol[:, :, 0], ALU.subtract)
                dve.sem_inc(g_made, 1)
                dve.memset(gcol[:, :, 2], 1.0).then_inc(used, 1)

                def difference(t, b):
                    dve.wait_ge(hi_made, t + 1)
                    dve.scalar_tensor_tensor(flat(x_all[:, ds(t, 1), :]), flat(x_all[:, ds(t, 1), :]), co[:, ds(t, 1)],
                                             flat(xs_hi[:, ds(t, 1), :]), ALU.mult, ALU.subtract).then_inc(diff_made, 1)

                loop_tiles(dve, difference)
                for c, (t0, n) in enumerate(CHUNKS):
                    if c not in LOW_BY_ACT:
                        dve.wait_ge(diff_made, t0 + n)
                        dve.tensor_scalar(xs_lo[:, t0:t0 + n, :], x_all[:, t0:t0 + n, :], LS, None, ALU.mult).then_inc(used, 1)

        kit.close()


def midpoint2(nc, dram, keep):
    with ExitStack() as stack:
        kit = Kit(nc, stack, "m2")
        HJ = T // 2
        at = kit.sb("at", [2, HJ, BW], F16)
        lowp, nom, rel = kit.sb("lowp", [2, D]), kit.sb("nom", [2, D]), kit.sb("rel", [2, D])
        sq = kit.sb("sq", [2, 2, D])
        ss, sm, v = kit.sb("ss", [2, T]), kit.sb("sm", [3, T]), kit.sb("v", [10, T])
        hi = kit.ps("hi", [2, D])
        lo = kit.ps("lo", [2, D])
        small = kit.ps("small", [2, 512])
        xs_hi, xs_lo, gcol, factor = keep["xs_hi"], keep["xs_lo"], keep["gcol"], keep["factor"]
        at_in, r_out = kit.sems("at_in0 at_in1"), kit.sems("r_out0 r_out1")
        (prod_done, half_used, low_made, nom_made, sm_made, acc_free, nsq_made, rel_made, rsq_made, ss_done, link, asked,
         answered, gate) = kit.sems(
            "prod_done half_used low_made nom_made sm_made acc_free nsq_made rel_made rsq_made ss_done link asked "
            "answered gate")
        den, nn, rr, t1, t2, ln, ee, un, xn, th = (v[:, i, :] for i in range(10))

        def loop_blocks(eng, step):
            with eng.Fori(0, IB) as ib:
                for q in range(2):
                    step(ib, q)

        with nc.Block() as block:
            @block.sync
            def _(sp):
                for ring in (acc_free, nom_made, rsq_made, ss_done):
                    sp.sem_inc(ring, 2)
                for out in r_out:
                    sp.sem_inc(out, 16)
                for half in range(2):
                    sp.sem_inc(half_used, 1)

                def load(ib, half):
                    wait_count(sp, half_used, 2 * ib + half + 1, gate)
                    sp.dma_start(at[:, half], dram["at16"][ds(ib, 1), :, half * HJ:(half + 1) * HJ, :].rearrange(
                        "o p t c -> p (o t) c")).then_inc(at_in[half], 16)

                def store(ib):
                    for q in range(2):
                        wait_count(sp, rel_made, 2 * ib + q + 1, gate)
                        sp.dma_start(dram["part2"].rearrange("(t p) d -> t p d", p=P)[ds(2 * ib + q, 1)].rearrange(
                            "o p d -> p (o d)"), rel[:, q, :]).then_inc(r_out[q], 16)

                load(0, 0)
                load(0, 1)
                with sp.Fori(1, IB) as ib:
                    load(ib, 0)
                    load(ib, 1)
                    store(ib - 1)
                store(IB - 1)
                for out in r_out:
                    sp.wait_ge(out, 16 * (IB + 1))

            @block.tensor
            def _(pe):
                def tile(ib, q):
                    pe.wait_ge(acc_free, free(2 * ib + q))
                    for j in range(T):
                        if q == 0 and j % HJ == 0:
                            pe.wait_ge(at_in[j // HJ], ib * 16 + 16)
                        a = at[:, j // HJ, j % HJ, q * P:(q + 1) * P]
                        ends = dict(start=(j == 0), stop=(j == T - 1))
                        pe.matmul(hi[:, q, :], a, xs_hi[:, j, :], **ends)
                        pe.matmul(lo[:, q, :], a, xs_lo[:, j, :], **ends)
                        last = pe.matmul(small[:, q, 0:3], a, gcol[:, j, :], **ends)
                        if j == HJ - 1 and q == 1:
                            last.then_inc(half_used, 1)
                        if j == T - 1:
                            last.then_inc(prod_done, 1)
                            if q == 1:
                                pe.wait_ge(prod_done, 2 * ib + 2)
                                pe.sem_inc(half_used, 1)

                loop_blocks(pe, tile)

            @block.scalar
            def _(act):
                def tile(ib, q):
                    t = 2 * ib + q
                    act.wait_ge(prod_done, t + 1)
                    act.wait_ge(nom_made, free(t))
                    act.activation(lowp[:, q, :], lo[:, q, :], ACT.Copy, scale=1 / LS).then_inc(low_made, 1)
                    act.wait_ge(nom_made, done(t))
                    act.wait_ge(ss_done, free(t))
                    act.activation(sq[:, q, 0, :], nom[:, q, :], ACT.Square).then_inc(nsq_made, 1)
                    act.wait_ge(rel_made, t + 1)
                    act.activation(sq[:, q, 1, :], rel[:, q, :], ACT.Square).then_inc(rsq_made, 1)

                loop_blocks(act, tile)
                answers(act, asked, answered, [(v[:, 1:3, :], ACT.Sqrt, ss[:], 1.0), (t1, ACT.Sqrt, t1, 1.0),
                                               (ln, ACT.Ln, ln, 1.0), (ee, ACT.Exp, un, -2.0)])

            @block.vector
            def _(dve):
                def tile(ib, q):
                    t = 2 * ib + q
                    dve.wait_ge(prod_done, t + 1)
                    dve.tensor_copy(sm[:, :, ds(t, 1)], small[:, q, 0:3].unsqueeze(2)).then_inc(sm_made, 1)
                    dve.wait_ge(low_made, t + 1)
                    dve.wait_ge(rsq_made, free(t))
                    dve.tensor_tensor(nom[:, q, :], hi[:, q, :], lowp[:, q, :], ALU.add).then_inc(nom_made, 1)
                    dve.wait_ge(nom_made, done(t))
                    dve.wait_ge(sm_made, t + 1)
                    dve.sem_inc(acc_free, 1)
                    dve.wait_ge(r_out[q], ib * 16 + 16)
                    dve.tensor_scalar(rel[:, q, :], nom[:, q, :], 0.0, None, ALU.max).then_inc(rel_made, 1)
                    dve.wait_ge(nsq_made, t + 1)
                    dve.wait_ge(rsq_made, done(t))
                    dve.tensor_reduce(ss[:, :, ds(t, 1)], sq[:, q], AXX, ALU.add).then_inc(ss_done, 1)

                loop_blocks(dve, tile)
                dve.wait_ge(ss_done, done(T - 1))
                dve.wait_ge(sm_made, T)
                ch = Chain(dve, link, asked, answered)
                alpha = sm[:, 2, :]
                ch.fused(den, sm[:, 1, :], 1 / LS, sm[:, 0, :], ALU.mult, ALU.add)
                ch.scale(den, den, 1e-10 * XS, ALU.max)
                ch.invert(den, den)
                ch.ask()
                ch.pair(xn, nn, den)
                ch.pair(t2, xn, xn)
                ch.scale(t1, t2, -1.0, ALU.mult, 1.0, ALU.add)
                ch.scale(t1, t1, 1e-10, ALU.max)
                ch.ask()
                ch.scale(t1, t1, 1.0, ALU.add)
                ch.invert(t1, t1)
                ch.pair(xn, xn, t1)
                ch.scale(xn, xn, 1e-10, ALU.max)
                ch.atanh(un, xn, t1, t2, ln)
                ch.pair(un, un, alpha)
                ch.scale(un, un, ATMAX, ALU.min)
                ch.scale(nn, nn, 1e-30, ALU.max)
                ch.invert(nn, nn)
                ch.pair(un, un, nn)
                ch.pair(un, un, rr)
                ch.tanh(th, un, t1, t2, ee)
                ch.scale(rr, rr, 1e-30, ALU.max)
                ch.invert(rr, rr)
                ch.pair(factor[:], th, rr)

        kit.close()

def prep3(nc, dram, keep):
    with ExitStack() as stack:
        kit = Kit(nc, stack, "p3")
        x_all, h = kit.sb("x_all", [T, D]), kit.sb("h", [2, D])
        hT_hi, hT_lo = kit.sb("hT_hi", [2, KC, P], F16), kit.sb("hT_lo", [2, KC, P], F16)
        NX = 2 * D + 1
        w = kit.sb("w", [KC, NX])
        w_hi, w_lo = kit.sb("w_hi", [KC, NX], F16), kit.sb("w_lo", [KC, NX], F16)
        r = kit.sb("r", [6, D])
        stats, mv = kit.sb("stats", [2, 6]), kit.sb("mv", [2, 2])
        std, rstd, nmr = kit.sb("std", [2]), kit.sb("rstd", [2]), kit.sb("nmr", [2])
        valid, nl, ne = kit.sb("valid", [T]), kit.sb("nl", [T]), kit.sb("ne", [T])
        one = kit.sb("one", [4, 1])
        tp = kit.ps("tp", [2, KC, P])
        main = kit.ps("main", [2, D])
        edge = kit.ps("edge", [2, KC, P])
        small = kit.ps("small", [2, 256])
        s_hi, s_lo, e_hi, e_lo, node = (keep[n] for n in ("s_hi", "s_lo", "e_hi", "e_lo", "node"))
        x_in = kit.sems(" ".join(f"x_in{c}" for c in range(len(CHUNKS))))
        s = dict(zip("stats mv var std rstd nmr w_hi w_lo".split(),
                     kit.sems("stats mv var std rstd nmr w_hi w_lo")))
        (w_in, gate, r_in, v_in, x_made, x_out, h_ready, tp_ready, hi_ready, lo_done, prod_done, s_hi_made, s_lo_done,
         e_hi_made, e_lo_done, nl_done, link, asked, answered, m_made, m_all, z_all) = kit.sems(
            "w_in gate r_in v_in x_made x_out h_ready tp_ready hi_ready lo_done prod_done s_hi_made s_lo_done "
            "e_hi_made e_lo_done nl_done link asked answered m_made m_all z_all")
        x_t, r_t = tiles(dram["x2"]), tiles(dram["part2"])
        gm, gmall, gz, gzall = (one[:, i, :] for i in range(4))

        with nc.Block() as block:
            @block.sync
            def _(sp):
                for ring in (lo_done, prod_done, s_lo_done, e_lo_done, nl_done):
                    sp.sem_inc(ring, 2)
                for c, (t0, n) in enumerate(CHUNKS):
                    sp.dma_start(x_all[:, t0:t0 + n, :], x_t[:, t0:t0 + n, :]).then_inc(x_in[c], 16)
                    if c >= 1:
                        sp.wait_ge(x_made, c)
                    sp.dma_start(r[:, 0:n, :], r_t[:, t0:t0 + n, :]).then_inc(r_in, 16)
                    if c == 0:
                        sp.dma_start(w[:], dram["w3"].rearrange("(k p) n -> p k n", p=P)).then_inc(w_in, 16)
                        sp.dma_start(valid[:], dram["valid"]).then_inc(v_in, 16)
                for c, (t0, n) in enumerate(CHUNKS):
                    sp.wait_ge(x_made, c + 1)
                    sp.dma_start(tiles(dram["x3"])[:, t0:t0 + n, :], x_all[:, t0:t0 + n, :]).then_inc(x_out, 16)
                sp.wait_ge(x_out, 16 * len(CHUNKS))

            @block.gpsimd
            def _(pool):
                pool.wait_ge(m_made, 1)
                pool.partition_all_reduce(gmall, gm, P, RMAX).then_inc(m_all, 1)
                pool.wait_ge(answered, 1)
                pool.partition_all_reduce(gzall, gz, P, RADD).then_inc(z_all, 1)

            @block.scalar
            def _(act):

                def normalise(t, b):
                    act.wait_ge(s["nmr"], t + 1)
                    act.wait_ge(tp_ready, free(t))
                    act.activation(h[:, b, :], flat(x_all[:, ds(t, 1), :]), ACT.Relu,
                                   bias=nmr[:, b:b + 1], scale=rstd[:, b:b + 1]).then_inc(h_ready, 1)

                def high(t, b):
                    act.wait_ge(tp_ready, done(t))
                    act.wait_ge(prod_done, free(t))
                    act.activation(hT_hi[:, b], tp[:, b], ACT.Copy).then_inc(hi_ready, 1)

                def finish(t, b):
                    act.wait_ge(prod_done, done(t))
                    act.activation(flat(s_hi[:, ds(t, 1), :]), main[:, b, :], ACT.Copy, scale=1 / WS).then_inc(s_hi_made, 1)
                    act.activation(e_hi[:, :, ds(t * P, P)], edge[:, b], ACT.Copy, scale=1 / WS).then_inc(e_hi_made, 1)

                act.sem_inc(tp_ready, 2)
                pipeline(act, (2, high), (4, lambda t, b: root(act, t, b, std, s)), (3, normalise), (0, finish))
                act.wait_ge(asked, 1)
                act.activation(ne[:], nl[:], ACT.Exp, accum_out=gz).then_inc(answered, 1)

            @block.tensor
            def _(pe):
                def transpose(t, b):
                    pe.wait_ge(h_ready, t + 1)
                    pe.wait_ge(lo_done, free(t))
                    for k in range(KC):
                        last = pe.transpose(tp[:, b, k, :], h[:, b, k * P:(k + 1) * P], keep["ident"][:])
                    last.then_inc(tp_ready, 1)

                def products(t, b):
                    pe.wait_ge(lo_done, done(t))
                    pe.wait_ge(s_lo_done, free(t))
                    split_product(pe, main[:, b, :], hT_hi[:, b], hT_lo[:, b], w_hi, w_lo, slice(0, D))
                    pe.wait_ge(e_lo_done, free(t))
                    for m in range(KC):
                        of = slice(D + m * P, D + (m + 1) * P)
                        for k in range(KC):
                            for n, (a, b_) in enumerate(((w_hi, hT_hi), (w_lo, hT_hi), (w_hi, hT_lo))):
                                pe.matmul(edge[:, b, m, :], a[:, k, of], b_[:, b, k, :], start=(m == 0 and k == 0 and n == 0),
                                          stop=(k == KC - 1 and n == 2), skip_group_check=True)
                    pe.wait_ge(nl_done, done(t - 1))
                    split_product(pe, small[:, b, 0:1], hT_hi[:, b], hT_lo[:, b], w_hi, w_lo, slice(2 * D, NX)).then_inc(prod_done, 1)

                pipeline(pe, (2, transpose), (1, products),
                         before=[(-1, lambda: pe.wait_ge(s["w_lo"], 1))])

            @block.vector
            def _(dve):
                def weights():
                    dve.wait_ge(w_in, 16)
                    split_weights(dve, w, w_hi, w_lo, s)

                def residual(c):
                    t0, n = CHUNKS[c]
                    dve.wait_ge(x_in[c], 16)
                    dve.wait_ge(r_in, 16 * (c + 1))
                    for t in range(n):
                        last = dve.scalar_tensor_tensor(x_all[:, t0 + t, :], r[:, t, :], keep["factor"][:, t0 + t:t0 + t + 1],
                                                        x_all[:, t0 + t, :], ALU.mult, ALU.add)
                    last.then_inc(x_made, 1)
                    dve.wait_ge(x_made, c + 1)


                def split(t, b):
                    dve.wait_ge(hi_ready, t + 1)
                    dve.tensor_tensor(hT_lo[:, b], tp[:, b], hT_hi[:, b], ALU.subtract).then_inc(lo_done, 1)

                def dots(t, b):
                    dve.wait_ge(prod_done, done(t))
                    dve.tensor_scalar(nl[:, ds(t, 1)], small[:, b, 0:1], 1 / WS, None, ALU.mult).then_inc(nl_done, 1)

                def low(t, b):
                    dve.wait_ge(s_hi_made, t + 1)
                    dve.scalar_tensor_tensor(flat(s_lo[:, ds(t, 1), :]), main[:, b, :], 1 / WS, flat(s_hi[:, ds(t, 1), :]),
                                             ALU.mult, ALU.subtract).then_inc(s_lo_done, 1)
                    dve.wait_ge(e_hi_made, t + 1)
                    dve.scalar_tensor_tensor(e_lo[:, :, ds(t * P, P)], edge[:, b], 1 / WS, e_hi[:, :, ds(t * P, P)],
                                             ALU.mult, ALU.subtract).then_inc(e_lo_done, 1)

                here = residual
                pipeline(dve, (0, dots), (2, split), (5, lambda t, b: moments(dve, t, b, x_all, stats, mv, std, s, gate)),
                         (4, lambda t, b: shift(dve, t, b, mv, std, rstd, nmr, h_ready, s, gate)), (0, low),
                         before=[(-4, weights)] + [(t0 - 6, lambda c=c: here(c)) for c, (t0, n) in enumerate(CHUNKS)])
                dve.wait_ge(nl_done, done(T - 1))
                dve.wait_ge(v_in, 16)
                ch = Chain(dve, link, asked, answered)
                ch.scale(valid[:], valid[:], BIG, ALU.mult, -BIG, ALU.add)
                ch.pair(nl[:], nl[:], valid[:], ALU.add)
                dve.tensor_reduce(gm, nl[:], AXX, ALU.max).then_inc(m_made, 1)
                dve.wait_ge(m_all, 1)
                ch.scale(nl[:], nl[:], gmall, ALU.subtract)
                ch.ask()
                dve.wait_ge(z_all, 1)
                ch.invert(gzall, gzall)
                ch.scale(nl[:], keep["iso"][:], -1.0, ALU.mult, 1.0, ALU.add)
                ch.fused(node[:], ne[:], gzall, nl[:], ALU.mult, ALU.mult)

        kit.close()


def attention3(nc, dram, keep):
    with ExitStack() as stack:
        kit = Kit(nc, stack, "m3")
        EC = [(c * 512, min(512, NP - c * 512)) for c in range(-(-NP // 512))]
        GROUPS = [(g, min(8, T - g)) for g in range(0, T, 8)]
        a = kit.sb("a", [2, NP])
        am = kit.sb("am", [2, NP], BF16)
        em = kit.sb("em", [2, NP])
        w_hi, w_lo = kit.sb("w_hi", [NP], F16), kit.sb("w_lo", [NP], F16)
        wT_hi, wT_lo = kit.sb("wT_hi", [T, P], F16), kit.sb("wT_lo", [T, P], F16)
        mx, nm, rs, co = kit.sb("mx", [2, len(EC)]), kit.sb("nm", [2, 1]), kit.sb("rs", [2, 1]), kit.sb("co", [2, 1])
        x, o, bias = kit.sb("x", [2, D]), kit.sb("o", [2, D]), kit.sb("bias", [D])
        sc = kit.ps("sc", [4, 512])
        tw = kit.ps("tw", [2, 8, P], F16)
        acc = kit.ps("acc", [2, D])
        s_hi, s_lo, e_hi, e_lo, node = (keep[n] for n in ("s_hi", "s_lo", "e_hi", "e_lo", "node"))
        a_in, x_in, out_done = kit.sems("a_in0 a_in1"), kit.sems("x_in0 x_in1"), kit.sems("out_done0 out_done1")
        (bias_in, am_made, sc_made, sc_used, max_made, exp_made, hi_made, lo_made, t_hi, t_lo, wt_hi, wt_lo,
         acc_made, acc_used, out_made, link, gate) = kit.sems(
            "bias_in am_made sc_made sc_used max_made exp_made hi_made lo_made t_hi t_lo wt_hi wt_lo "
            "acc_made acc_used out_made link gate")
        NE, NG = len(EC), len(GROUPS)
        AFTER = (0, 2, 4)
        bank = lambda b, c: (NE * b + c) % 4

        with nc.Block() as block:
            @block.sync
            def _(sp):
                for ring in (am_made, max_made, acc_used, out_made, lo_made):
                    sp.sem_inc(ring, 2)
                sp.sem_inc(sc_used, 4)
                for done_ in out_done:
                    sp.sem_inc(done_, 16)
                sp.dma_start(bias[:], dram["bias3"].broadcast_to([P, D])).then_inc(bias_in, 16)

                def load_mask(t, b):
                    wait_count(sp, am_made, free(t), gate)
                    sp.dma_start(a[:, b, :], dram["adj"].rearrange("(t p) n -> t p n", p=P)[ds(t, 1)].rearrange(
                        "o p n -> p (o n)")).then_inc(a_in[b], 16)

                def load_x(t, b):
                    wait_count(sp, out_done[b], (t - b) * 8 + 16, gate)
                    sp.dma_start(x[:, b, :], dram["x3"].rearrange("(t p) d -> t p d", p=P)[ds(t, 1)].rearrange(
                        "o p d -> p (o d)")).then_inc(x_in[b], 16)

                def store(t, b):
                    wait_count(sp, out_made, done(t), gate)
                    rows = LAST if isinstance(t, int) and t == T - 1 else P
                    sp.dma_start(dram["out"][ds(t * P, rows), :], x[0:rows, b, :]).then_inc(out_done[b], 16)

                for t in range(2):
                    load_mask(t, t)
                    load_x(t, t)
                load_mask(2, 0)
                with sp.Fori(3, T - 1, 2) as t:
                    for b in range(2):
                        load_mask(t + b, 1 - b)
                        store(t + b - 3, b)
                        load_x(t + b - 1, b)
                load_mask(T - 1, 1)
                store(T - 4, 0)
                load_x(T - 2, 0)
                store(T - 3, 1)
                load_x(T - 1, 1)
                store(T - 2, 0)
                store(T - 1, 1)
                for done_ in out_done:
                    sp.wait_ge(done_, 16 * (T // 2 + 1))

            @block.tensor
            def _(pe):
                def chunk(t, b, c):
                    n0, n = EC[c]
                    pe.wait_ge(sc_used, t * NE + c + 1)
                    for k in range(KC):
                        for i, (l, r) in enumerate(((e_hi, e_hi), (e_hi, e_lo), (e_lo, e_hi))):
                            last = pe.matmul(sc[:, bank(b, c), 0:n], l[:, k, ds(t * P, P)], r[:, k, n0:n0 + n],
                                             start=(k == 0 and i == 0), stop=(k == KC - 1 and i == 2))
                    last.then_inc(sc_made, 1)

                def transposes(t, g):
                    j0, nj = GROUPS[g]
                    if g == 0:
                        pe.wait_ge(lo_made, done(t))
                    for part, half, made, moved in ((w_hi, 0, t_hi, wt_hi), (w_lo, 1, t_lo, wt_lo)):
                        if not (isinstance(t, int) and t == 0 and g == 0):
                            pe.wait_ge(moved, t * NG + g)
                        for j in range(nj):
                            last = pe.transpose(tw[:, half, j, :], part[:, (j0 + j) * P:(j0 + j + 1) * P], keep["ident16"][:])
                        last.then_inc(made, 1)

                def products(t, b):
                    pe.wait_ge(acc_used, free(t))
                    for g, (j0, nj) in enumerate(GROUPS):
                        pe.wait_ge(wt_hi, t * NG + g + 1)
                        pe.wait_ge(wt_lo, t * NG + g + 1)
                        for j in range(j0, j0 + nj):
                            pe.matmul(acc[:, b, :], wT_hi[:, j, :], s_hi[:, j, :], start=(j == 0), stop=False)
                            pe.matmul(acc[:, b, :], wT_hi[:, j, :], s_lo[:, j, :], start=False, stop=False)
                            last = pe.matmul(acc[:, b, :], wT_lo[:, j, :], s_hi[:, j, :], start=False, stop=(j == T - 1))
                    last.then_inc(acc_made, 1)

                def step(t, b):
                    for c in range(NE):
                        chunk(t + 1, 1 - b, c)
                        if c in AFTER:
                            transposes(t, AFTER.index(c))
                    products(t, b)

                for c in range(NE):
                    chunk(0, 0, c)
                with pe.Fori(0, T - 2, 2) as t:
                    for b in range(2):
                        step(t + b, b)
                step(T - 2, 0)
                for g in range(NG):
                    transposes(T - 1, g)
                products(T - 1, 1)

            @block.vector
            def _(dve):
                dve.wait_ge(bias_in, 16)

                def chunk_max(t, b, c):
                    n0, n = EC[c]
                    if c == 0:
                        dve.wait_ge(am_made, done(t))
                        dve.wait_ge(lo_made, free(t))
                    wait_count(dve, sc_made, t * NE + c + 1, gate)
                    dve.tensor_tensor_reduce(em[:, b, n0:n0 + n], sc[:, bank(b, c), 0:n], am[:, b, n0:n0 + n], 1.0, -3e38,
                                             ALU.add, ALU.max, mx[:, b, c:c + 1]).then_inc(sc_used, 1)

                def row_max(t, b):
                    dve.wait_ge(sc_used, (t + 1) * NE + 4)
                    dve.tensor_reduce(nm[:, b, :], mx[:, b, :], AXX, ALU.max, negate=True).then_inc(max_made, 1)

                def low(t, b):
                    dve.wait_ge(hi_made, t + 1)
                    dve.tensor_tensor(w_lo[:], em[:, b, :], w_hi[:], ALU.subtract).then_inc(lo_made, 1)

                def move(t, g):
                    j0, nj = GROUPS[g]
                    dve.wait_ge(t_lo, t * NG + g + 1)
                    if g == 0 and not (isinstance(t, int) and t == 0):
                        dve.wait_ge(acc_made, t)
                    dve.tensor_copy(wT_lo[:, j0:j0 + nj, :], tw[:, 1, 0:nj, :]).then_inc(wt_lo, 1)

                def finish(t, b):
                    dve.wait_ge(exp_made, t + 1)
                    dve.reciprocal(co[:, b, :], rs[:, b, :]).then_inc(link, 1)
                    dve.wait_ge(link, 2 * t + 1)
                    dve.tensor_tensor(co[:, b, :], co[:, b, :], node[:, ds(t, 1)], ALU.mult).then_inc(link, 1)
                    dve.wait_ge(link, 2 * t + 2)
                    dve.wait_ge(acc_made, t + 1)
                    dve.wait_ge(out_made, free(t))
                    dve.scalar_tensor_tensor(o[:, b, :], acc[:, b, :], co[:, b, :], bias[:], ALU.mult, ALU.add).then_inc(acc_used, 1)

                def step(t, b, first=False):
                    low(t, b)
                    for c in range(NE):
                        chunk_max(t + 1, 1 - b, c)
                        if c in AFTER:
                            move(t, AFTER.index(c))
                        if c == 1 and not first:
                            finish(t - 1, 1 - b)
                    row_max(t + 1, 1 - b)

                for c in range(NE):
                    chunk_max(0, 0, c)
                row_max(0, 0)
                step(0, 0, True)
                with dve.Fori(1, T - 2, 2) as t:
                    for b in range(2):
                        step(t + b, 1 - b)
                low(T - 1, 1)
                finish(T - 2, 0)
                for g in range(NG):
                    move(T - 1, g)
                finish(T - 1, 1)

            @block.scalar
            def _(act):
                def mask(t, b):
                    act.wait_ge(a_in[b], (t - b) * 8 + 16)
                    act.wait_ge(max_made, free(t))
                    act.activation(am[:, b, :], a[:, b, :], ACT.Copy, scale=BIG, bias=-BIG).then_inc(am_made, 1)

                def softmax(t, b):
                    act.wait_ge(max_made, done(t))
                    act.activation(em[:, b, :], em[:, b, :], ACT.Exp, bias=nm[:, b, :], accum_out=rs[:, b, :]).then_inc(exp_made, 1)
                    act.wait_ge(exp_made, t + 1)
                    if not (isinstance(t, int) and t == 0):
                        act.wait_ge(t_hi, t * NG)
                        act.wait_ge(t_lo, t * NG)
                    act.activation(w_hi[:], em[:, b, :], ACT.Copy).then_inc(hi_made, 1)

                def move(t, b):
                    for g, (j0, nj) in enumerate(GROUPS):
                        act.wait_ge(t_hi, t * NG + g + 1)
                        if g == 0 and not (isinstance(t, int) and t == 0):
                            act.wait_ge(acc_made, t)
                        act.activation(wT_hi[:, j0:j0 + nj, :], tw[:, 0, 0:nj, :], ACT.Copy).then_inc(wt_hi, 1)

                mask(0, 0)
                mask(1, 1)
                with act.Fori(0, T - 3, 2) as t:
                    for b in range(2):
                        softmax(t + b, b)
                        mask(t + b + 2, b)
                        move(t + b, b)
                for t in (T - 2, T - 1):
                    softmax(t, t % 2)
                    move(t, t % 2)

            @block.gpsimd
            def _(pool):
                def add(t, b):
                    pool.wait_ge(x_in[b], (t - b) * 8 + 16)
                    pool.wait_ge(acc_used, done(t))
                    pool.tensor_tensor(x[:, b, :], x[:, b, :], o[:, b, :], ALU.add).then_inc(out_made, 1)

                loop_tiles(pool, add)

        kit.close()

def build(nc, dram):
    with ExitStack() as stack:
        kit = Kit(nc, stack, "keep")
        keep = {"ident": kit.sb("ident", [P]), "ident16": kit.sb("ident16", [P], F16),
                "ones16": kit.sb("ones16", [P], F16), "iso": kit.sb("iso", [T]), "factor": kit.sb("factor", [T])}
        setup(nc, dram, keep)
        with ExitStack() as layer:
            kit = Kit(nc, layer, "keep0")
            keep |= {"z_hi": kit.sb("z_hi", [T, 2 * D], F16), "z_lo": kit.sb("z_lo", [T, 2 * D], F16),
                     "uv": kit.sb("uv", [2, T]), "cs0": kit.sb("cs0", [2 * D]),
                     "v08": kit.sb("v08", [T]), "v02": kit.sb("v02", [T])}
            prep0(nc, dram, keep)
            attention0(nc, dram, keep)
        with ExitStack() as layer:
            kit = Kit(nc, layer, "keep1")
            keep |= {n: kit.sb(n, [H, T]) for n in ("r1", "f1", "f2", "d1", "d2", "nv")}
            prep1(nc, dram, keep)
            attention1(nc, dram, keep)
        with ExitStack() as layer:
            kit = Kit(nc, layer, "keep2")
            keep |= {"xs_hi": kit.sb("xs_hi", [T, D], F16), "xs_lo": kit.sb("xs_lo", [T, D], F16), "gcol": kit.sb("gcol", [T, 3], F16)}
            prep2(nc, dram, keep)
            midpoint2(nc, dram, keep)
        with ExitStack() as layer:
            kit = Kit(nc, layer, "keep3")
            keep |= {n: kit.sb(n, [T, D], F16) for n in ("s_hi", "s_lo")}
            keep |= {n: kit.sb(n, [KC, NP], F16) for n in ("e_hi", "e_lo")}
            keep["node"] = kit.sb("node", [T])
            prep3(nc, dram, keep)
            attention3(nc, dram, keep)


def layouts(inputs):
    import numpy as np

    x, adj = np.asarray(inputs["x"]), np.asarray(inputs["adj"])
    f32 = x.dtype
    x0 = np.zeros((NP, D), f32)
    x0[:N] = x
    rows = np.zeros((NP, NP), f32)
    rows[:N, :N] = adj
    adjT = np.ascontiguousarray(rows.reshape(IB, BW, T, P).transpose(0, 3, 2, 1))
    get = lambda name: np.ascontiguousarray(np.asarray(inputs[name]))
    valid = np.zeros((NP,), f32)
    valid[:N] = 1
    return {
        "x0": x0, "adj": rows, "adjT": adjT, "ident": np.eye(P, dtype=f32),
        "valid": np.ascontiguousarray(valid.reshape(T, P).T),
        "w0t": np.ascontiguousarray(get("L0_gnn_W").T),
        "a0": np.ascontiguousarray(get("L0_gnn_a").reshape(2, KC, P).transpose(2, 1, 0)),
        "wtr0": get("L0_gnn_wtrans"), "w1": get("L1_gnn_W"),
        "a1": np.ascontiguousarray(get("L1_gnn_a1").T).reshape(1, -1),
        "a2": np.ascontiguousarray(get("L1_gnn_a2").T).reshape(1, -1),
        "aln": get("L1_gnn_a_ln").reshape(1, -1), "bln": get("L1_gnn_b_ln").reshape(1, -1),
        "w2": get("L2_gnn_W"), "w3": np.concatenate([get("L3_gnn_weight"), get("L3_gnn_edge_w"), get("L3_gnn_node_w")], axis=1),
        "bias3": get("L3_gnn_bias").reshape(1, -1),
    }


SCRATCH = {"rows": (2 * T, P), "rows1": (H * T, P), "at16": (IB, P, T, BW), "x1": (NP, D), "x2": (NP, D), "x3": (NP, D),
           "c1": (NP, D), "y1": (NP, D), "part2": (NP, D)}


def kernel(**inputs):
    import concourse.bacc as bacc
    from concourse.bass_utils import run_bass_kernel_spmd

    nc = bacc.Bacc("TRN2", target_bir_lowering=False, num_devices=1)
    arrays = layouts(inputs)
    dram = {name: nc.dram_tensor(name, a.shape, F32, kind="ExternalInput").ap() for name, a in arrays.items()}
    for name, shape in SCRATCH.items():
        dram[name] = nc.dram_tensor(name, shape, F16 if name == "at16" else F32).ap()
    dram["out"] = nc.dram_tensor("out", (N, D), F32, kind="ExternalOutput").ap()
    build(nc, dram)
    result = run_bass_kernel_spmd(nc, [arrays], core_ids=[0])
    return result.results[0]["out"]
```
